# Optimizing a Trainium2 kernel written in Bass

```python
import numpy as np
import jax
import jax.numpy as jnp

def _softmax(x, axis=-1):
    return jax.nn.softmax(x, axis=axis)

def _gelu(x):
    return jax.nn.gelu(x, approximate=True)

def _silu(x):
    return jax.nn.silu(x)

def _sigmoid(x):
    return jax.nn.sigmoid(x)

def _layernorm(x, axis=-1, eps=1e-05):
    m = jnp.mean(x, axis=axis, keepdims=True)
    v = jnp.var(x, axis=axis, keepdims=True)
    return (x - m) / jnp.sqrt(v + eps)

def _scatter_add(tgt, idx, src, axis=0):
    return tgt.at[idx].add(src)

def _segment_sum(src, seg, n):
    return jax.ops.segment_sum(src, seg, n)
kernel_name = 'mk_decoder_postln_d2_seqx_r4_8ad161'

def setup_inputs(seed: int=0):
    np.random.seed(seed)
    _w = jnp.asarray

    def _rec_inputs():
        import jax
        import jax.numpy as jnp
        _rk = jax.random.key(seed)
        x = 7.22e-05 + 1 * jax.random.normal(jax.random.fold_in(_rk, 1), (16, 128, 256), jnp.float32)
        _lenS = 128 - jax.random.randint(jax.random.fold_in(_rk, 7), (16,), 0, max(1, 128 // 4) + 1, jnp.int32)
        _lenS2 = 128 - jax.random.randint(jax.random.fold_in(_rk, 8), (16,), 0, max(1, 128 // 4) + 1, jnp.int32)
        _ctx_1024P = jax.random.normal(jax.random.fold_in(_rk, 11), (16, 16, 256), jnp.float32)
        _ctx_1024c = jax.random.dirichlet(jax.random.fold_in(_rk, 511), 0.3 * jnp.ones((16,), jnp.float32), (16, 128))
        _ctx_1024t = jnp.einsum('bsk,bkd->bsd', _ctx_1024c, _ctx_1024P)
        _ctx_1024t = _ctx_1024t * jax.lax.rsqrt(jnp.mean(jnp.square(_ctx_1024t)) + 1e-12) * 0.953939
        ctx_1024 = 4.13588e-05 + 0.999923 * (_ctx_1024t + 0.3 * jax.random.normal(jax.random.fold_in(_rk, 611), (16, 128, 256), jnp.float32))
        _validS = jnp.arange(128)[None, :] < _lenS[:, None]
        _validS2 = jnp.arange(128)[None, :] < _lenS2[:, None]
        _causal = jnp.tril(jnp.ones((128, 128), dtype=bool))
        mask_Bx1xS2_bf1 = jnp.ones((16, 1, 128), dtype=bool)
        mask_SxS_bc0 = jnp.logical_not(jnp.broadcast_to(_causal[:, :], (128, 128)))
        return (x, ctx_1024, mask_Bx1xS2_bf1, mask_SxS_bc0)
    x, ctx_1024, mask_Bx1xS2_bf1, mask_SxS_bc0 = _rec_inputs()

    def _L0_attn_setup():
        import jax, jax.numpy as jnp
        import numpy as np
        B, L = (2, 256)
        D_MODEL, D_CKV, D_CQ = (256, 64, 128)
        N_HEAD, D_HEAD, D_ROPE = (8, 64, 32)
        N_IDX_HEAD = 4
        K_TS, LW = (96, 64)
        ROPE_BASE = 10000.0

        def _pope(x, angles):
            cos, sin = (jnp.cos(angles), jnp.sin(angles))
            mu1, mu2 = jnp.split(jax.nn.softplus(x), 2, axis=-1)
            return jnp.concatenate([mu1 * cos - mu2 * sin, mu1 * sin + mu2 * cos], axis=-1)

        def _forward(x, W_dkv, W_uk, W_uv, W_dq, W_uq, W_qr, W_kr, W_out, idx_wq, idx_wk, idx_w, raw_delta):
            B_, L_, _ = x.shape
            c_kv = x @ W_dkv
            q_i = (x @ idx_wq).reshape(B_, L_, N_IDX_HEAD, D_HEAD)
            k_i = x @ idx_wk
            s_i = jax.nn.relu(jnp.einsum('bthd,bsd->bths', q_i, k_i))
            I = jnp.einsum('bths,h->bts', s_i, idx_w)
            qpos = jnp.arange(L_)[:, None]
            kpos = jnp.arange(L_)[None, :]
            local = (kpos >= qpos - LW + 1) & (kpos <= qpos)
            causal = kpos > qpos
            I = jnp.where(local[None], jnp.inf, I)
            I = jnp.where(causal[None], -jnp.inf, I)
            kk = min(K_TS, L_)
            _, idx = jax.lax.top_k(I, kk)
            bi = jnp.arange(B_)[:, None, None]
            key_c = (c_kv @ W_uk)[bi, idx].reshape(B_, L_, kk, N_HEAD, D_HEAD)
            value = (c_kv @ W_uv)[bi, idx].reshape(B_, L_, kk, N_HEAD, D_HEAD)
            c_q = x @ W_dq
            query_c = (c_q @ W_uq).reshape(B_, L_, N_HEAD, D_HEAD)
            half = D_ROPE // 2
            theta = 1.0 / ROPE_BASE ** (2.0 * jnp.arange(half, dtype=jnp.float32) / D_ROPE)
            delta = -2.0 * jnp.pi * jax.nn.sigmoid(raw_delta)
            angles_q = jnp.arange(L_, dtype=jnp.float32)[:, None] * theta[None, :] + delta
            query_r = _pope((c_q @ W_qr).reshape(B_, L_, N_HEAD, D_ROPE), angles_q[None, :, None, :])
            kr_sel = (x @ W_kr)[bi, idx]
            angles_k = jnp.arange(kk, dtype=jnp.float32)[:, None] * theta[None, :] + delta
            key_r = _pope(kr_sel, angles_k[None, None, :, :])
            scale = (D_HEAD + D_ROPE) ** (-0.5)
            q_c = query_c.transpose(0, 2, 1, 3)
            q_r = query_r.transpose(0, 2, 1, 3)
            k_c = key_c.transpose(0, 3, 1, 2, 4)
            v = value.transpose(0, 3, 1, 2, 4)
            scores = (jnp.einsum('bhld,bhlkd->bhlk', q_c, k_c) + jnp.einsum('bhld,blkd->bhlk', q_r, key_r)) * scale
            attn = jax.nn.softmax(scores.astype(jnp.float32), axis=-1).astype(v.dtype)
            out = jnp.einsum('bhlk,bhlkd->bhld', attn, v)
            out = out.transpose(0, 2, 1, 3).reshape(B_, L_, N_HEAD * D_HEAD)
            return out @ W_out
        key = jax.random.key(seed)
        ks = jax.random.split(key, 14)

        def w(k, shape, fan_in):
            return jax.random.normal(k, shape, dtype=jnp.float32) * fan_in ** (-0.5)
        return {'x': jax.random.normal(ks[0], (B, L, D_MODEL), dtype=jnp.float32), 'W_dkv': w(ks[1], (D_MODEL, D_CKV), D_MODEL), 'W_uk': w(ks[2], (D_CKV, N_HEAD * D_HEAD), D_CKV), 'W_uv': w(ks[3], (D_CKV, N_HEAD * D_HEAD), D_CKV), 'W_dq': w(ks[4], (D_MODEL, D_CQ), D_MODEL), 'W_uq': w(ks[5], (D_CQ, N_HEAD * D_HEAD), D_CQ), 'W_qr': w(ks[6], (D_CQ, N_HEAD * D_ROPE), D_CQ), 'W_kr': w(ks[7], (D_MODEL, D_ROPE), D_MODEL), 'W_out': w(ks[8], (N_HEAD * D_HEAD, D_MODEL), N_HEAD * D_HEAD), 'idx_wq': w(ks[9], (D_MODEL, N_IDX_HEAD * D_HEAD), D_MODEL), 'idx_wk': w(ks[10], (D_MODEL, D_HEAD), D_MODEL), 'idx_w': jnp.ones((N_IDX_HEAD,), dtype=jnp.float32), 'raw_delta': jax.random.normal(ks[11], (D_ROPE // 2,), dtype=jnp.float32) * 0.1}
    _L0_attn_all = _L0_attn_setup()
    _L0_attn_in = {k: v for k, v in _L0_attn_all.items() if k in ('W_dkv', 'W_uk', 'W_uv', 'W_dq', 'W_uq', 'W_qr', 'W_kr', 'W_out', 'idx_wq', 'idx_wk', 'idx_w', 'raw_delta')}
    del _L0_attn_all

    def _L0_xattn_setup():
        import jax, jax.numpy as jnp
        import numpy as np
        D_MODEL = 256
        N_HEADS = 16
        D_K = D_MODEL // N_HEADS
        key = jax.random.key(seed)
        ks = jax.random.split(key, 12)
        B, S, D = (4, 512, D_MODEL)
        s = 1.0 / np.sqrt(D)
        return {'Q': jax.random.normal(ks[0], (B, S, D), jnp.float32), 'K': jax.random.normal(ks[1], (B, S, D), jnp.float32), 'V': jax.random.normal(ks[2], (B, S, D), jnp.float32), 'mask': jnp.ones((B, 1, S), dtype=bool), 'Wq': jax.random.normal(ks[3], (D, D), jnp.float32) * s, 'bq': jnp.zeros((D,), jnp.float32), 'Wk': jax.random.normal(ks[4], (D, D), jnp.float32) * s, 'bk': jnp.zeros((D,), jnp.float32), 'Wv': jax.random.normal(ks[5], (D, D), jnp.float32) * s, 'bv': jnp.zeros((D,), jnp.float32), 'Wo': jax.random.normal(ks[6], (D, D), jnp.float32) * s, 'bo': jnp.zeros((D,), jnp.float32)}
    _L0_xattn_all = _L0_xattn_setup()
    _L0_xattn_in = {k: v for k, v in _L0_xattn_all.items() if k in ('Wq', 'bq', 'Wk', 'bk', 'Wv', 'bv', 'Wo', 'bo')}
    del _L0_xattn_all

    def _L0_ffn_setup():
        import jax, jax.numpy as jnp
        import numpy as np
        HIDDEN = 256
        INNER = 1024

        def _weight_quant(w):
            scale = 1.0 / jnp.clip(jnp.mean(jnp.abs(w)), 1e-05)
            wq = jnp.clip(jnp.round(w * scale), -1.0, 1.0) / scale
            return w + jax.lax.stop_gradient(wq - w)

        def _act_quant(x):
            scale = 127.0 / jnp.clip(jnp.max(jnp.abs(x), axis=-1, keepdims=True), 1e-05)
            xq = jnp.clip(jnp.round(x * scale), -128.0, 127.0) / scale
            return x + jax.lax.stop_gradient(xq - x)

        def _bitlinear(x, w):
            return jnp.einsum('bsi,oi->bso', _act_quant(x), _weight_quant(w))
        key = jax.random.key(seed)
        k0, k1, k2, k3 = jax.random.split(key, 4)
        x = jax.random.normal(k0, (4, 512, HIDDEN), dtype=jnp.float32)
        w_gate = jax.random.normal(k1, (INNER, HIDDEN), dtype=jnp.float32) / np.sqrt(HIDDEN)
        w_up = jax.random.normal(k2, (INNER, HIDDEN), dtype=jnp.float32) / np.sqrt(HIDDEN)
        w_down = jax.random.normal(k3, (HIDDEN, INNER), dtype=jnp.float32) / np.sqrt(INNER)
        return {'x': x, 'w_gate': w_gate, 'w_up': w_up, 'w_down': w_down}
    _L0_ffn_all = _L0_ffn_setup()
    _L0_ffn_in = {k: v for k, v in _L0_ffn_all.items() if k in ('w_gate', 'w_up', 'w_down')}
    del _L0_ffn_all

    def _L1_attn_setup():
        import jax, jax.numpy as jnp
        import numpy as np
        B, N, D, H, C = (4, 2048, 256, 16, 128)
        HD = D // H
        THRESHOLD = 0.99

        def _chunk_scan(qc, kc, vc, lf):
            mask = jnp.tril(jnp.ones((C, C), bool))

            def step(S, inputs):
                qb, kb, vb, lb = inputs
                o_inter = jnp.einsum('bhid,bhde->bhie', qb * jnp.exp(lb)[..., None], S)
                A = jnp.einsum('bhid,bhjd->bhij', qb, kb)
                diff = jnp.where(mask, lb[..., :, None] - lb[..., None, :], -jnp.inf)
                A = A * jnp.exp(diff)
                o_intra = jnp.einsum('bhij,bhjd->bhid', A, vb)
                tot = lb[..., -1]
                kd = kb * jnp.exp(tot[..., None, None] - lb[..., None])
                S_new = jnp.exp(tot)[..., None, None] * S + jnp.einsum('bhjd,bhje->bhde', kd, vb)
                return (S_new, o_inter + o_intra)
            S0 = jnp.zeros((qc.shape[1], H, HD, HD), qc.dtype)
            _, o = jax.lax.scan(step, S0, (qc, kc, vc, lf))
            return o
        key = jax.random.key(seed)
        ks = jax.random.split(key, 6)
        std = 0.02
        return {'x': jax.random.normal(ks[0], (B, N, D), jnp.float32), 'Wq': jax.random.normal(ks[1], (D, D), jnp.float32) * std, 'Wk': jax.random.normal(ks[2], (D, D), jnp.float32) * std, 'Wv': jax.random.normal(ks[3], (D, D), jnp.float32) * std, 'Wo': jax.random.normal(ks[4], (D, D), jnp.float32) * std, 'Wf': jax.random.normal(ks[5], (H, D), jnp.float32) * std, 'delta': jnp.full((H,), float(np.log(THRESHOLD / (1.0 - THRESHOLD))), jnp.float32), 'norm_weight': jnp.ones((D,), jnp.float32)}
    _L1_attn_all = _L1_attn_setup()
    _L1_attn_in = {k: v for k, v in _L1_attn_all.items() if k in ('Wq', 'Wk', 'Wv', 'Wo', 'Wf', 'delta', 'norm_weight')}
    del _L1_attn_all

    def _L1_xattn_setup():
        import jax, jax.numpy as jnp
        import numpy as np
        from jax import lax
        H = 16
        K1, K2 = (3, 3)
        LN_EPS = 1e-05

        def _ln(x, g, b):
            m = jnp.mean(x, axis=-1, keepdims=True)
            v = jnp.mean(jnp.square(x - m), axis=-1, keepdims=True)
            return (x - m) * lax.rsqrt(v + LN_EPS) * g + b

        def _gelu(x):
            return jax.nn.gelu(x, approximate=False)
        key = jax.random.key(seed)
        B, T, D, Th = (4, 256, 256, 64)
        C = 2 * D
        ks = jax.random.split(key, 16)

        def w(k, shape):
            fan_in = shape[0]
            return (jax.random.normal(k, shape, jnp.float32) / np.sqrt(fan_in)).astype(jnp.float32)
        inp = {'x': jax.random.normal(ks[0], (B, T, D), jnp.float32), 'historical_data': jax.random.normal(ks[1], (B, Th, D), jnp.float32), 'Wq': w(ks[2], (D, D)), 'Wk': w(ks[3], (D, D)), 'Wv': w(ks[4], (D, D)), 'hist_W': w(ks[5], (D, C)), 'hist_b': jnp.zeros((C,), jnp.float32), 'hist_ln_g': jnp.ones((C,), jnp.float32), 'hist_ln_b': jnp.zeros((C,), jnp.float32), 'ctx_W1': w(ks[6], (C, C // 4)), 'ctx_b1': jnp.zeros((C // 4,), jnp.float32), 'ctx_W2': w(ks[7], (C // 4, 1)), 'ctx_b2': jnp.zeros((1,), jnp.float32), 'kg_W1': w(ks[8], (C, D)), 'kg_b1': jnp.zeros((D,), jnp.float32), 'kg_ln_g': jnp.ones((D,), jnp.float32), 'kg_ln_b': jnp.zeros((D,), jnp.float32), 'kg_W2': w(ks[9], (D, H * K1 * K2)), 'kg_b2': jnp.zeros((H * K1 * K2,), jnp.float32), 'proj_W': w(ks[10], (D, D)), 'proj_b': jnp.zeros((D,), jnp.float32), 'causal_mask': jnp.triu(jnp.ones((T, T), bool), k=1)}
        return inp
    _L1_xattn_all = _L1_xattn_setup()
    _L1_xattn_in = {k: v for k, v in _L1_xattn_all.items() if k in ('Wq', 'Wk', 'Wv', 'hist_W', 'hist_b', 'hist_ln_g', 'hist_ln_b', 'ctx_W1', 'ctx_b1', 'ctx_W2', 'ctx_b2', 'kg_W1', 'kg_b1', 'kg_ln_g', 'kg_ln_b', 'kg_W2', 'kg_b2', 'proj_W', 'proj_b')}
    del _L1_xattn_all

    def _L1_ffn_setup():
        import jax, jax.numpy as jnp
        import numpy as np
        from jax import lax
        HIDDEN = 256
        INTER = 128
        E = 64
        K = 6
        G = 8
        TG = 4
        NSH = 2
        ISH = INTER * NSH

        def _moe_forward(hidden_states, gate_w, gate_bias, eg_w, eu_w, ed_w, sg_w, su_w, sd_w):
            B, S, H = hidden_states.shape
            x = hidden_states.reshape(-1, H)
            T = x.shape[0]
            shared = jax.nn.silu(x @ sg_w.T) * (x @ su_w.T) @ sd_w.T
            logits = x @ gate_w.T
            scores = jax.nn.sigmoid(logits) + gate_bias
            group_scores = scores.reshape(T, G, E // G).max(axis=-1)
            _, sel_groups = lax.top_k(group_scores, TG)
            group_mask = jnp.zeros((T, G), scores.dtype).at[jnp.arange(T)[:, None], sel_groups].set(1.0)
            mask = jnp.repeat(group_mask, E // G, axis=1)
            masked_scores = scores * mask
            topk_w, topk_i = lax.top_k(masked_scores, K)
            topk_w = topk_w / (topk_w.sum(axis=-1, keepdims=True) + 1e-08)
            comb = jnp.zeros((T, E), x.dtype).at[jnp.arange(T)[:, None], topk_i].add(topk_w)
            h = jax.nn.silu(jnp.einsum('th,eih->eti', x, eg_w)) * jnp.einsum('th,eih->eti', x, eu_w)
            routed = jnp.einsum('eti,ehi,te->th', h, ed_w, comb)
            return (shared + routed).reshape(B, S, H)
        key = jax.random.key(seed)
        ks = jax.random.split(key, 9)
        s = 0.02
        return {'hidden_states': jax.random.normal(ks[0], (1, 256, HIDDEN), jnp.float32), 'gate_w': jax.random.normal(ks[1], (E, HIDDEN), jnp.float32) * s, 'gate_bias': jnp.zeros((E,), jnp.float32), 'eg_w': jax.random.normal(ks[2], (E, INTER, HIDDEN), jnp.float32) * s, 'eu_w': jax.random.normal(ks[3], (E, INTER, HIDDEN), jnp.float32) * s, 'ed_w': jax.random.normal(ks[4], (E, HIDDEN, INTER), jnp.float32) * s, 'sg_w': jax.random.normal(ks[5], (ISH, HIDDEN), jnp.float32) * s, 'su_w': jax.random.normal(ks[6], (ISH, HIDDEN), jnp.float32) * s, 'sd_w': jax.random.normal(ks[7], (HIDDEN, ISH), jnp.float32) * s}
    _L1_ffn_all = _L1_ffn_setup()
    _L1_ffn_in = {k: v for k, v in _L1_ffn_all.items() if k in ('gate_w', 'gate_bias', 'eg_w', 'eu_w', 'ed_w', 'sg_w', 'su_w', 'sd_w')}
    del _L1_ffn_all
    return {'x': x, 'ctx_1024': ctx_1024, 'mask_Bx1xS2_bf1': mask_Bx1xS2_bf1, 'mask_SxS_bc0': mask_SxS_bc0, 'L0_attn_W_dkv': _L0_attn_in['W_dkv'], 'L0_attn_W_uk': _L0_attn_in['W_uk'], 'L0_attn_W_uv': _L0_attn_in['W_uv'], 'L0_attn_W_dq': _L0_attn_in['W_dq'], 'L0_attn_W_uq': _L0_attn_in['W_uq'], 'L0_attn_W_qr': _L0_attn_in['W_qr'], 'L0_attn_W_kr': _L0_attn_in['W_kr'], 'L0_attn_W_out': _L0_attn_in['W_out'], 'L0_attn_idx_wq': _L0_attn_in['idx_wq'], 'L0_attn_idx_wk': _L0_attn_in['idx_wk'], 'L0_attn_idx_w': _L0_attn_in['idx_w'], 'L0_attn_raw_delta': _L0_attn_in['raw_delta'], 'L0_xattn_Wq': _L0_xattn_in['Wq'], 'L0_xattn_bq': _L0_xattn_in['bq'], 'L0_xattn_Wk': _L0_xattn_in['Wk'], 'L0_xattn_bk': _L0_xattn_in['bk'], 'L0_xattn_Wv': _L0_xattn_in['Wv'], 'L0_xattn_bv': _L0_xattn_in['bv'], 'L0_xattn_Wo': _L0_xattn_in['Wo'], 'L0_xattn_bo': _L0_xattn_in['bo'], 'L0_ffn_w_gate': _L0_ffn_in['w_gate'], 'L0_ffn_w_up': _L0_ffn_in['w_up'], 'L0_ffn_w_down': _L0_ffn_in['w_down'], 'L1_attn_Wq': _L1_attn_in['Wq'], 'L1_attn_Wk': _L1_attn_in['Wk'], 'L1_attn_Wv': _L1_attn_in['Wv'], 'L1_attn_Wo': _L1_attn_in['Wo'], 'L1_attn_Wf': _L1_attn_in['Wf'], 'L1_attn_delta': _L1_attn_in['delta'], 'L1_attn_norm_weight': _L1_attn_in['norm_weight'], 'L1_xattn_Wq': _L1_xattn_in['Wq'], 'L1_xattn_Wk': _L1_xattn_in['Wk'], 'L1_xattn_Wv': _L1_xattn_in['Wv'], 'L1_xattn_hist_W': _L1_xattn_in['hist_W'], 'L1_xattn_hist_b': _L1_xattn_in['hist_b'], 'L1_xattn_hist_ln_g': _L1_xattn_in['hist_ln_g'], 'L1_xattn_hist_ln_b': _L1_xattn_in['hist_ln_b'], 'L1_xattn_ctx_W1': _L1_xattn_in['ctx_W1'], 'L1_xattn_ctx_b1': _L1_xattn_in['ctx_b1'], 'L1_xattn_ctx_W2': _L1_xattn_in['ctx_W2'], 'L1_xattn_ctx_b2': _L1_xattn_in['ctx_b2'], 'L1_xattn_kg_W1': _L1_xattn_in['kg_W1'], 'L1_xattn_kg_b1': _L1_xattn_in['kg_b1'], 'L1_xattn_kg_ln_g': _L1_xattn_in['kg_ln_g'], 'L1_xattn_kg_ln_b': _L1_xattn_in['kg_ln_b'], 'L1_xattn_kg_W2': _L1_xattn_in['kg_W2'], 'L1_xattn_kg_b2': _L1_xattn_in['kg_b2'], 'L1_xattn_proj_W': _L1_xattn_in['proj_W'], 'L1_xattn_proj_b': _L1_xattn_in['proj_b'], 'L1_ffn_gate_w': _L1_ffn_in['gate_w'], 'L1_ffn_gate_bias': _L1_ffn_in['gate_bias'], 'L1_ffn_eg_w': _L1_ffn_in['eg_w'], 'L1_ffn_eu_w': _L1_ffn_in['eu_w'], 'L1_ffn_ed_w': _L1_ffn_in['ed_w'], 'L1_ffn_sg_w': _L1_ffn_in['sg_w'], 'L1_ffn_su_w': _L1_ffn_in['su_w'], 'L1_ffn_sd_w': _L1_ffn_in['sd_w']}

def reference(x, ctx_1024, mask_Bx1xS2_bf1, mask_SxS_bc0, L0_attn_W_dkv, L0_attn_W_uk, L0_attn_W_uv, L0_attn_W_dq, L0_attn_W_uq, L0_attn_W_qr, L0_attn_W_kr, L0_attn_W_out, L0_attn_idx_wq, L0_attn_idx_wk, L0_attn_idx_w, L0_attn_raw_delta, L0_xattn_Wq, L0_xattn_bq, L0_xattn_Wk, L0_xattn_bk, L0_xattn_Wv, L0_xattn_bv, L0_xattn_Wo, L0_xattn_bo, L0_ffn_w_gate, L0_ffn_w_up, L0_ffn_w_down, L1_attn_Wq, L1_attn_Wk, L1_attn_Wv, L1_attn_Wo, L1_attn_Wf, L1_attn_delta, L1_attn_norm_weight, L1_xattn_Wq, L1_xattn_Wk, L1_xattn_Wv, L1_xattn_hist_W, L1_xattn_hist_b, L1_xattn_hist_ln_g, L1_xattn_hist_ln_b, L1_xattn_ctx_W1, L1_xattn_ctx_b1, L1_xattn_ctx_W2, L1_xattn_ctx_b2, L1_xattn_kg_W1, L1_xattn_kg_b1, L1_xattn_kg_ln_g, L1_xattn_kg_ln_b, L1_xattn_kg_W2, L1_xattn_kg_b2, L1_xattn_proj_W, L1_xattn_proj_b, L1_ffn_gate_w, L1_ffn_gate_bias, L1_ffn_eg_w, L1_ffn_eu_w, L1_ffn_ed_w, L1_ffn_sg_w, L1_ffn_su_w, L1_ffn_sd_w):
    import jax
    import jax.numpy as jnp

    def _L0_attn_ref(x, W_dkv, W_uk, W_uv, W_dq, W_uq, W_qr, W_kr, W_out, idx_wq, idx_wk, idx_w, raw_delta):
        import jax, jax.numpy as jnp
        import numpy as np
        B, L = (2, 256)
        D_MODEL, D_CKV, D_CQ = (256, 64, 128)
        N_HEAD, D_HEAD, D_ROPE = (8, 64, 32)
        N_IDX_HEAD = 4
        K_TS, LW = (96, 64)
        ROPE_BASE = 10000.0

        def _pope(x, angles):
            cos, sin = (jnp.cos(angles), jnp.sin(angles))
            mu1, mu2 = jnp.split(jax.nn.softplus(x), 2, axis=-1)
            return jnp.concatenate([mu1 * cos - mu2 * sin, mu1 * sin + mu2 * cos], axis=-1)

        def _forward(x, W_dkv, W_uk, W_uv, W_dq, W_uq, W_qr, W_kr, W_out, idx_wq, idx_wk, idx_w, raw_delta):
            B_, L_, _ = x.shape
            c_kv = x @ W_dkv
            q_i = (x @ idx_wq).reshape(B_, L_, N_IDX_HEAD, D_HEAD)
            k_i = x @ idx_wk
            s_i = jax.nn.relu(jnp.einsum('bthd,bsd->bths', q_i, k_i))
            I = jnp.einsum('bths,h->bts', s_i, idx_w)
            qpos = jnp.arange(L_)[:, None]
            kpos = jnp.arange(L_)[None, :]
            local = (kpos >= qpos - LW + 1) & (kpos <= qpos)
            causal = kpos > qpos
            I = jnp.where(local[None], jnp.inf, I)
            I = jnp.where(causal[None], -jnp.inf, I)
            kk = min(K_TS, L_)
            _, idx = jax.lax.top_k(I, kk)
            bi = jnp.arange(B_)[:, None, None]
            key_c = (c_kv @ W_uk)[bi, idx].reshape(B_, L_, kk, N_HEAD, D_HEAD)
            value = (c_kv @ W_uv)[bi, idx].reshape(B_, L_, kk, N_HEAD, D_HEAD)
            c_q = x @ W_dq
            query_c = (c_q @ W_uq).reshape(B_, L_, N_HEAD, D_HEAD)
            half = D_ROPE // 2
            theta = 1.0 / ROPE_BASE ** (2.0 * jnp.arange(half, dtype=jnp.float32) / D_ROPE)
            delta = -2.0 * jnp.pi * jax.nn.sigmoid(raw_delta)
            angles_q = jnp.arange(L_, dtype=jnp.float32)[:, None] * theta[None, :] + delta
            query_r = _pope((c_q @ W_qr).reshape(B_, L_, N_HEAD, D_ROPE), angles_q[None, :, None, :])
            kr_sel = (x @ W_kr)[bi, idx]
            angles_k = jnp.arange(kk, dtype=jnp.float32)[:, None] * theta[None, :] + delta
            key_r = _pope(kr_sel, angles_k[None, None, :, :])
            scale = (D_HEAD + D_ROPE) ** (-0.5)
            q_c = query_c.transpose(0, 2, 1, 3)
            q_r = query_r.transpose(0, 2, 1, 3)
            k_c = key_c.transpose(0, 3, 1, 2, 4)
            v = value.transpose(0, 3, 1, 2, 4)
            scores = (jnp.einsum('bhld,bhlkd->bhlk', q_c, k_c) + jnp.einsum('bhld,blkd->bhlk', q_r, key_r)) * scale
            attn = jax.nn.softmax(scores.astype(jnp.float32), axis=-1).astype(v.dtype)
            out = jnp.einsum('bhlk,bhlkd->bhld', attn, v)
            out = out.transpose(0, 2, 1, 3).reshape(B_, L_, N_HEAD * D_HEAD)
            return out @ W_out
        return _forward(x, W_dkv, W_uk, W_uv, W_dq, W_uq, W_qr, W_kr, W_out, idx_wq, idx_wk, idx_w, raw_delta)

    def _L0_xattn_ref(Q, K, V, mask, Wq, bq, Wk, bk, Wv, bv, Wo, bo):
        import jax, jax.numpy as jnp
        import numpy as np
        D_MODEL = 256
        N_HEADS = 16
        D_K = D_MODEL // N_HEADS
        B, S, D = Q.shape
        H, dk = (N_HEADS, D_K)
        q = (Q @ Wq + bq).reshape(B, S, H, dk).transpose(0, 2, 1, 3)
        k = (K @ Wk + bk).reshape(B, S, H, dk).transpose(0, 2, 1, 3)
        v = (V @ Wv + bv).reshape(B, S, H, dk).transpose(0, 2, 1, 3)
        scores = jnp.einsum('bhqd,bhkd->bhqk', q, k) / jnp.sqrt(jnp.float32(dk))
        m = mask[:, None, :, :]
        scores = jnp.where(m, scores, jnp.float32(-1000000000.0))
        att = jax.nn.softmax(scores, axis=-1)
        out = jnp.einsum('bhqk,bhkd->bhqd', att, v)
        out = out.transpose(0, 2, 1, 3).reshape(B, S, D)
        return out @ Wo + bo

    def _L0_ffn_ref(x, w_gate, w_up, w_down):
        import jax, jax.numpy as jnp
        import numpy as np
        HIDDEN = 256
        INNER = 1024

        def _weight_quant(w):
            scale = 1.0 / jnp.clip(jnp.mean(jnp.abs(w)), 1e-05)
            wq = jnp.clip(jnp.round(w * scale), -1.0, 1.0) / scale
            return w + jax.lax.stop_gradient(wq - w)

        def _act_quant(x):
            scale = 127.0 / jnp.clip(jnp.max(jnp.abs(x), axis=-1, keepdims=True), 1e-05)
            xq = jnp.clip(jnp.round(x * scale), -128.0, 127.0) / scale
            return x + jax.lax.stop_gradient(xq - x)

        def _bitlinear(x, w):
            return jnp.einsum('bsi,oi->bso', _act_quant(x), _weight_quant(w))
        gate = jax.nn.silu(_bitlinear(x, w_gate))
        up = _bitlinear(x, w_up)
        return _bitlinear(gate * up, w_down)

    def _L1_attn_ref(x, Wq, Wk, Wv, Wo, Wf, delta, norm_weight):
        import jax, jax.numpy as jnp
        import numpy as np
        B, N, D, H, C = (4, 2048, 256, 16, 128)
        HD = D // H
        THRESHOLD = 0.99

        def _chunk_scan(qc, kc, vc, lf):
            mask = jnp.tril(jnp.ones((C, C), bool))

            def step(S, inputs):
                qb, kb, vb, lb = inputs
                o_inter = jnp.einsum('bhid,bhde->bhie', qb * jnp.exp(lb)[..., None], S)
                A = jnp.einsum('bhid,bhjd->bhij', qb, kb)
                diff = jnp.where(mask, lb[..., :, None] - lb[..., None, :], -jnp.inf)
                A = A * jnp.exp(diff)
                o_intra = jnp.einsum('bhij,bhjd->bhid', A, vb)
                tot = lb[..., -1]
                kd = kb * jnp.exp(tot[..., None, None] - lb[..., None])
                S_new = jnp.exp(tot)[..., None, None] * S + jnp.einsum('bhjd,bhje->bhde', kd, vb)
                return (S_new, o_inter + o_intra)
            S0 = jnp.zeros((qc.shape[1], H, HD, HD), qc.dtype)
            _, o = jax.lax.scan(step, S0, (qc, kc, vc, lf))
            return o
        b, n, d = x.shape
        q = jax.nn.silu(x @ Wq.T)
        k = jax.nn.silu(x @ Wk.T)
        v = x @ Wv.T
        log_f = jax.nn.log_sigmoid(x @ Wf.T + delta)
        nc = n // C

        def to_chunks(t):
            return t.reshape(b, nc, C, H, HD).transpose(1, 0, 3, 2, 4)
        qc, kc, vc = map(to_chunks, (q, k, v))
        lf = jnp.cumsum(log_f.reshape(b, nc, C, H).transpose(1, 0, 3, 2), axis=-1)
        o = _chunk_scan(qc, kc, vc, lf)
        o = o.transpose(1, 0, 3, 2, 4).reshape(b, n, d)
        o = o * jax.lax.rsqrt(jnp.mean(o * o, axis=-1, keepdims=True) + 1e-06) * norm_weight
        return o @ Wo.T

    def _L1_xattn_ref(x, historical_data, Wq, Wk, Wv, hist_W, hist_b, hist_ln_g, hist_ln_b, ctx_W1, ctx_b1, ctx_W2, ctx_b2, kg_W1, kg_b1, kg_ln_g, kg_ln_b, kg_W2, kg_b2, proj_W, proj_b, causal_mask):
        import jax, jax.numpy as jnp
        import numpy as np
        from jax import lax
        H = 16
        K1, K2 = (3, 3)
        LN_EPS = 1e-05

        def _ln(x, g, b):
            m = jnp.mean(x, axis=-1, keepdims=True)
            v = jnp.mean(jnp.square(x - m), axis=-1, keepdims=True)
            return (x - m) * lax.rsqrt(v + LN_EPS) * g + b

        def _gelu(x):
            return jax.nn.gelu(x, approximate=False)
        B, T, D = x.shape
        hd = D // H
        scale = hd ** (-0.5)
        q = (x @ Wq).reshape(B, T, H, hd).transpose(0, 2, 1, 3)
        k = (x @ Wk).reshape(B, T, H, hd).transpose(0, 2, 1, 3)
        v = (x @ Wv).reshape(B, T, H, hd).transpose(0, 2, 1, 3)
        attn = jnp.einsum('bhqd,bhkd->bhqk', q, k) * scale
        eh = _gelu(_ln(historical_data @ hist_W + hist_b, hist_ln_g, hist_ln_b))
        aw = _gelu(eh @ ctx_W1 + ctx_b1) @ ctx_W2 + ctx_b2
        aw = jax.nn.softmax(aw, axis=1)
        cc = jnp.sum(eh * aw, axis=1)
        kp = _gelu(_ln(cc @ kg_W1 + kg_b1, kg_ln_g, kg_ln_b)) @ kg_W2 + kg_b2
        kernels = jax.nn.softmax(kp.reshape(B, H, K1 * K2), axis=-1)
        kernels = kernels.reshape(B * H, 1, K1, K2)
        mask = causal_mask[None, None]
        attn0 = jnp.where(mask, 0.0, attn).reshape(1, B * H, T, T)
        attn = lax.conv_general_dilated(attn0, kernels, window_strides=(1, 1), padding=((K1 // 2, K1 // 2), (K2 // 2, K2 // 2)), feature_group_count=B * H, dimension_numbers=('NCHW', 'OIHW', 'NCHW')).reshape(B, H, T, T)
        attn = jnp.where(mask, -jnp.inf, attn)
        p = jax.nn.softmax(attn, axis=-1)
        out = jnp.einsum('bhqk,bhkd->bhqd', p, v)
        out = out.transpose(0, 2, 1, 3).reshape(B, T, D)
        return out @ proj_W + proj_b

    def _L1_ffn_ref(hidden_states, gate_w, gate_bias, eg_w, eu_w, ed_w, sg_w, su_w, sd_w):
        import jax, jax.numpy as jnp
        import numpy as np
        from jax import lax
        HIDDEN = 256
        INTER = 128
        E = 64
        K = 6
        G = 8
        TG = 4
        NSH = 2
        ISH = INTER * NSH

        def _moe_forward(hidden_states, gate_w, gate_bias, eg_w, eu_w, ed_w, sg_w, su_w, sd_w):
            B, S, H = hidden_states.shape
            x = hidden_states.reshape(-1, H)
            T = x.shape[0]
            shared = jax.nn.silu(x @ sg_w.T) * (x @ su_w.T) @ sd_w.T
            logits = x @ gate_w.T
            scores = jax.nn.sigmoid(logits) + gate_bias
            group_scores = scores.reshape(T, G, E // G).max(axis=-1)
            _, sel_groups = lax.top_k(group_scores, TG)
            group_mask = jnp.zeros((T, G), scores.dtype).at[jnp.arange(T)[:, None], sel_groups].set(1.0)
            mask = jnp.repeat(group_mask, E // G, axis=1)
            masked_scores = scores * mask
            topk_w, topk_i = lax.top_k(masked_scores, K)
            topk_w = topk_w / (topk_w.sum(axis=-1, keepdims=True) + 1e-08)
            comb = jnp.zeros((T, E), x.dtype).at[jnp.arange(T)[:, None], topk_i].add(topk_w)
            h = jax.nn.silu(jnp.einsum('th,eih->eti', x, eg_w)) * jnp.einsum('th,eih->eti', x, eu_w)
            routed = jnp.einsum('eti,ehi,te->th', h, ed_w, comb)
            return (shared + routed).reshape(B, S, H)
        return _moe_forward(hidden_states, gate_w, gate_bias, eg_w, eu_w, ed_w, sg_w, su_w, sd_w)
    x = _layernorm(x + _L0_attn_ref(x, L0_attn_W_dkv, L0_attn_W_uk, L0_attn_W_uv, L0_attn_W_dq, L0_attn_W_uq, L0_attn_W_qr, L0_attn_W_kr, L0_attn_W_out, L0_attn_idx_wq, L0_attn_idx_wk, L0_attn_idx_w, L0_attn_raw_delta), axis=-1)
    x = _layernorm(x + _L0_xattn_ref(x, ctx_1024, ctx_1024, mask_Bx1xS2_bf1, L0_xattn_Wq, L0_xattn_bq, L0_xattn_Wk, L0_xattn_bk, L0_xattn_Wv, L0_xattn_bv, L0_xattn_Wo, L0_xattn_bo), axis=-1)
    x = _layernorm(x + _L0_ffn_ref(x, L0_ffn_w_gate, L0_ffn_w_up, L0_ffn_w_down), axis=-1)
    x = _layernorm(x + _L1_attn_ref(x, L1_attn_Wq, L1_attn_Wk, L1_attn_Wv, L1_attn_Wo, L1_attn_Wf, L1_attn_delta, L1_attn_norm_weight), axis=-1)
    x = _layernorm(x + _L1_xattn_ref(x, ctx_1024, L1_xattn_Wq, L1_xattn_Wk, L1_xattn_Wv, L1_xattn_hist_W, L1_xattn_hist_b, L1_xattn_hist_ln_g, L1_xattn_hist_ln_b, L1_xattn_ctx_W1, L1_xattn_ctx_b1, L1_xattn_ctx_W2, L1_xattn_ctx_b2, L1_xattn_kg_W1, L1_xattn_kg_b1, L1_xattn_kg_ln_g, L1_xattn_kg_ln_b, L1_xattn_kg_W2, L1_xattn_kg_b2, L1_xattn_proj_W, L1_xattn_proj_b, mask_SxS_bc0), axis=-1)
    x = _layernorm(x + _L1_ffn_ref(x, L1_ffn_gate_w, L1_ffn_gate_bias, L1_ffn_eg_w, L1_ffn_eu_w, L1_ffn_ed_w, L1_ffn_sg_w, L1_ffn_su_w, L1_ffn_sd_w), axis=-1)
    return x

_drawn_inputs = setup_inputs


def setup_inputs(seed=0):
    import zlib

    import numpy as np

    out = dict(_drawn_inputs(seed))
    spreads = {'L0_attn_idx_w': (1.0, 0.6),
     'L0_xattn_bq': (0.0, 0.282),
     'L0_xattn_bk': (0.0, 2.0),
     'L0_xattn_bv': (0.0, 0.1),
     'L0_xattn_bo': (0.0, 0.1),
     'L1_attn_delta': (4.595119953155518, 0.2),
     'L1_attn_norm_weight': (1.0, 0.2),
     'L1_xattn_hist_b': (0.0, 0.8),
     'L1_xattn_hist_ln_g': (1.0, 0.6),
     'L1_xattn_hist_ln_b': (0.0, 0.8),
     'L1_xattn_ctx_b1': (0.0, 2.0),
     'L1_xattn_kg_b1': (0.0, 0.8),
     'L1_xattn_kg_ln_g': (1.0, 0.6),
     'L1_xattn_kg_ln_b': (0.0, 0.8),
     'L1_xattn_kg_b2': (0.0, 0.8),
     'L1_xattn_proj_b': (0.0, 0.1),
     'L1_ffn_gate_bias': (0.0, 0.8)}
    factors = {'L0_attn_raw_delta': 64.0,
     'L1_attn_Wf': 6.54,
     'L1_xattn_hist_W': 2.857,
     'L1_xattn_ctx_W1': 8.0,
     'L1_xattn_ctx_W2': 8.0,
     'L1_ffn_gate_w': 8.0,
     'L1_ffn_eg_w': 8.0,
     'L1_ffn_eu_w': 8.0,
     'L1_ffn_ed_w': 8.0,
     'L1_ffn_sg_w': 3.168,
     'L1_ffn_su_w': 3.277,
     'L1_ffn_sd_w': 3.185}
    for name, (base, spread) in spreads.items():
        noise = np.random.default_rng([zlib.crc32(name.encode()), seed]).standard_normal(out[name].shape)
        drawn = base * np.exp(spread * noise) if base else spread * noise
        out[name] = jnp.asarray(drawn.astype(out[name].dtype))
    for name, factor in factors.items():
        out[name] = (out[name] * factor).astype(out[name].dtype)
    return out
```

```python
from contextlib import ExitStack

import numpy as np

import concourse.bass as bass
from concourse import mybir

F32 = mybir.dt.float32
BF16 = mybir.dt.bfloat16
U8 = mybir.dt.uint8
U32 = mybir.dt.uint32
ALU = mybir.AluOpType
ACT = mybir.ActivationFunctionType
AX = mybir.AxisListType

B, S, D = 16, 128, 256
P = 128
KC = D // P
BANK = 512
MAGIC = 1.5 * 2.0**23
LN_EPS = 1e-5
E, TOP_K = 64, 6
TILES_OF_ROWS = (B * S * TOP_K + E * (P - 1)) // P + 1
CLEAR = TILES_OF_ROWS // B


class Phase:

    def __init__(self, nc, ctx, name):
        self.nc, self.ctx, self.name, self.semaphores = nc, ctx, name, []
        ctx.callback(self.clear)

    def clear(self):
        self.nc.clear_and_free_semaphores(self.semaphores)
        self.nc.all_engine_barrier()

    def sb(self, name, shape, dt=F32):
        return self.ctx.enter_context(self.nc.sbuf_tensor(f"{self.name}_{name}", shape, dt))

    def bank(self, name, dt=F32):
        return self.ctx.enter_context(self.nc.psum_tensor(f"{self.name}_{name}", [P, BANK * (2 if dt == BF16 else 1)], dt))

    def sem(self, name):
        self.semaphores.append(self.nc.alloc_semaphore(name=f"{self.name}_{name}"))
        return self.semaphores[-1]

    def sems(self, name, n=2):
        return [self.sem(f"{name}{i}") for i in range(n)]


def wait(eng, sem, value):
    if not isinstance(value, int) or value > 0:
        eng.wait_ge(sem, value)


def landed(b, i, loads=1, buffers=2):
    return 16 // buffers * loads * (b - i) + 16 * loads


def pipeline(eng, stages, n=B, body=2):
    most = max(lag for lag, _ in stages)
    peel = -(-most // body) * body + body

    def straight(times):
        for t in times:
            for lag, f in stages:
                if 0 <= t - lag < n:
                    f(t - lag, (t - lag) % body)

    straight(range(peel))
    with eng.Fori(peel // body, n // body) as m:
        for k in range(body):
            for lag, f in stages:
                f(body * m + (k - lag), (k - lag) % body)
    straight(range(n, n + most))


def tokens(dram, b):
    return dram[bass.ds(b, 1)].rearrange("o p d -> (o p) d")


def to_all(row, parts=P):
    return row.rearrange("(o n) -> o n", o=1).to_broadcast([parts, row.shape[0]])


class LayerNorm:

    def __init__(self, ph, eps=LN_EPS, tag="ln"):
        self.nc, self.eps = ph.nc, eps
        self.stats, self.mv = ph.sb(tag + "_stats", [P, 6]), ph.sb(tag + "_mv", [P, 2])
        self.var, self.rstd, self.half = ph.sb(tag + "_var", [P, 1]), ph.sb(tag + "_rstd", [P, 1]), ph.sb(tag + "_half", [P, 1])
        self.one = ph.sb(tag + "_one", [P, 1])
        self.spare = ph.sb(tag + "_spare", [P, 1])
        self.s_half = ph.sem(tag + "_half")
        self.s_stats = ph.sem(tag + "_stats")
        self.s_rstd, self.s_done = ph.sem(tag + "_rstd"), ph.sem(tag + "_done")

    def constants(self, pool):
        self.nc.gpsimd.memset(self.half[:], -0.5).then_inc(self.s_half, 1)
        self.nc.gpsimd.memset(self.one[:], 1.0).then_inc(self.s_half, 1)
        pool.wait_ge(self.s_half, 2)

    def statistics(self, dve, y, b):
        nc = self.nc
        nc.vector.bn_stats(self.stats[:], y).then_inc(self.s_stats, 1)
        dve.wait_ge(self.s_stats, 3 * b + 1)
        nc.vector.memset(self.spare[:], 0.0)
        nc.vector.bn_aggr(self.mv[:], self.stats[:]).then_inc(self.s_stats, 1)
        dve.wait_ge(self.s_stats, 3 * b + 2)
        wait(dve, self.s_rstd, b)
        nc.vector.tensor_scalar(self.var[:], self.mv[:, 1:2], self.eps, None, ALU.add).then_inc(self.s_stats, 1)

    def power(self, pool, b):
        pool.wait_ge(self.s_stats, 3 * b + 3)
        wait(pool, self.s_done, b)
        self.nc.gpsimd.tensor_tensor(self.rstd[:], self.var[:], self.half[:], ALU.pow).then_inc(self.s_rstd, 1)

    def result(self, dve, y, xo, b):
        dve.wait_ge(self.s_rstd, b + 1)
        self.nc.vector.tensor_scalar(xo, y, self.mv[:, 0:1], self.rstd[:], ALU.subtract, ALU.mult).then_inc(self.s_done, 1)


def lagged(b, n, last=B):
    return min(b + n, last) if isinstance(b, int) else b + n


HA, DH, DR = 8, 64, 32
HI, W = 4, 64
TOP = 96
SORTED = TOP - W
NEVER = -1e30


def rank_keys_0(nc, x_in, ranks, hidden, w):
    with ExitStack() as ctx:
        ph = Phase(nc, ctx, "rk0")
        NP = B // 2
        wq, wk = ph.sb("wq", [P, KC, HI * DH]), ph.sb("wk", [P, KC, P])
        wi, ident = ph.sb("wi", [P, HI]), ph.sb("ident", [P, P])
        cap, floor, never = ph.sb("cap", [P, W]), ph.sb("floor", [P, W]), ph.sb("never", [P, W])
        later = ph.sb("later", [P, 8, 8], BF16)
        x, xT = ph.sb("x", [P, 2, 2, D]), ph.sb("xT", [P, 2, KC, S])
        qT, kT = ph.sb("qT", [P, 2, 2, W]), ph.sb("kT", [P, 2, W])
        r, index0, index = ph.sb("r", [P, HI, W]), ph.sb("index0", [P, W]), ph.sb("index", [P, W])
        before = ph.sb("before", [P, W, W], BF16)
        same, tie = ph.sb("same", [P, 8, 8, 8], BF16), ph.sb("tie", [P, W])
        count, rank0 = ph.sb("count", [P, W]), ph.sb("rank0", [P, W])
        rank, hid = ph.sb("rank", [P, 2, W], BF16), ph.sb("hid", [P, 2, S], BF16)
        pT, pQ, pK, pI = ph.bank("pT"), ph.bank("pQ"), ph.bank("pK"), [ph.bank("pI0"), ph.bank("pI1")]
        s_r = ph.sem("r")
        s_w, s_x, s_stored = ph.sem("weights"), ph.sems("x"), ph.sems("stored")
        s_turned, s_xT, s_q, s_qs, s_i, s_iv, s_rank, s_hid = (ph.sem(n) for n in ("turned", "xT", "q", "qs", "i", "iv", "rank", "hid"))
        block = ctx.enter_context(nc.Block())
        loads = [
            (wq[:], w["L0_attn_idx_wq"].rearrange("(c p) n -> p c n", p=P)), (wk[:], w["L0_attn_idx_wk_twice"].rearrange("(c p) n -> p c n", p=P)),
            (wi[:], to_all(w["L0_attn_idx_w"])), (ident[:], w["ident"]), (cap[:], w["rank_cap"]), (floor[:], w["rank_floor"]),
            (never[:], w["rank_never"]), (later[:], w["rank_later"]),
            (hid[:, 0, :], w["rank_hidden"]), (hid[:, 1, :], w["rank_hidden"]),
        ]
        NV = 17 + 3 + 2

        @block.sync
        def _(sp):
            for to, of in loads:
                sp.dma_start(to, of).then_inc(s_w, 16)

            def load(b, i):
                wait(sp, s_turned, b - 1)
                sp.dma_start(x[:, i, :, :], x_in[bass.ds(2 * b, 2)].rearrange("o p d -> p o d")).then_inc(s_x[i], 16)

            pipeline(sp, [(0, load)], n=NP)

        @block.tensor
        def _(pe):
            pe.wait_ge(s_w, 16 * len(loads))

            def index_scores(b, i):
                pe.wait_ge(s_x[i], landed(b, i))
                wait(pe, s_xT, b)
                for o in range(2):
                    for k in range(KC):
                        t = nc.tensor.transpose(pT[:, (2 * o + k) * P:(2 * o + k + 1) * P], x[:, i, o, k * P:(k + 1) * P], ident[:])
                t.then_inc(s_turned, 1)
                pe.wait_ge(s_xT, b + 1)
                wait(pe, s_qs, 2 * b)
                for m in range(2):
                    for k in range(KC):
                        nc.tensor.matmul(pQ[:, m * P:(m + 1) * P].rearrange("p (o t) -> p o t", o=2), wq[:, k, m * P:(m + 1) * P],
                                         xT[:, :, k, W:S], start=k == 0, stop=k == KC - 1)
                for k in range(KC):
                    mm = nc.tensor.matmul(pK[:, 0:P].rearrange("p (o t) -> p o t", o=2), wk[:, k, :], xT[:, :, k, 0:W], start=k == 0, stop=k == KC - 1)
                mm.then_inc(s_q, 1)
                pe.wait_ge(s_qs, 2 * b + 2)
                wait(pe, s_r, 2 * b)
                nc.tensor.matmul(pK[:, P:P + 2], ident[:], ident[:, 0:2], start=True, stop=True)
                for o in range(2):
                    for h in range(HI):
                        rows = slice(64 * (h % 2), 64 * (h % 2) + DH)
                        mm = nc.tensor.matmul(pI[h % 2][64 * o:64 * o + W, (h // 2) * W:(h // 2 + 1) * W], qT[rows, h // 2, o, :], kT[rows, o, :],
                                              start=True, stop=True)
                mm.then_inc(s_i, 1)

            pipeline(pe, [(0, index_scores)], n=NP)

        @block.scalar
        def _(act):
            def copies(b, i):
                act.wait_ge(s_turned, b + 1)
                wait(act, s_q, b)
                nc.scalar.activation(xT[:].rearrange("p a b c -> p (a b c)"), pT[:], ACT.Copy).then_inc(s_xT, 1)
                act.wait_ge(s_q, b + 1)
                wait(act, s_i, b)
                nc.scalar.activation(qT[:].rearrange("p a b c -> p (a b c)"), pQ[:, 0:2 * P], ACT.Copy).then_inc(s_qs, 1)
                nc.scalar.activation(kT[:].rearrange("p a b -> p (a b)"), pK[:, 0:P], ACT.Copy).then_inc(s_qs, 1)

            def store(b, i):
                act.wait_ge(s_rank, b + 1)
                act.wait_ge(s_hid, b + 1)
                act.dma_start(ranks[bass.ds(2 * b, 2)].rearrange("o t j -> (o t) j"), rank[:, i, :]).then_inc(s_stored[i], 16)
                act.dma_start(hidden[bass.ds(2 * b, 2)].rearrange("o t j -> (o t) j"), hid[:, i, :]).then_inc(s_stored[i], 16)

            pipeline(act, [(0, copies), (1, store)], n=NP)
            for i in range(2):
                act.wait_ge(s_stored[i], 16 * NP)

        @block.vector
        def _(dve):
            dve.wait_ge(s_w, 16 * len(loads))

            def rank_all(b, i):
                dve.wait_ge(s_i, b + 1)
                for e in range(2):
                    nc.vector.scalar_tensor_tensor(r[:, e::2, :], pI[e][:, 0:2 * W].rearrange("p (m j) -> p m j", m=2), 0.0,
                                                   wi[:, e::2].unsqueeze(2).to_broadcast([P, 2, W]), ALU.max, ALU.mult).then_inc(s_r, 1)
                dve.wait_ge(s_r, 2 * b + 2)
                nc.vector.tensor_reduce(index0[:], r[:].rearrange("p h j -> p j h"), AX.X, ALU.add).then_inc(s_iv, 1)
                dve.wait_ge(s_iv, NV * b + 1)
                nc.vector.tensor_tensor(index[:], index0[:], cap[:], ALU.min).then_inc(s_iv, 1)
                dve.wait_ge(s_iv, NV * b + 2)
                for n in range(8):
                    js = slice(8 * n, 8 * n + 8)
                    mine = index[:, js].unsqueeze(2)
                    low = 8 * n + 8
                    nc.vector.tensor_tensor(before[:, js, 0:low], index[:, 0:low].unsqueeze(1).to_broadcast([P, 8, low]),
                                            mine.to_broadcast([P, 8, low]), ALU.is_ge).then_inc(s_iv, 1)
                    if low < W:
                        nc.vector.tensor_tensor(before[:, js, low:W], index[:, low:W].unsqueeze(1).to_broadcast([P, 8, W - low]),
                                                mine.to_broadcast([P, 8, W - low]), ALU.is_gt).then_inc(s_iv, 1)
                blocks = index[:].rearrange("p (n j) -> p n j", j=8)
                nc.vector.tensor_tensor(same[:], blocks.unsqueeze(2).to_broadcast([P, 8, 8, 8]), blocks.unsqueeze(3).to_broadcast([P, 8, 8, 8]),
                                        ALU.is_equal).then_inc(s_iv, 1)
                dve.wait_ge(s_iv, NV * b + 18)
                nc.vector.tensor_tensor(same[:], same[:], later[:].unsqueeze(1).to_broadcast([P, 8, 8, 8]), ALU.mult).then_inc(s_iv, 1)
                nc.vector.tensor_reduce(count[:], before[:], AX.X, ALU.add).then_inc(s_iv, 1)
                dve.wait_ge(s_iv, NV * b + 20)
                nc.vector.tensor_reduce(tie[:], same[:].rearrange("p n j k -> p (n j) k"), AX.X, ALU.add).then_inc(s_iv, 1)
                dve.wait_ge(s_iv, NV * b + 21)
                nc.vector.tensor_tensor(rank0[:], count[:], tie[:], ALU.subtract).then_inc(s_iv, 1)
                dve.wait_ge(s_iv, NV * b + 22)
                wait(dve, s_stored[i], landed(b - 2, i, 2))
                nc.vector.tensor_tensor(rank[:, i, :], rank0[:], floor[:], ALU.max).then_inc(s_rank, 1)
                nc.vector.scalar_tensor_tensor(hid[:, i, 0:W], rank0[:], float(SORTED), never[:], ALU.is_ge, ALU.mult).then_inc(s_hid, 1)

            pipeline(dve, [(0, rank_all)], n=NP)


def sparse_attention_0(nc, x_in, x_out, w, ranks=None, hidden=None):
    with ExitStack() as ctx:
        ph = Phase(nc, ctx, "sa0")
        LATE = S - W
        Q4 = LATE // 4
        NT = HA // 2
        SCALE = float(DH + DR) ** -0.5
        PI = 3.1415925
        wdq, wdkv, wkr = ph.sb("wdq", [P, KC, P]), ph.sb("wdkv", [P, KC, DH]), ph.sb("wkr", [P, KC, 2, P])
        wuq, wuk, wuv = ph.sb("wuq", [P, BANK]), ph.sb("wuk", [DH, BANK]), ph.sb("wuv", [DH, BANK])
        wqr, wout = ph.sb("wqr", [P, HA, P]), ph.sb("wout", [P, NT, D])
        ident, identb = ph.sb("ident", [P, P]), ph.sb("identb", [P, P], BF16)
        fold = ph.sb("fold", [P, P])
        trig = ph.sb("trig", [P, 3, 2, P])
        srt = ph.sb("srt", [TOP, 2, 2, DR])
        raw_c, raw_r, sel = ph.sb("raw_c", [P, 1]), ph.sb("raw_r", [TOP, DR]), ph.sb("sel", [TOP, 1])
        local, future = ph.sb("local", [P, W]), ph.sb("future", [P, W])
        ang = [ph.sb(f"ang{n}", [P, 1 + DR]) for n in range(5)]
        cs = ph.sb("cs", [P, 2, 1 + DR])
        tab, tab2 = ph.sb("tab", [P, 3, P]), ph.sb("tab2", [P, 3, P])
        st, st2 = ph.sb("st", [TOP, 2, DR]), ph.sb("st2", [TOP, 2, DR])
        part, parts = [ph.sb(f"part{n}", [TOP, 2, DR], BF16) for n in range(3)], ph.sb("parts", [TOP, 2, DR], BF16)
        x, xr, xT = ph.sb("x", [P, 2, D]), ph.sb("xr", [P, 2, D]), ph.sb("xT", [P, KC, P])
        rank, onehot = ph.sb("rank", [TOP, 2, LATE * W], BF16), ph.sb("onehot", [TOP, 2, LATE * W], BF16)
        hid = ph.sb("hid", [W, 2, S], BF16)
        low = ph.sb("low", [P, 2, P])
        kmin, kexp, kmu, krot = ph.sb("kmin", [P, 2 * P]), ph.sb("kexp", [P, 2 * P]), ph.sb("kmu", [P, 2 * P]), ph.sb("krot", [P, 2, P])
        qc, kc, v = ph.sb("qc", [P, 2, NT, 2, P]), ph.sb("kc", [P, 2, NT, P]), ph.sb("v", [P, 2, HA, DH + 1])
        qmin, qmu = ph.sb("qmin", [P, 2, BANK]), ph.sb("qmu", [P, 2, BANK])
        qrot = ph.sb("qrot", [P, 2, HA, P])
        ka, kb = ph.sb("ka", [P, 2, P]), ph.sb("kb", [P, 2, P])
        ql = ph.sb("ql", [P, 2, Q4, 4, HA])
        g1, g2, ks = ph.sb("g1", [P, BANK]), ph.sb("g2", [P, BANK]), ph.sb("ks", [P, 2, Q4, W])
        sa, sb_ = ph.sb("sa", [TOP, BANK]), ph.sb("sbb", [P, BANK])
        m1, m2 = ph.sb("m1", [P, BANK]), ph.sb("m2", [P, BANK])
        neg, rs = ph.sb("neg", [P, 2, NT]), ph.sb("rs", [P, 2, NT])
        pa, pb = ph.sb("pa", [P, NT, TOP]), ph.sb("pb", [P, NT, P])
        paT, pbT = ph.sb("paT", [TOP, BANK]), ph.sb("pbT", [P, BANK])
        rinv, o, oT = ph.sb("rinv", [P, HA]), ph.sb("o", [P, HA * DH]), ph.sb("oT", [P, NT, P])
        y, xo = ph.sb("y", [P, 2, D]), ph.sb("xo", [P, 2, D])
        ln = LayerNorm(ph)
        pT, p1, pA, pB = ph.bank("pT"), ph.bank("p1"), ph.bank("pA"), ph.bank("pB")
        bA, b1, b2, b3 = ph.bank("bA"), ph.bank("b1"), ph.bank("b2"), ph.bank("b3")
        names = ("weights const tab turned xTs xr low lows kmin kexp kmu krot onehot qk qcs kcs v vs qr qmin qexp qmu qrot fold ql "
                 "g gs ks s sab m st stn max prob pt pts o rinv on oT oTs y ys").split()
        s = {n: ph.sem(n) for n in names}
        s_set, s_ang, s_ang2 = ph.sem("set"), ph.sem("ang"), ph.sem("ang2")
        s_x, s_rank, s_stored = ph.sems("x"), ph.sems("rank"), ph.sems("stored")
        block = ctx.enter_context(nc.Block())
        g = lambda n: w["L0_attn_" + n]
        loads = [
            (wdq[:], g("W_dq").rearrange("(c p) n -> p c n", p=P)), (wdkv[:], g("W_dkv").rearrange("(c p) n -> p c n", p=P)),
            (wkr[:], g("W_kr_copies").rearrange("(c p) (a n) -> p c a n", p=P, a=2)), (wuq[:], g("W_uq")), (wuk[:], g("W_uk")), (wuv[:], g("W_uv")),
            (wqr[:], g("W_qr_copies").rearrange("p (h n) -> p h n", h=HA)), (wout[:], g("W_out").rearrange("(c p) n -> p c n", p=P)),
            (ident[:], w["ident"]), (identb[:], w["ident_bf16"]), (fold[:], w["rope_fold"]), (trig[:], w["rope_trig"]), (srt[:], w["rope_sorted"]),
            (raw_c[:], g("raw_columns")), (raw_r[:], g("raw_rows").to_broadcast([TOP, DR])), (sel[:], w["rope_rank_of_row"]),
            (local[:], w["rope_local"]), (future[:], w["rope_future"]),
        ]
        NZ = 6

        @block.sync
        def _(sp):
            for to, of in loads:
                sp.dma_start(to, of).then_inc(s["weights"], 16)

            def load(b, i):
                wait(sp, s["xr"], b - 1)
                wait(sp, s["turned"], b - 1)
                sp.dma_start(x[:, i, :], tokens(x_in, b)).then_inc(s_x[i], 16)
                wait(sp, s["onehot"], b - 1)
                wait(sp, s["s"], b - 1)
                sp.dma_start(rank[:, i, :], ranks[bass.ds(b, 1)].rearrange("o t j -> o (t j)").to_broadcast([TOP, LATE * W])).then_inc(s_rank[i], 16)
                sp.dma_start(hid[:, i, :], hidden[bass.ds(b, 1)].rearrange("o t j -> (o t) j")).then_inc(s_rank[i], 16)

            pipeline(sp, [(0, load)])

        @block.gpsimd
        def _(pool):
            ln.constants(pool)
            for t in (qc, ka, kb, ql):
                nc.gpsimd.memset(t[:], 0.0).then_inc(s["const"], 1)
            nc.gpsimd.memset(v[:], 1.0).then_inc(s["const"], 1)
            nc.gpsimd.memset(rs[:], 0.0).then_inc(s["const"], 1)

            def keep(b, i):
                pool.wait_ge(s_x[i], landed(b, i))
                wait(pool, s["ys"], b - 1)
                nc.gpsimd.tensor_tensor(xr[:, i, :], x[:, i, :], ln.one[:].to_broadcast([P, D]), ALU.mult).then_inc(s["xr"], 1)

            def sorted_keys(b, i):
                for n in range(2):
                    pool.wait_ge(s["gs"], 4 * b + 2 * n + 2)
                    nc.gpsimd.tensor_tensor(ks[:, i, 8 * n:8 * n + 8, :].rearrange("p t j -> p (t j)"), g1[:], g2[:], ALU.add).then_inc(s["ks"], 1)

            def mix(b, i):
                pool.wait_ge(s["m"], 2 * b + 2)
                nc.gpsimd.tensor_tensor(m1[:], m1[:], m2[:], ALU.add).then_inc(s["sab"], 1)

            pipeline(pool, [(2, lambda b, i: ln.power(pool, b)), (0, keep), (1, mix), (0, sorted_keys)])

        @block.tensor
        def _(pe):
            pe.wait_ge(s["weights"], 16 * len(loads))
            pe.wait_ge(s["const"], NZ)
            pe.wait_ge(s["tab"], 1)

            def low_rank(b, i):
                pe.wait_ge(s_x[i], landed(b, i))
                wait(pe, s["vs"], b)
                wait(pe, s["oTs"], b - 1)
                for k in range(KC):
                    t = nc.tensor.transpose(pT[:, k * P:(k + 1) * P], x[:, i, k * P:(k + 1) * P], ident[:])
                t.then_inc(s["turned"], 1)
                pe.wait_ge(s["xTs"], b + 1)
                wait(pe, s["ys"], b - 1)
                for k in range(KC):
                    nc.tensor.matmul(p1[:, 0:P], wdq[:, k, :], xT[:, k, :], start=k == 0, stop=k == KC - 1)
                for k in range(KC):
                    nc.tensor.matmul(p1[0:DH, P:2 * P], wdkv[:, k, :], xT[:, k, :], start=k == 0, stop=k == KC - 1)
                for a in range(2):
                    for k in range(KC):
                        mm = nc.tensor.matmul(p1[:, (2 + a) * P:(3 + a) * P], wkr[:, k, a, :], xT[:, k, :], start=k == 0, stop=k == KC - 1)
                mm.then_inc(s["low"], 1)

            def content(b, i):
                pe.wait_ge(s["lows"], 2 * b + 2)
                wait(pe, s["gs"], 4 * b)
                for t in range(NT):
                    mm = nc.tensor.matmul(pA[:, t * P:(t + 1) * P], wuq[:, t * P:(t + 1) * P], low[:, 0, :], start=True, stop=True)
                for t in range(NT):
                    mm = nc.tensor.matmul(pB[:, t * P:(t + 1) * P], wuk[:, t * P:(t + 1) * P], low[0:DH, 1, :], start=True, stop=True)
                mm.then_inc(s["qk"], 1)
                mm = nc.tensor.matmul(pT[:], low[0:DH, 1, :], wuv[:], start=True, stop=True)
                mm.then_inc(s["v"], 1)

            def rotary(b, i):
                pe.wait_ge(s["qcs"], 2 * b + 2)
                pe.wait_ge(s["kcs"], b + 1)
                for h in range(HA):
                    bank = pA if h < 4 else pB
                    mm = nc.tensor.matmul(bank[:, (h % 4) * P:(h % 4 + 1) * P], wqr[:, h, :], low[:, 0, :], start=True, stop=True)
                    if h % 4 == 3:
                        mm.then_inc(s["qr"], 1)

            def sorted_tables(b, i):
                pe.wait_ge(s["qrot"], 2 * b + 2)
                nc.tensor.matmul(pA[:].rearrange("p (h t) -> p h t", h=HA), fold[:], qrot[:, i, :, W:S], start=True, stop=True).then_inc(s["fold"], 1)
                pe.wait_ge(s["onehot"], b + 1)
                for n in range(2):
                    pe.wait_ge(s["ql"], 4 * b + 4)
                    wait(pe, s["gs"], 4 * b + 2 * n)
                    for c, bank in enumerate((pA, pB)):
                        for q in range(4):
                            at = (q * Q4 + 8 * n) * W
                            mm = nc.tensor.matmul(bank[32 * q:32 * q + 32, :], parts[:, c, :], onehot[:, i, at:at + BANK], start=True, stop=True)
                    mm.then_inc(s["g"], 1)

            def scores(b, i):
                pe.wait_ge(s["ks"], 2 * b + 2)
                pe.wait_ge(s["krot"], 3 * b + 3)
                wait(pe, s["on"], 2 * b)
                wait(pe, s["pts"], 2 * b)
                nc.tensor.matmul(b1[:].rearrange("p (h t) -> p h t", h=HA), hid[:, i, :], identb[0:W, 0:W].unsqueeze(1).to_broadcast([W, HA, W]),
                                 start=True, stop=False, skip_group_check=True)
                nc.tensor.matmul(b3[:].rearrange("p (h t) -> p h t", h=HA), ka[:, i, :], qrot[:, i, :, W:S], start=True, stop=True)
                nc.tensor.matmul(b2[:].rearrange("p (h t) -> p h t", h=HA), kb[:, i, :], qrot[:, i, :, W:S], start=True, stop=True)
                nc.tensor.matmul(bA[0:TOP, :].rearrange("p (h t) -> p h t", h=HA), ka[:, i, 0:TOP], qrot[:, i, :, 0:W],
                                 start=True, stop=False, skip_group_check=True)
                for t in range(NT):
                    nc.tensor.matmul(bA[0:TOP, t * P:(t + 1) * P].rearrange("p (h t) -> p h t", h=2), kc[:, i, t, 0:TOP], qc[:, i, t, :, 0:W],
                                     start=False, stop=False, skip_group_check=True)
                for t in range(NT):
                    nc.tensor.matmul(b1[:, t * P:(t + 1) * P].rearrange("p (h t) -> p h t", h=2), kc[:, i, t, :], qc[:, i, t, :, W:S],
                                     start=False, stop=False, skip_group_check=True)
                by_quarter = b1[0:W, :].rearrange("p (h q t) -> p q h t", h=HA, q=4)
                for t in range(Q4):
                    mm = nc.tensor.matmul(by_quarter[:, :, :, t], ks[:, i, t, :], ql[:, i, t, :, :],
                                          start=False, stop=t == Q4 - 1, skip_group_check=True)
                mm.then_inc(s["s"], 1)

            def turn_scores(b, i):
                pe.wait_ge(s["st"], 2 * b + 2)
                for t in range(NT):
                    nc.tensor.transpose(bA[:, t * TOP:(t + 1) * TOP], sa[:, t * P:(t + 1) * P], ident[0:TOP, 0:TOP])
                for t in range(NT):
                    mm = nc.tensor.transpose(b1[:, t * P:(t + 1) * P], sb_[:, t * P:(t + 1) * P], ident[:])
                mm.then_inc(s["stn"], 1)

            def turn_probabilities(b, i):
                pe.wait_ge(s["prob"], 2 * b + 2)
                for t in range(NT):
                    nc.tensor.transpose(b2[0:TOP, t * P:(t + 1) * P], pa[:, t, :], ident[:])
                for t in range(NT):
                    mm = nc.tensor.transpose(b3[:, t * P:(t + 1) * P], pb[:, t, :], ident[:])
                mm.then_inc(s["pt"], 1)

            def values(b, i):
                pe.wait_ge(s["pts"], 2 * b + 2)
                for h in range(HA):
                    bank = bA if h < 4 else b1
                    at = (h % 4) * (DH + 1)
                    nc.tensor.matmul(bank[0:W, at:at + DH + 1], paT[:, h * W:(h + 1) * W], v[0:TOP, i, h, :], start=True, stop=True)
                    mm = nc.tensor.matmul(bank[W:S, at:at + DH + 1], pbT[:, h * W:(h + 1) * W], v[:, i, h, :], start=True, stop=True)
                mm.then_inc(s["o"], 1)

            def output(b, i):
                pe.wait_ge(s["on"], 2 * b + 2)
                pe.wait_ge(s["vs"], lagged(b, 2))
                for t in range(NT):
                    mm = nc.tensor.transpose(pT[:, t * P:(t + 1) * P], o[:, t * P:(t + 1) * P], ident[:])
                mm.then_inc(s["oT"], 1)
                pe.wait_ge(s["oTs"], b + 1)
                pe.wait_ge(s["lows"], lagged(2 * b, 4, 2 * B))
                pe.wait_ge(s["kmin"], lagged(b, 2))
                pe.wait_ge(s["kmu"], lagged(b, 2))
                for t in range(NT):
                    mm = nc.tensor.matmul(p1[:, 0:D], oT[:, t, :], wout[:, t, :], start=t == 0, stop=t == NT - 1)
                mm.then_inc(s["y"], 1)

            pipeline(pe, [(0, low_rank), (1, scores), (0, content), (1, turn_scores), (0, rotary), (1, turn_probabilities), (1, values),
                          (0, sorted_tables), (1, output)])

        @block.scalar
        def _(act):
            flat = lambda t: t.rearrange("p a b -> p (a b)")
            act.wait_ge(s_ang, 1)
            nc.scalar.activation(ang[1][:], ang[0][:], ACT.Exp, scale=-1.0).then_inc(s_ang2, 1)
            act.wait_ge(s_ang, 6)
            nc.scalar.activation(cs[:, 1, :], ang[3][:], ACT.Sin).then_inc(s_ang2, 1)
            nc.scalar.activation(cs[:, 0, :], ang[4][:], ACT.Sin).then_inc(s_ang2, 1)

            def turned(b, i):
                act.wait_ge(s["turned"], b + 1)
                wait(act, s["low"], b)
                nc.scalar.activation(flat(xT[:]), pT[:, 0:D], ACT.Copy).then_inc(s["xTs"], 1)
                act.wait_ge(s["low"], b + 1)
                wait(act, s["qr"], 2 * b)
                wait(act, s["v"], b)
                nc.scalar.activation(low[:, 0, :], p1[:, 0:P], ACT.Copy).then_inc(s["lows"], 1)
                nc.scalar.activation(low[0:DH, 1, :], p1[0:DH, P:2 * P], ACT.Copy).then_inc(s["lows"], 1)

            def content(b, i):
                act.wait_ge(s["qk"], b + 1)
                wait(act, s["s"], b - 1)
                nc.scalar.activation(flat(kc[:, i, :, :]), pB[:], ACT.Copy).then_inc(s["kcs"], 1)
                act.wait_ge(s["v"], b + 1)
                wait(act, s["o"], b - 1)
                nc.scalar.activation(v[:, i, :, 0:DH], pT[:].rearrange("p (h d) -> p h d", h=HA), ACT.Copy).then_inc(s["vs"], 1)

            def softplus(b, i):
                act.wait_ge(s["kmin"], b + 1)
                wait(act, s["kmu"], b)
                nc.scalar.activation(kexp[:], kmin[:], ACT.Exp).then_inc(s["kexp"], 1)
                for n in range(2):
                    act.wait_ge(s["qmin"], 2 * b + n + 1)
                    nc.scalar.activation(qmin[:, n, :], qmin[:, n, :], ACT.Exp).then_inc(s["qexp"], 1)
                act.wait_ge(s["kexp"], 2 * b + 1)
                nc.scalar.activation(kexp[:], kexp[:], ACT.Ln, bias=1.0).then_inc(s["kexp"], 1)
                for n in range(2):
                    act.wait_ge(s["qexp"], 4 * b + 2 + n)
                    nc.scalar.activation(qmin[:, n, :], qmin[:, n, :], ACT.Ln, bias=1.0).then_inc(s["qexp"], 1)

            def early_scores(b, i):
                act.wait_ge(s["s"], b + 1)
                wait(act, s["stn"], b)
                nc.scalar.activation(sa[:], bA[0:TOP, :], ACT.Copy).then_inc(s["st"], 1)

            def softmax(b, i):
                act.wait_ge(s["max"], 2 * b + 2)
                wait(act, s["pt"], b)
                for n, (bank, p, width) in enumerate(((bA, pa, TOP), (b1, pb, P))):
                    for t in range(NT):
                        e = nc.scalar.activation(p[:, t, :], bank[:, t * width:(t + 1) * width], ACT.Exp, bias=neg[:, n, t:t + 1])
                    e.then_inc(s["prob"], 1)

            def late_probabilities(b, i):
                act.wait_ge(s["pt"], b + 1)
                wait(act, s["o"], b)
                nc.scalar.activation(pbT[:], b3[:], ACT.Copy).then_inc(s["pts"], 1)

            def output(b, i):
                act.wait_ge(s["oT"], b + 1)
                wait(act, s["y"], b)
                nc.scalar.activation(flat(oT[:]), pT[:], ACT.Copy).then_inc(s["oTs"], 1)

            def store(b, i):
                act.wait_ge(ln.s_done, b + 1)
                act.dma_start(tokens(x_out, b), xo[:, i, :]).then_inc(s_stored[i], 16)

            pipeline(act, [(0, turned), (1, early_scores), (0, content), (1, softmax), (0, softplus), (1, late_probabilities),
                           (1, output), (2, store)])
            for i in range(2):
                act.wait_ge(s_stored[i], 16 * B // 2)

        @block.vector
        def _(dve):
            dve.wait_ge(s["weights"], 16 * len(loads))
            done = [0]

            def step(instruction):
                done[0] += 1
                instruction.then_inc(s_ang, 1)
                dve.wait_ge(s_ang, done[0])

            nc.vector.memset(ang[0][:], 0.0).then_inc(s_set, 1)
            dve.wait_ge(s_set, 1)
            nc.vector.tensor_copy(ang[0][:, 0:1], raw_c[:]).then_inc(s_set, 1)
            dve.wait_ge(s_set, 2)
            step(nc.vector.tensor_copy(ang[0][0:TOP, 1:1 + DR], raw_r[:]))
            dve.wait_ge(s_ang2, 1)
            step(nc.vector.tensor_scalar(ang[2][:], ang[1][:], 1.0, None, ALU.add))
            step(nc.vector.reciprocal(ang[1][:], ang[2][:]))
            step(nc.vector.tensor_scalar(ang[2][:], ang[1][:], -2.0 * float(np.pi), float(np.pi), ALU.mult, ALU.add))
            step(nc.vector.tensor_scalar(ang[3][:], ang[2][:], PI, -PI, ALU.min, ALU.max))
            nc.vector.scalar_tensor_tensor(ang[2][:], ang[3][:], -1.0, ang[3][:], ALU.mult, ALU.max).then_inc(s_set, 1)
            dve.wait_ge(s_set, 3)
            step(nc.vector.tensor_scalar(ang[4][:], ang[2][:], -1.0, float(np.pi) / 2, ALU.mult, ALU.add))
            dve.wait_ge(s_ang2, 3)
            step(nc.vector.tensor_scalar(cs[:], cs[:], -1.0, None, ALU.mult))
            step(nc.vector.tensor_scalar(tab[:], trig[:, :, 0, :], cs[:, 0, 0:1], None, ALU.mult))
            step(nc.vector.scalar_tensor_tensor(tab2[:], trig[:, :, 1, :], cs[:, 1, 0:1], tab[:], ALU.mult, ALU.add))
            step(nc.vector.tensor_scalar(tab[:, 0, :], tab2[:, 0, :], SCALE, None, ALU.mult))
            for n in range(2):
                rows = cs[0:TOP, n, 1:1 + DR].unsqueeze(1).to_broadcast([TOP, 2, DR])
                step(nc.vector.tensor_tensor((st, st2)[n][:], srt[:, n, :, :], rows, ALU.mult))
            step(nc.vector.tensor_tensor(st[:], st[:], st2[:], ALU.add))
            for n in range(3):
                step(nc.vector.tensor_copy(part[n][:], st[:]))
                if n < 2:
                    step(nc.vector.tensor_tensor(st[:], st[:], part[n][:], ALU.subtract))
            for n in range(3):
                rows = slice(32 * n, 32 * n + 32)
                step(nc.vector.tensor_copy(parts[rows], part[n][rows]))
            nc.vector.memset(rinv[:], 0.0).then_inc(s["tab"], 1)
            dve.wait_ge(s["const"], NZ)

            def key_angles(b, i):
                dve.wait_ge(s["lows"], 2 * b + 2)
                wait(dve, s["kexp"], 2 * b)
                nc.vector.tensor_scalar(kmin[:], p1[:, 2 * P:4 * P], 60.0, None, ALU.min).then_inc(s["kmin"], 1)

            def contents(b, i):
                dve.wait_ge(s["qk"], b + 1)
                wait(dve, s["s"], b - 1)
                for n in range(2):
                    rows = slice(64 * n, 64 * n + 64)
                    nc.vector.tensor_scalar(qc[rows, i, :, n, :], pA[rows, :].rearrange("p (t q) -> p t q", t=NT), SCALE, None, ALU.mult).then_inc(s["qcs"], 1)
                dve.wait_ge(s_rank[i], landed(b, i, 2))
                wait(dve, s["g"], 2 * (b - 1))
                nc.vector.tensor_scalar(onehot[:, i, :], rank[:, i, :], sel[:], None, ALU.is_equal).then_inc(s["onehot"], 1)

            def angles(b, i):
                for n, bank in enumerate((pA, pB)):
                    dve.wait_ge(s["qr"], 2 * b + n + 1)
                    wait(dve, s["qmu"], 2 * b)
                    nc.vector.tensor_scalar(qmin[:, n, :], bank[:], 60.0, None, ALU.min).then_inc(s["qmin"], 1)
                dve.wait_ge(s["kexp"], 2 * b + 2)
                nc.vector.tensor_tensor(kmu[:], kexp[:], p1[:, 2 * P:4 * P], ALU.max).then_inc(s["kmu"], 1)
                for n, bank in enumerate((pA, pB)):
                    dve.wait_ge(s["qexp"], 4 * b + 3 + n)
                    nc.vector.tensor_tensor(qmu[:, n, :], qmin[:, n, :], bank[:], ALU.max).then_inc(s["qmu"], 1)
                    dve.wait_ge(s["qmu"], 2 * b + n + 1)
                    wait(dve, s["s"], b - 1)
                    nc.vector.tensor_tensor(qrot[:, i, 4 * n:4 * n + 4, :], qmu[:, n, :].rearrange("p (h t) -> p h t", h=4),
                                            tab[:, 0, :].unsqueeze(1).to_broadcast([P, 4, P]), ALU.mult).then_inc(s["qrot"], 1)
                dve.wait_ge(s["kmu"], b + 1)
                nc.vector.tensor_tensor(krot[:], kmu[:].rearrange("p (a j) -> p a j", a=2), tab2[:, 1:3, :], ALU.mult).then_inc(s["krot"], 1)
                dve.wait_ge(s["krot"], 3 * b + 1)
                nc.vector.tensor_tensor(ka[0:64, i, :], krot[0:64, 0, :], krot[0:64, 1, :], ALU.add).then_inc(s["krot"], 1)
                nc.vector.tensor_tensor(kb[64:128, i, :], krot[64:128, 0, :], krot[64:128, 1, :], ALU.add).then_inc(s["krot"], 1)

            def sorted_keys(b, i):
                dve.wait_ge(s["fold"], b + 1)
                for q in range(4):
                    rows = slice(32 * q, 32 * q + 32)
                    nc.vector.tensor_copy(ql[rows, i, :, q, :], pA[rows, :].rearrange("p (h q t) -> p q t h", h=HA, q=4)[:, q, :, :]).then_inc(s["ql"], 1)
                for n in range(2):
                    dve.wait_ge(s["g"], 2 * b + n + 1)
                    wait(dve, s["ks"], 2 * b + n)
                    for c, (bank, t) in enumerate(((pA, g1), (pB, g2))):
                        nc.vector.tensor_tensor(t[:].rearrange("p (t j) -> p t j", j=W), bank[:].rearrange("p (t j) -> p t j", j=W),
                                                kmu[:, c * P:c * P + W].unsqueeze(1).to_broadcast([P, 8, W]), ALU.mult).then_inc(s["gs"], 1)

            def late_scores(b, i):
                dve.wait_ge(s["s"], b + 1)
                for bank, t, mask in ((b2, m1, local), (b3, m2, future)):
                    nc.vector.tensor_tensor(t[:].rearrange("p (h t) -> p h t", h=HA), bank[:].rearrange("p (h t) -> p h t", h=HA),
                                            mask[:].unsqueeze(1).to_broadcast([P, HA, W]), ALU.mult).then_inc(s["m"], 1)
                dve.wait_ge(s["sab"], b + 1)
                nc.vector.tensor_tensor(sb_[:], b1[:], m1[:], ALU.add).then_inc(s["st"], 1)

            def largest(b, i):
                dve.wait_ge(s["stn"], b + 1)
                for n, (bank, width) in enumerate(((bA, TOP), (b1, P))):
                    nc.vector.tensor_reduce(neg[:, n, :], bank[:, 0:NT * width].rearrange("p (t j) -> p t j", t=NT), AX.X, ALU.max,
                                            negate=True).then_inc(s["max"], 1)

            def early_probabilities(b, i):
                dve.wait_ge(s["pt"], b + 1)
                wait(dve, s["o"], b)
                nc.vector.tensor_copy(paT[:], b2[0:TOP, :]).then_inc(s["pts"], 1)

            def output(b, i):
                dve.wait_ge(s["o"], b + 1)
                by_head = [bank[:, 0:4 * (DH + 1)].rearrange("p (h d) -> p h d", h=4) for bank in (bA, b1)]
                for n in range(2):
                    nc.vector.reciprocal(rinv[:, 4 * n:4 * n + 4], by_head[n][:, :, DH]).then_inc(s["rinv"], 1)
                dve.wait_ge(s["rinv"], 2 * b + 2)
                wait(dve, s["oT"], b)
                for n in range(2):
                    nc.vector.tensor_tensor(o[:, n * D:(n + 1) * D].rearrange("p (h d) -> p h d", h=4), by_head[n][:, :, 0:DH],
                                            rinv[:, 4 * n:4 * n + 4].unsqueeze(2).to_broadcast([P, 4, DH]), ALU.mult).then_inc(s["on"], 1)
                dve.wait_ge(s["y"], b + 1)
                dve.wait_ge(s["xr"], b + 1)
                nc.vector.tensor_tensor(y[:, i, :], p1[:, 0:D], xr[:, i, :], ALU.add).then_inc(s["ys"], 1)
                dve.wait_ge(s["ys"], b + 1)
                ln.statistics(dve, y[:, i, :], b)

            def norm(b, i):
                wait(dve, s_stored[i], landed(b - 2, i))
                ln.result(dve, y[:, i, :], xo[:, i, :], b)

            pipeline(dve, [(2, norm), (0, key_angles), (1, late_scores), (0, contents), (1, largest), (0, angles), (1, early_probabilities),
                           (0, sorted_keys), (1, output)])


H, DK = 16, 16
SLOTS, TILES = 4, 4
PAIR = 2


def cross_attention_0(nc, x_in, x_out, w):
    with ExitStack() as ctx:
        ph = Phase(nc, ctx, "xa0")
        wq, wk = ph.sb("wq", [P, KC, TILES, P]), ph.sb("wk", [P, KC, TILES, P])
        wv, wo = ph.sb("wv", [P, KC, D]), ph.sb("wo", [P, KC, D])
        bq, bk, bq4 = ph.sb("bq", [P, TILES]), ph.sb("bk", [P, TILES]), ph.sb("bq4", [P, TILES])
        bv, bo = ph.sb("bv", [P, D]), ph.sb("bo", [P, D])
        ident = ph.sb("ident", [P, P])
        mask_u8, mask = ph.sb("mask_u8", [P, B * S], U8), ph.sb("mask", [P, B * S], BF16)
        mask_b = ph.sb("mask_b", [P, 2, S], BF16)
        ones = ph.sb("ones", [P, P], BF16)
        x, c = ph.sb("x", [P, 2, D]), ph.sb("c", [P, 2, D])
        xbo = ph.sb("xbo", [P, 2, D])
        xcT = ph.sb("xcT", [P, 4, P])
        qT, kT, v = ph.sb("qT", [P, 2, TILES, P]), ph.sb("kT", [P, 2, TILES, P]), ph.sb("v", [P, 2, D])
        prob, probT = ph.sb("prob", [P, 2, BANK]), ph.sb("probT", [P, 2, BANK])
        negmax, rowsum, rinv = ph.sb("negmax", [P, 2, H]), ph.sb("rowsum", [P, 2, H]), ph.sb("rinv", [P, H])
        o, oT = ph.sb("o", [P, D]), ph.sb("oT", [P, KC, P])
        y, xo = ph.sb("y", [P, 2, D]), ph.sb("xo", [P, 2, D])
        ln = LayerNorm(ph)
        pT, pQK, pV, pY = ph.bank("pT"), ph.bank("pQK"), ph.bank("pV"), ph.bank("pY")
        pS, pP, pO = [ph.bank("pS0"), ph.bank("pS1")], ph.bank("pP"), ph.bank("pO")
        s_w, s_const, s_mask, s_bq4 = ph.sem("weights"), ph.sem("ones"), ph.sem("mask"), ph.sem("bq4")
        s_x, s_stored = ph.sems("x"), ph.sems("stored")
        s_xbo, s_mask_b = ph.sem("xbo"), ph.sem("mask_b")
        s_turned, s_xcT = ph.sem("turned"), ph.sem("xcT")
        s_q, s_k, s_v = ph.sem("q"), ph.sem("k"), ph.sem("v")
        s_qs, s_ks, s_vs = ph.sem("qs"), ph.sem("ks"), ph.sem("vs")
        s_scores, s_max, s_prob = ph.sem("scores"), ph.sem("max"), ph.sem("prob")
        s_pT, s_pTs, s_o = ph.sem("probT"), ph.sem("probTs"), ph.sem("o")
        s_rinv, s_on, s_oT, s_oTs, s_y, s_ys = (ph.sem(n) for n in ("rinv", "on", "oT", "oTs", "y", "ys"))
        G = SLOTS
        SCALE = float(DK) ** -0.5
        NW = 10
        block = ctx.enter_context(nc.Block())

        @block.sync
        def _(sp):
            sp.dma_start(ident[:], w["ident"]).then_inc(s_w, 16)
            sp.dma_start(wq[:], w["L0_xattn_Wq_slots"].rearrange("(c p) (t m) -> p c t m", p=P, t=TILES)).then_inc(s_w, 16)
            sp.dma_start(wk[:], w["L0_xattn_Wk_slots"].rearrange("(c p) (t m) -> p c t m", p=P, t=TILES)).then_inc(s_w, 16)
            sp.dma_start(wv[:], w["L0_xattn_Wv"].rearrange("(c p) n -> p c n", p=P)).then_inc(s_w, 16)
            sp.dma_start(wo[:], w["L0_xattn_Wo"].rearrange("(c p) n -> p c n", p=P)).then_inc(s_w, 16)
            sp.dma_start(bq[:], w["L0_xattn_bq_slots"]).then_inc(s_w, 16)
            sp.dma_start(bk[:], w["L0_xattn_bk_slots"]).then_inc(s_w, 16)
            sp.dma_start(bv[:], to_all(w["L0_xattn_bv"])).then_inc(s_w, 16)
            sp.dma_start(bo[:], to_all(w["L0_xattn_bo"])).then_inc(s_w, 16)
            sp.dma_start(mask_u8[:], w["mask_keys"].rearrange("b o s -> o (b s)").to_broadcast([P, B * S])).then_inc(s_w, 16)

            def load(b, i):
                wait(sp, s_xbo, b - 1)
                wait(sp, s_turned, b - 1)
                sp.dma_start(x[:, i, :], tokens(x_in, b)).then_inc(s_x[i], 16)
                sp.dma_start(c[:, i, :], tokens(w["ctx_1024"], b)).then_inc(s_x[i], 16)

            pipeline(sp, [(0, load)])

        @block.gpsimd
        def _(pool):
            nc.gpsimd.memset(ones[:], 1.0).then_inc(s_const, 1)
            pool.wait_ge(s_w, 16 * NW)

            def add_bo(b, i):
                pool.wait_ge(s_x[i], landed(b, i, 2))
                wait(pool, s_ys, b - 1)
                nc.gpsimd.tensor_tensor(xbo[:, i, :], x[:, i, :], bo[:], ALU.add).then_inc(s_xbo, 1)

            def copy_mask(b, i):
                wait(pool, s_scores, G * (b - 1))
                nc.gpsimd.tensor_copy(mask_b[:, i, :], mask[:, bass.ds(b * S, S)]).then_inc(s_mask_b, 1)

            def norm(b, i):
                ln.power(pool, b)

            ln.constants(pool)
            pool.wait_ge(s_mask, 1)
            pipeline(pool, [(0, add_bo), (0, copy_mask), (2, norm)])

        @block.tensor
        def _(pe):
            pe.wait_ge(s_w, 16 * NW)
            pe.wait_ge(s_const, 1)
            def project(b, i):
                pe.wait_ge(s_x[i], landed(b, i, 2))
                wait(pe, s_oTs, b - 1)
                for j, src in enumerate((x, c)):
                    for k in range(KC):
                        t = nc.tensor.transpose(pT[:, (2 * j + k) * P:(2 * j + k + 1) * P], src[:, i, k * P:(k + 1) * P], ident[:])
                t.then_inc(s_turned, 1)
                pe.wait_ge(s_xcT, b + 1)
                wait(pe, s_ks, b)
                for t in range(TILES):
                    for k in range(KC):
                        mm = nc.tensor.matmul(pQK[:, t * P:(t + 1) * P], wq[:, k, t, :], xcT[:, k, :], start=k == 0, stop=k == KC - 1)
                mm.then_inc(s_q, 1)
                wait(pe, s_vs, b)
                for k in range(KC):
                    mm = nc.tensor.matmul(pV[:, 0:D], xcT[:, 2 + k, :], wv[:, k, :], start=k == 0, stop=k == KC - 1)
                mm.then_inc(s_v, 1)
                pe.wait_ge(s_qs, b + 1)
                for t in range(TILES):
                    for k in range(KC):
                        mm = nc.tensor.matmul(pQK[:, t * P:(t + 1) * P], wk[:, k, t, :], xcT[:, 2 + k, :], start=k == 0, stop=k == KC - 1)
                mm.then_inc(s_k, 1)

            def attend(b, i):
                pe.wait_ge(s_qs, b + 1)
                pe.wait_ge(s_ks, b + 1)
                pe.wait_ge(s_vs, b + 1)
                pe.wait_ge(s_mask_b, b + 1)

                def scores(g):
                    wait(pe, s_prob, G * b + g - 1)
                    nc.tensor.matmul(pS[g % 2][:].rearrange("p (t s) -> p t s", t=TILES), ones[32 * g:32 * g + 1, :],
                                     mask_b[32 * g:32 * g + 1, i, :].unsqueeze(1).to_broadcast([1, TILES, S]),
                                     start=True, stop=False, skip_group_check=True)
                    r = slice(32 * g, 32 * g + DK)
                    for t in range(TILES):
                        mm = nc.tensor.matmul(pS[g % 2][:, t * P:(t + 1) * P], qT[r, i, t, :], kT[r, i, t, :],
                                              start=False, stop=t == TILES - 1, skip_group_check=True)
                    mm.then_inc(s_scores, 1)

                def turn(g):
                    pe.wait_ge(s_prob, G * b + g + 1)
                    wait(pe, s_pTs, G * b + g)
                    for t in range(TILES):
                        mm = nc.tensor.transpose(pP[:, t * P:(t + 1) * P], prob[:, g % 2, t * P:(t + 1) * P], ident[:])
                    mm.then_inc(s_pT, 1)

                def values(g):
                    pe.wait_ge(s_pTs, G * b + g + 1)
                    if g == 0:
                        wait(pe, s_on, b)
                    for t in range(TILES):
                        h = TILES * g + t
                        mm = nc.tensor.matmul(pO[:, h * DK:(h + 1) * DK], probT[:, g % 2, t * P:(t + 1) * P],
                                              v[:, i, h * DK:(h + 1) * DK], start=True, stop=True)
                    mm.then_inc(s_o, 1)

                scores(0)
                scores(1)
                turn(0)
                for g in range(G):
                    if g + 2 < G:
                        scores(g + 2)
                    if g + 1 < G:
                        turn(g + 1)
                    values(g)

            def output(b, i):
                pe.wait_ge(s_on, b + 1)
                pe.wait_ge(s_xcT, lagged(b, 2))
                for k in range(KC):
                    mm = nc.tensor.transpose(pT[:, k * P:(k + 1) * P], o[:, k * P:(k + 1) * P], ident[:])
                mm.then_inc(s_oT, 1)
                pe.wait_ge(s_oTs, b + 1)
                wait(pe, s_ys, b)
                for k in range(KC):
                    mm = nc.tensor.matmul(pY[:, 0:D], oT[:, k, :], wo[:, k, :], start=k == 0, stop=k == KC - 1)
                mm.then_inc(s_y, 1)

            pipeline(pe, [(0, project), (1, attend), (1, output)])

        @block.scalar
        def _(act):
            def turned(b, i):
                act.wait_ge(s_turned, b + 1)
                wait(act, s_k, b)
                nc.scalar.activation(xcT[:].rearrange("p a b -> p (a b)"), pT[:], ACT.Copy).then_inc(s_xcT, 1)

            def softmax(b, i):
                for g in range(G):
                    act.wait_ge(s_max, G * b + g + 1)
                    wait(act, s_pT, G * b + g - 1)
                    for t in range(TILES):
                        h = TILES * g + t
                        e = nc.scalar.activation(prob[:, g % 2, t * P:(t + 1) * P], pS[g % 2][:, t * P:(t + 1) * P], ACT.Exp,
                                                 bias=negmax[:, i, h:h + 1], accum_out=rowsum[:, i, h:h + 1])
                    e.then_inc(s_prob, 1)

            def output(b, i):
                act.wait_ge(s_oT, b + 1)
                wait(act, s_y, b)
                nc.scalar.activation(oT[:].rearrange("p a b -> p (a b)"), pT[:, 0:D], ACT.Copy).then_inc(s_oTs, 1)

            def store(b, i):
                act.wait_ge(ln.s_done, b + 1)
                act.dma_start(tokens(x_out, b), xo[:, i, :]).then_inc(s_stored[i], 16)

            pipeline(act, [(0, turned), (1, softmax), (1, output), (2, store)])
            for i in range(2):
                act.wait_ge(s_stored[i], 16 * B // 2)

        @block.vector
        def _(dve):
            dve.wait_ge(s_w, 16 * NW)
            nc.vector.tensor_scalar(mask[:], mask_u8[:], 1.0, 1e9, ALU.subtract, ALU.mult).then_inc(s_mask, 1)
            nc.vector.tensor_scalar(bq4[:], bq[:], SCALE, None, ALU.mult).then_inc(s_bq4, 1)
            dve.wait_ge(s_bq4, 1)

            def evacuate(b, i):
                dve.wait_ge(s_q, b + 1)
                wait(dve, s_scores, G * (b - 1))
                nc.vector.scalar_tensor_tensor(qT[:, i, :, :], pQK[:].rearrange("p (t s) -> p t s", t=TILES), SCALE,
                                               bq4[:].unsqueeze(2).to_broadcast([P, TILES, S]), ALU.mult, ALU.add).then_inc(s_qs, 1)
                dve.wait_ge(s_v, b + 1)
                wait(dve, s_o, G * (b - 1))
                nc.vector.tensor_tensor(v[:, i, :], pV[:, 0:D], bv[:], ALU.add).then_inc(s_vs, 1)
                dve.wait_ge(s_k, b + 1)
                nc.vector.tensor_tensor(kT[:, i, :, :], pQK[:].rearrange("p (t s) -> p t s", t=TILES),
                                        bk[:].unsqueeze(2).to_broadcast([P, TILES, S]), ALU.add).then_inc(s_ks, 1)

            def softmax(b, i):
                def largest(g):
                    dve.wait_ge(s_scores, G * b + g + 1)
                    if g == 0:
                        wait(dve, s_prob, G * (b - 1))
                    nc.vector.tensor_reduce(negmax[:, i, TILES * g:TILES * g + TILES], pS[g % 2][:].rearrange("p (t s) -> p t s", t=TILES),
                                            AX.X, ALU.max, negate=True).then_inc(s_max, 1)

                def turned(g):
                    dve.wait_ge(s_pT, G * b + g + 1)
                    wait(dve, s_o, G * b + g - 1)
                    nc.vector.tensor_copy(probT[:, g % 2, :], pP[:]).then_inc(s_pTs, 1)

                largest(0)
                largest(1)
                for g in range(G):
                    turned(g)
                    if g + 2 < G:
                        largest(g + 2)

            def output(b, i):
                dve.wait_ge(s_prob, G * b + G)
                nc.vector.reciprocal(rinv[:], rowsum[:, i, :]).then_inc(s_rinv, 1)
                dve.wait_ge(s_rinv, b + 1)
                dve.wait_ge(s_o, G * b + G)
                wait(dve, s_oT, b)
                nc.vector.tensor_tensor(o[:].rearrange("p (h d) -> p h d", h=H), pO[:, 0:D].rearrange("p (h d) -> p h d", h=H),
                                        rinv[:].unsqueeze(2).to_broadcast([P, H, DK]), ALU.mult).then_inc(s_on, 1)
                dve.wait_ge(s_y, b + 1)
                dve.wait_ge(s_xbo, b + 1)
                nc.vector.tensor_tensor(y[:, i, :], pY[:, 0:D], xbo[:, i, :], ALU.add).then_inc(s_ys, 1)

            def norm(b, i):
                wait(dve, s_stored[i], landed(b - 2, i))
                ln.result(dve, y[:, i, :], xo[:, i, :], b)

            def statistics(b, i):
                dve.wait_ge(s_ys, b + 1)
                ln.statistics(dve, y[:, i, :], b)

            pipeline(dve, [(2, norm), (0, evacuate), (1, softmax), (1, output), (1, statistics)])


INNER = 1024
IC = INNER // P
QMAX = 127.0


def ternary_ffn_0(nc, x_in, x_out, w, rows):
    with ExitStack() as ctx:
        ph = Phase(nc, ctx, "ff0")
        raw = [ph.sb(f"raw{n}", [P, 2 * INNER]) for n in range(3)]
        tern = [ph.sb(f"tern{n}", [P, 2 * INNER], BF16) for n in range(3)]
        wg = tern[0][:].rearrange("p (c n) -> p c n", c=KC)
        wu = tern[1][:].rearrange("p (c n) -> p c n", c=KC)
        wd = tern[2][:].rearrange("p (c n) -> p c n", c=IC)
        ones, ident = ph.sb("ones", [P, P]), ph.sb("ident", [P, P], BF16)
        sums, mean, wscale = ph.sb("sums", [P, 3]), ph.sb("mean", [P, 3]), ph.sb("wscale", [P, 3])
        x, amax = ph.sb("x", [P, 4, D]), ph.sb("amax", [P, 2])
        rx, sx, step = ph.sb("rx", [P, 1]), ph.sb("sx", [P, 2]), ph.sb("step", [P, 2, 3])
        xr, xq, xqT = ph.sb("xr", [P, D]), ph.sb("xq", [P, D], BF16), ph.sb("xqT", [P, KC, P], BF16)
        g, h, hr = ph.sb("g", [P, INNER]), ph.sb("h", [P, INNER]), ph.sb("hr", [P, INNER])
        hamax, hclip, rh, sh, hstep = (ph.sb(n, [P, 1]) for n in ("hamax", "hclip", "rh", "sh", "hstep"))
        hq, hqT = ph.sb("hq", [P, INNER], BF16), ph.sb("hqT", [P, INNER], BF16)
        y, xo = ph.sb("y", [P, 2, D]), ph.sb("xo", [P, 2, D])
        zeros, s_zeros, s_cleared = ph.sb("zeros", [P, CLEAR * D]), ph.sem("zeros"), ph.sem("cleared")
        ln = LayerNorm(ph)
        pX, pH = ph.bank("pX", BF16), ph.bank("pH", BF16)
        pG, pU, pY = [ph.bank(f"pG{n}") for n in range(2)], [ph.bank(f"pU{n}") for n in range(2)], ph.bank("pY")
        s_raw, s_id, s_ones, s_sum, s_tot, s_mean, s_tern = (ph.sem(n) for n in ("raw", "ident", "ones", "sum", "tot", "mean", "tern"))
        s_x, s_stored = ph.sems("x", 4), ph.sems("stored")
        s_amax, s_xq, s_xT, s_xTs = ph.sem("amax"), ph.sem("xq"), ph.sem("xT"), ph.sem("xTs")
        s_gate, s_up, s_g, s_h = ph.sem("gate"), ph.sem("up"), ph.sem("g"), ph.sem("h")
        s_hmax, s_hr, s_hq, s_hT, s_hTs = ph.sem("hmax"), ph.sem("hr"), ph.sem("hq"), ph.sem("hT"), ph.sem("hTs")
        s_y, s_ys = ph.sem("y"), ph.sem("ys")
        NH = INNER // BANK
        block = ctx.enter_context(nc.Block())

        @block.sync
        def _(sp):
            for n, name in enumerate(("L0_ffn_w_gateT", "L0_ffn_w_upT", "L0_ffn_w_downT")):
                sp.dma_start(raw[n][:].rearrange("p (c n) -> p c n", c=IC if n == 2 else KC),
                             w[name].rearrange("(c p) n -> p c n", p=P)).then_inc(s_raw, 16)
            sp.dma_start(ident[:], w["ident_bf16"]).then_inc(s_id, 16)

            def load(b, i):
                wait(sp, s_ys, b - 1)
                sp.dma_start(x[:, i, :], tokens(x_in, b)).then_inc(s_x[i], 16)
                sp.dma_start(rows[bass.ds(b * CLEAR * P, CLEAR * P), :].rearrange("(p a) d -> p (a d)", p=P), zeros[:]).then_inc(s_cleared, 16)

            sp.wait_ge(s_zeros, 1)
            pipeline(sp, [(0, load)])
            sp.wait_ge(s_cleared, 16 * B)

        @block.gpsimd
        def _(pool):
            ln.constants(pool)
            nc.gpsimd.memset(ones[:], 1.0).then_inc(s_ones, 1)
            nc.gpsimd.memset(zeros[:], 0.0).then_inc(s_zeros, 1)
            pipeline(pool, [(2, lambda b, i: ln.power(pool, b))])

        @block.tensor
        def _(pe):
            pe.wait_ge(s_ones, 1)
            pe.wait_ge(s_id, 16)
            pe.wait_ge(s_sum, 3)
            nc.tensor.matmul(pY[:, 0:3], ones[:], sums[:], start=True, stop=True).then_inc(s_tot, 1)
            pe.wait_ge(s_tern, 9)

            def gate_up(b, i):
                pe.wait_ge(s_xq, 2 * b + 2)
                wait(pe, s_xTs, b)
                for k in range(KC):
                    t = nc.tensor.transpose(pX[:, k * P:(k + 1) * P], xq[:, k * P:(k + 1) * P], ident[:])
                t.then_inc(s_xT, 1)
                pe.wait_ge(s_xTs, b + 1)
                for weights, banks, free, done in ((wg, pG, s_g, s_gate), (wu, pU, s_h, s_up)):
                    wait(pe, free, NH * b if free is s_g else b)
                    for n in range(NH):
                        for k in range(KC):
                            mm = nc.tensor.matmul(banks[n][:], xqT[:, k, :], weights[:, k, n * BANK:(n + 1) * BANK], start=k == 0, stop=k == KC - 1)
                    mm.then_inc(done, 1)

            def down(b, i):
                pe.wait_ge(s_hq, b + 1)
                wait(pe, s_hTs, b)
                for k in range(IC):
                    t = nc.tensor.transpose(pH[:, k * P:(k + 1) * P], hq[:, k * P:(k + 1) * P], ident[:])
                t.then_inc(s_hT, 1)
                pe.wait_ge(s_hTs, b + 1)
                wait(pe, s_ys, b)
                for k in range(IC):
                    mm = nc.tensor.matmul(pY[:, 0:D], hqT[:, k * P:(k + 1) * P], wd[:, k, :], start=k == 0, stop=k == IC - 1)
                mm.then_inc(s_y, 1)

            pipeline(pe, [(0, gate_up), (1, down)])

        @block.scalar
        def _(act):
            def turned(b, i):
                act.wait_ge(s_xT, b + 1)
                wait(act, s_up, b)
                nc.scalar.activation(xqT[:].rearrange("p a b -> p (a b)"), pX[:, 0:D], ACT.Copy).then_inc(s_xTs, 1)

            def middle(b, i):
                act.wait_ge(s_gate, b + 1)
                wait(act, s_h, b)
                for n in range(NH):
                    nc.scalar.activation(g[:, n * BANK:(n + 1) * BANK], pG[n][:], ACT.Silu, scale=step[:, i, 0:1]).then_inc(s_g, 1)
                act.wait_ge(s_hmax, 4 * b + 4)
                nc.scalar.activation(hr[:], h[:], ACT.Copy, bias=MAGIC, scale=sh[:]).then_inc(s_hr, 1)
                act.wait_ge(s_hT, b + 1)
                wait(act, s_y, b)
                nc.scalar.activation(hqT[:], pH[:], ACT.Copy).then_inc(s_hTs, 1)

            def store(b, i):
                act.wait_ge(ln.s_done, b + 1)
                act.dma_start(tokens(x_out, b), xo[:, i, :]).then_inc(s_stored[i], 16)

            pipeline(act, [(0, turned), (1, middle), (2, store)])
            for i in range(2):
                act.wait_ge(s_stored[i], 16 * B // 2)

        @block.vector
        def _(dve):
            dve.wait_ge(s_raw, 48)
            for n in range(3):
                nc.vector.tensor_reduce(sums[:, n:n + 1], raw[n][:], AX.X, ALU.add, apply_absolute_value=True).then_inc(s_sum, 1)
            dve.wait_ge(s_tot, 1)
            nc.vector.tensor_scalar(mean[:], pY[:, 0:3], 1.0 / (D * INNER), 1e-5, ALU.mult, ALU.max).then_inc(s_mean, 1)
            dve.wait_ge(s_mean, 1)
            nc.vector.reciprocal(wscale[:], mean[:]).then_inc(s_mean, 1)
            dve.wait_ge(s_mean, 2)
            for n in range(3):
                nc.vector.tensor_scalar(raw[n][:], raw[n][:], wscale[:, n:n + 1], MAGIC, ALU.mult, ALU.add).then_inc(s_tern, 1)
                dve.wait_ge(s_tern, 3 * n + 1)
                nc.vector.tensor_scalar(raw[n][:], raw[n][:], MAGIC, 1.0, ALU.subtract, ALU.min).then_inc(s_tern, 1)
                dve.wait_ge(s_tern, 3 * n + 2)
                nc.vector.tensor_scalar(tern[n][:], raw[n][:], -1.0, None, ALU.max).then_inc(s_tern, 1)

            def quantise(b, i):
                dve.wait_ge(s_x[i], landed(b, i))
                nc.vector.tensor_reduce(amax[:, 0:1], x[:, i, :], AX.X, ALU.max, apply_absolute_value=True).then_inc(s_amax, 1)
                dve.wait_ge(s_amax, 4 * b + 1)
                nc.vector.tensor_scalar(amax[:, 1:2], amax[:, 0:1], 1e-5, 1.0 / QMAX, ALU.max, ALU.mult).then_inc(s_amax, 1)
                dve.wait_ge(s_amax, 4 * b + 2)
                nc.vector.reciprocal(rx[:], amax[:, 1:2]).then_inc(s_amax, 1)
                wait(dve, s_ys, b - 1)
                nc.vector.tensor_scalar(step[:, i, :], mean[:], amax[:, 1:2], None, ALU.mult).then_inc(s_amax, 1)
                dve.wait_ge(s_amax, 4 * b + 4)
                nc.vector.tensor_scalar(xr[:], x[:, i, :], rx[:], MAGIC, ALU.mult, ALU.add).then_inc(s_xq, 1)
                dve.wait_ge(s_xq, 2 * b + 1)
                wait(dve, s_xT, b)
                nc.vector.tensor_scalar(xq[:], xr[:], MAGIC, None, ALU.subtract).then_inc(s_xq, 1)

            def middle(b, i):
                dve.wait_ge(s_g, NH * b + NH)
                dve.wait_ge(s_up, b + 1)
                wait(dve, s_hr, b)
                for n in range(NH):
                    c = slice(n * BANK, (n + 1) * BANK)
                    u = nc.vector.scalar_tensor_tensor(h[:, c], pU[n][:], step[:, i, 1:2], g[:, c], ALU.mult, ALU.mult)
                u.then_inc(s_h, 1)
                dve.wait_ge(s_h, b + 1)
                nc.vector.tensor_reduce(hamax[:], h[:], AX.X, ALU.max, apply_absolute_value=True).then_inc(s_hmax, 1)
                dve.wait_ge(s_hmax, 4 * b + 1)
                nc.vector.tensor_scalar(hclip[:], hamax[:], 1e-5, 1.0 / QMAX, ALU.max, ALU.mult).then_inc(s_hmax, 1)
                dve.wait_ge(s_hmax, 4 * b + 2)
                nc.vector.tensor_scalar(hstep[:], hclip[:], mean[:, 2:3], None, ALU.mult).then_inc(s_hmax, 1)
                nc.vector.reciprocal(sh[:], hclip[:]).then_inc(s_hmax, 1)
                dve.wait_ge(s_hr, b + 1)
                wait(dve, s_hT, b)
                nc.vector.tensor_scalar(hq[:], hr[:], MAGIC, None, ALU.subtract).then_inc(s_hq, 1)
                dve.wait_ge(s_y, b + 1)
                dve.wait_ge(s_hmax, 4 * b + 3)
                nc.vector.scalar_tensor_tensor(y[:, i, :], pY[:, 0:D], hstep[:], x[:, i, :], ALU.mult, ALU.add).then_inc(s_ys, 1)
                dve.wait_ge(s_ys, b + 1)
                ln.statistics(dve, y[:, i, :], b)

            def norm(b, i):
                wait(dve, s_stored[i], landed(b - 2, i))
                ln.result(dve, y[:, i, :], xo[:, i, :], b)

            pipeline(dve, [(2, norm), (0, quantise), (1, middle)])


RMS_EPS = 1e-6


def linear_attention_1(nc, x_in, x_out, w):
    with ExitStack() as ctx:
        ph = Phase(nc, ctx, "la1")
        wq, wk = ph.sb("wq", [P, KC, TILES, P]), ph.sb("wk", [P, KC, TILES, P])
        wvf, wo = ph.sb("wvf", [P, KC, D + H]), ph.sb("wo", [P, KC, D])
        delta, weight = ph.sb("delta", [P, H]), ph.sb("weight", [P, D])
        ident, identb = ph.sb("ident", [P, P]), ph.sb("identb", [P, P], BF16)
        upto, future = ph.sb("upto", [P, P]), ph.sb("future", [P, P], BF16)
        x, xr = ph.sb("x", [P, 2, D]), ph.sb("xr", [P, 2, D])
        xT = ph.sb("xT", [P, KC, P])
        qT, kT, v = ph.sb("qT", [P, 2, BANK]), ph.sb("kT", [P, 2, BANK]), ph.sb("v", [P, 2, D])
        z, az, ez, lz = ph.sb("z", [P, H]), ph.sb("az", [P, H]), ph.sb("ez", [P, H]), ph.sb("lz", [P, H])
        logf, negl = ph.sb("logf", [P, 2, H]), ph.sb("negl", [P, 2, H])
        decay, weighted = ph.sb("decay", [P, 2, BANK]), ph.sb("weighted", [P, 2, BANK])
        square, ssum, ms, rms = ph.sb("square", [P, D]), ph.sb("ssum", [P, 1]), ph.sb("ms", [P, 1]), ph.sb("rms", [P, 1])
        o, oT = ph.sb("o", [P, D]), ph.sb("oT", [P, KC, P])
        y, xo = ph.sb("y", [P, 2, D]), ph.sb("xo", [P, 2, D])
        ln = LayerNorm(ph)
        pT, pQ, pK, pV = ph.bank("pT"), ph.bank("pQ"), ph.bank("pK"), ph.bank("pV")
        pD, pA, pO, pY = ph.bank("pD"), ph.bank("pA"), ph.bank("pO"), ph.bank("pY")
        s_w = ph.sem("weights")
        s_x, s_stored = ph.sems("x"), ph.sems("stored")
        s_xr, s_turned, s_xT = ph.sem("xr"), ph.sem("turned"), ph.sem("xTs")
        s_q, s_k, s_v = ph.sem("q"), ph.sem("k"), ph.sem("v")
        s_qs, s_ks, s_vs = ph.sem("qs"), ph.sem("ks"), ph.sem("vs")
        s_z, s_ez, s_logf, s_l, s_negl = ph.sem("z"), ph.sem("ez"), ph.sem("logf"), ph.sem("l"), ph.sem("negl")
        s_diff, s_decay, s_a, s_aw, s_o = ph.sem("diff"), ph.sem("decay"), ph.sem("a"), ph.sem("aw"), ph.sem("o")
        s_ssum, s_ms, s_rms = ph.sem("ssum"), ph.sem("ms"), ph.sem("rms")
        s_on, s_oT, s_oTs, s_y, s_ys = (ph.sem(n) for n in ("on", "oT", "oTs", "y", "ys"))
        G = SLOTS
        L0 = D + H
        block = ctx.enter_context(nc.Block())
        loads = [
            (ident[:], w["ident"]), (identb[:], w["ident_bf16"]), (upto[:], w["upto"]), (future[:], w["future_bf16"]),
            (wq[:], w["L1_attn_WqT_slots"].rearrange("(c p) (t m) -> p c t m", p=P, t=TILES)),
            (wk[:], w["L1_attn_WkT_slots"].rearrange("(c p) (t m) -> p c t m", p=P, t=TILES)),
            (wvf[:], w["L1_attn_WvfT"].rearrange("(c p) n -> p c n", p=P)),
            (wo[:], w["L1_attn_WoT"].rearrange("(c p) n -> p c n", p=P)),
            (delta[:], to_all(w["L1_attn_delta"])), (weight[:], to_all(w["L1_attn_norm_weight"])),
        ]

        @block.sync
        def _(sp):
            for to, of in loads:
                sp.dma_start(to, of).then_inc(s_w, 16)

            def load(b, i):
                wait(sp, s_xr, b - 1)
                wait(sp, s_turned, b - 1)
                sp.dma_start(x[:, i, :], tokens(x_in, b)).then_inc(s_x[i], 16)

            pipeline(sp, [(0, load)])

        @block.gpsimd
        def _(pool):
            ln.constants(pool)

            def keep(b, i):
                pool.wait_ge(s_x[i], landed(b, i))
                wait(pool, s_ys, b - 1)
                nc.gpsimd.tensor_tensor(xr[:, i, :], x[:, i, :], ln.one[:].to_broadcast([P, D]), ALU.mult).then_inc(s_xr, 1)

            def rms_power(b, i):
                pool.wait_ge(s_ms, b + 1)
                wait(pool, s_on, b)
                nc.gpsimd.tensor_tensor(rms[:], ms[:], ln.half[:], ALU.pow).then_inc(s_rms, 1)

            pipeline(pool, [(3, lambda b, i: ln.power(pool, b)), (1, keep), (1, rms_power)])

        @block.tensor
        def _(pe):
            pe.wait_ge(s_w, 16 * len(loads))

            def project(b, i):
                pe.wait_ge(s_x[i], landed(b, i))
                wait(pe, s_oTs, b - 1)
                for k in range(KC):
                    t = nc.tensor.transpose(pT[:, k * P:(k + 1) * P], x[:, i, k * P:(k + 1) * P], ident[:])
                t.then_inc(s_turned, 1)
                pe.wait_ge(s_xT, b + 1)
                wait(pe, s_vs, b)
                wait(pe, s_z, 2 * b)
                wait(pe, s_negl, b)
                for k in range(KC):
                    mm = nc.tensor.matmul(pV[:, 0:L0], xT[:, k, :], wvf[:, k, :], start=k == 0, stop=k == KC - 1)
                mm.then_inc(s_v, 1)
                for bank, weights, free, done in ((pQ, wq, s_qs, s_q), (pK, wk, s_ks, s_k)):
                    wait(pe, free, b)
                    for t in range(TILES):
                        for k in range(KC):
                            mm = nc.tensor.matmul(bank[:, t * P:(t + 1) * P], weights[:, k, t, :], xT[:, k, :], start=k == 0, stop=k == KC - 1)
                    mm.then_inc(done, 1)
                pe.wait_ge(s_logf, b + 1)
                pe.wait_ge(s_vs, b + 1)
                nc.tensor.matmul(pV[:, L0:L0 + H], upto[:], logf[:, i, :], start=True, stop=True).then_inc(s_l, 1)

            def attend(b, i):
                pe.wait_ge(s_qs, b + 1)
                pe.wait_ge(s_ks, b + 1)

                def differences(g):
                    wait(pe, s_decay, G * b + g)
                    nc.tensor.matmul(pD[:].rearrange("p (t s) -> p t s", t=TILES), identb[:], future[:].unsqueeze(1).to_broadcast([P, TILES, S]),
                                     start=True, stop=False, skip_group_check=True)
                    for t in range(TILES):
                        h = TILES * g + t
                        mm = nc.tensor.matmul(pD[:, t * P:(t + 1) * P], logf[:, i, h:h + 1].to_broadcast([P, P]), upto[:],
                                              start=False, stop=t == TILES - 1, skip_group_check=True)
                    mm.then_inc(s_diff, 1)

                def products(g):
                    wait(pe, s_aw, G * b + g)
                    r = slice(32 * g, 32 * g + DK)
                    for t in range(TILES):
                        mm = nc.tensor.matmul(pA[:, t * P:(t + 1) * P], kT[r, i, t * P:(t + 1) * P], qT[r, i, t * P:(t + 1) * P], start=True, stop=True)
                    mm.then_inc(s_a, 1)

                def values(g):
                    pe.wait_ge(s_aw, G * b + g + 1)
                    if g == 0:
                        wait(pe, s_on, b)
                        wait(pe, s_ssum, b)
                    for t in range(TILES):
                        h = TILES * g + t
                        mm = nc.tensor.matmul(pO[:, h * DK:(h + 1) * DK], weighted[:, g % 2, t * P:(t + 1) * P],
                                              v[:, i, h * DK:(h + 1) * DK], start=True, stop=True)
                    mm.then_inc(s_o, 1)

                differences(0)
                products(0)
                for g in range(G):
                    if g + 1 < G:
                        differences(g + 1)
                        products(g + 1)
                    values(g)

            def output(b, i):
                pe.wait_ge(s_on, b + 1)
                pe.wait_ge(s_xT, lagged(b, 2))
                for k in range(KC):
                    mm = nc.tensor.transpose(pT[:, k * P:(k + 1) * P], o[:, k * P:(k + 1) * P], ident[:])
                mm.then_inc(s_oT, 1)
                pe.wait_ge(s_oTs, b + 1)
                wait(pe, s_ys, b)
                for k in range(KC):
                    mm = nc.tensor.matmul(pY[:, 0:D], oT[:, k, :], wo[:, k, :], start=k == 0, stop=k == KC - 1)
                mm.then_inc(s_y, 1)

            pipeline(pe, [(2, output), (0, project), (1, attend)])

        @block.scalar
        def _(act):
            def turned(b, i):
                act.wait_ge(s_turned, b + 1)
                wait(act, s_k, b)
                nc.scalar.activation(xT[:].rearrange("p a b -> p (a b)"), pT[:, 0:D], ACT.Copy).then_inc(s_xT, 1)

            def silu(b, i):
                act.wait_ge(s_q, b + 1)
                wait(act, s_a, G * (b - 1))
                nc.scalar.activation(qT[:, i, :], pQ[:], ACT.Silu).then_inc(s_qs, 1)
                act.wait_ge(s_k, b + 1)
                nc.scalar.activation(kT[:, i, :], pK[:], ACT.Silu).then_inc(s_ks, 1)

            def gate(b, i):
                act.wait_ge(s_z, 2 * b + 2)
                nc.scalar.activation(ez[:], az[:], ACT.Exp, scale=-1.0).then_inc(s_ez, 1)
                act.wait_ge(s_ez, 2 * b + 1)
                wait(act, s_logf, b)
                nc.scalar.activation(lz[:], ez[:], ACT.Ln, bias=1.0).then_inc(s_ez, 1)

            def attend(b, i):
                act.wait_ge(s_negl, b + 1)
                for g in range(G):
                    act.wait_ge(s_diff, G * b + g + 1)
                    wait(act, s_aw, G * b + g - 1)
                    for t in range(TILES):
                        h = TILES * g + t
                        e = nc.scalar.activation(decay[:, g % 2, t * P:(t + 1) * P], pD[:, t * P:(t + 1) * P], ACT.Exp, bias=negl[:, i, h:h + 1])
                    e.then_inc(s_decay, 1)
                act.wait_ge(s_o, G * b + G)
                wait(act, s_ms, b)
                nc.scalar.activation(square[:], pO[:, 0:D], ACT.Square, accum_out=ssum[:]).then_inc(s_ssum, 1)

            def output(b, i):
                act.wait_ge(s_oT, b + 1)
                wait(act, s_y, b)
                nc.scalar.activation(oT[:].rearrange("p a b -> p (a b)"), pT[:, 0:D], ACT.Copy).then_inc(s_oTs, 1)

            def store(b, i):
                act.wait_ge(ln.s_done, b + 1)
                act.dma_start(tokens(x_out, b), xo[:, i, :]).then_inc(s_stored[i], 16)

            pipeline(act, [(3, store), (2, output), (0, turned), (0, silu), (0, gate), (1, attend)])
            for i in range(2):
                act.wait_ge(s_stored[i], 16 * B // 2)

        @block.vector
        def _(dve):
            dve.wait_ge(s_w, 16 * len(loads))

            def gate(b, i):
                dve.wait_ge(s_v, b + 1)
                wait(dve, s_ez, 2 * b)
                nc.vector.tensor_tensor(z[:], pV[:, D:L0], delta[:], ALU.add).then_inc(s_z, 1)
                wait(dve, s_o, G * (b - 1))
                nc.vector.tensor_copy(v[:, i, :], pV[:, 0:D]).then_inc(s_vs, 1)
                dve.wait_ge(s_z, 2 * b + 1)
                nc.vector.scalar_tensor_tensor(az[:], z[:], -1.0, z[:], ALU.mult, ALU.max).then_inc(s_z, 1)
                dve.wait_ge(s_ez, 2 * b + 2)
                wait(dve, s_diff, G * (b - 1))
                nc.vector.scalar_tensor_tensor(logf[:, i, :], z[:], 0.0, lz[:], ALU.min, ALU.subtract).then_inc(s_logf, 1)
                dve.wait_ge(s_l, b + 1)
                wait(dve, s_decay, G * (b - 1))
                nc.vector.tensor_scalar(negl[:, i, :], pV[:, L0:L0 + H], -1.0, None, ALU.mult).then_inc(s_negl, 1)

            def attend(b, i):
                for g in range(G):
                    dve.wait_ge(s_a, G * b + g + 1)
                    dve.wait_ge(s_decay, G * b + g + 1)
                    wait(dve, s_o, G * b + g - 1)
                    nc.vector.tensor_tensor(weighted[:, g % 2, :], pA[:], decay[:, g % 2, :], ALU.mult).then_inc(s_aw, 1)
                dve.wait_ge(s_ssum, b + 1)
                wait(dve, s_rms, b)
                nc.vector.tensor_scalar(ms[:], ssum[:], 1.0 / D, RMS_EPS, ALU.mult, ALU.add).then_inc(s_ms, 1)

            def output(b, i):
                dve.wait_ge(s_rms, b + 1)
                wait(dve, s_oT, b)
                nc.vector.scalar_tensor_tensor(o[:], pO[:, 0:D], rms[:], weight[:], ALU.mult, ALU.mult).then_inc(s_on, 1)
                dve.wait_ge(s_y, b + 1)
                dve.wait_ge(s_xr, b + 1)
                nc.vector.tensor_tensor(y[:, i, :], pY[:, 0:D], xr[:, i, :], ALU.add).then_inc(s_ys, 1)
                dve.wait_ge(s_ys, b + 1)
                ln.statistics(dve, y[:, i, :], b)

            def norm(b, i):
                wait(dve, s_stored[i], landed(b - 2, i))
                ln.result(dve, y[:, i, :], xo[:, i, :], b)

            pipeline(dve, [(3, norm), (2, output), (0, gate), (1, attend)])


C = 2 * D
F1 = 128
TAPS = 9
ROW3 = 129


def context_kernels_1(nc, kernels, w):
    with ExitStack() as ctx:
        ph = Phase(nc, ctx, "ck1")
        hw, hb, hg, hbb = ph.sb("hw", [P, KC, C]), ph.sb("hb", [P, C]), ph.sb("hg", [P, C]), ph.sb("hbb", [P, C])
        w1, b1, w2, b2 = ph.sb("w1", [P, C // P, F1]), ph.sb("b1", [P, 1]), ph.sb("w2", [P, 1]), ph.sb("b2", [B, 1])
        k1, kb1, kg, kb = ph.sb("k1", [P, C // P, D]), ph.sb("kb1", [B, D]), ph.sb("kg", [B, D]), ph.sb("kb", [B, D])
        k2, kb2 = ph.sb("k2", [P, KC, H * TAPS]), ph.sb("kb2", [B, H * TAPS])
        ident, diag = ph.sb("ident", [P, P]), ph.sb("diag", [P, B, B])
        c, cT = ph.sb("c", [P, 2, D]), ph.sb("cT", [P, KC, P])
        e1, e2, e3 = ph.sb("e1", [P, C]), ph.sb("e2", [P, C]), ph.sb("e3", [P, C])
        e4 = ph.sb("e4", [P, C])
        ehs = ph.sb("ehs", [P, 2, C])
        eh, ehT, t1 = ph.sb("eh", [P, B, C]), ph.sb("ehT", [P, C // P, P]), ph.sb("t1", [P, P])
        score_row = ph.sb("score_row", [1, B * S])
        stats, mv, var, rstd, half, spare = (ph.sb(n, [P, k]) for n, k in (("stats", 6), ("mv", 2), ("var", 1), ("rstd", 1), ("half", 1), ("spare", 1)))
        sc, neg, ex, esum, er, aw = ph.sb("sc", [B, S]), ph.sb("neg", [B, 1]), ph.sb("ex", [B, S]), ph.sb("esum", [B, 1]), ph.sb("er", [B, 1]), ph.sb("aw", [B, S])
        awT, awd = ph.sb("awT", [P, B]), ph.sb("awd", [P, B, B])
        cc, ccT = ph.sb("cc", [B, C]), ph.sb("ccT", [P, C // P, B])
        u1, u2, u3, u4, uT = ph.sb("u1", [B, D]), ph.sb("u2", [B, D]), ph.sb("u3", [B, D]), ph.sb("u4", [B, D]), ph.sb("uT", [P, KC, B])
        kp, kmax, kd, ksum, kr, kout = ph.sb("kp", [B, H * TAPS]), ph.sb("kmax", [B, H]), ph.sb("kd", [B, H * TAPS]), ph.sb("ksum", [B, H]), ph.sb("kr", [B, H]), ph.sb("kout", [B, H * TAPS])
        pT, pE, pU, pH, pA = ph.bank("pT"), ph.bank("pE"), ph.bank("pU"), ph.bank("pH"), ph.bank("pA")
        s_kept = ph.sem("kept")
        s_w, s_half = ph.sem("weights"), ph.sem("half")
        s_c = ph.sems("c")
        s_turned, s_cT, s_e, s_stats, s_rstd, s_en, s_e4, s_eh = (ph.sem(n) for n in ("turned", "cT", "e", "stats", "rstd", "en", "e4", "eh"))
        s_ehT, s_ehTs, s_h, s_t1, s_a, s_row = (ph.sem(n) for n in ("ehT", "ehTs", "h", "t1", "a", "row"))
        s_sc, s_tail_v, s_tail_a, s_tail_p, s_tail_g, s_out = (ph.sem(n) for n in ("sc", "tail_v", "tail_a", "tail_p", "tail_g", "out"))
        block = ctx.enter_context(nc.Block())
        loads = [
            (ident[:], w["ident"]), (diag[:], w["diag"]),
            (hw[:], w["L1_xattn_hist_W"].rearrange("(c p) n -> p c n", p=P)), (hb[:], to_all(w["L1_xattn_hist_b"])),
            (hg[:], to_all(w["L1_xattn_hist_ln_g"])), (hbb[:], to_all(w["L1_xattn_hist_ln_b"])),
            (w1[:], w["L1_xattn_ctx_W1"].rearrange("(c p) n -> p c n", p=P)), (b1[:], w["L1_xattn_ctx_b1"].rearrange("(p o) -> p o", o=1)),
            (w2[:], w["L1_xattn_ctx_W2"]), (b2[:], w["L1_xattn_ctx_b2"].rearrange("(o n) -> o n", o=1).to_broadcast([B, 1])),
            (k1[:], w["L1_xattn_kg_W1"].rearrange("(c p) n -> p c n", p=P)), (kb1[:], to_all(w["L1_xattn_kg_b1"], B)),
            (kg[:], to_all(w["L1_xattn_kg_ln_g"], B)), (kb[:], to_all(w["L1_xattn_kg_ln_b"], B)),
            (k2[:], w["L1_xattn_kg_W2"].rearrange("(c p) n -> p c n", p=P)), (kb2[:], to_all(w["L1_xattn_kg_b2"], B)),
        ]

        @block.sync
        def _(sp):
            for to, of in loads:
                sp.dma_start(to, of).then_inc(s_w, 16)

            def load(b, i):
                wait(sp, s_turned, b - 1)
                sp.dma_start(c[:, i, :], tokens(w["ctx_1024"], b)).then_inc(s_c[i], 16)

            pipeline(sp, [(0, load)])
            sp.wait_ge(s_row, B)
            sp.dma_start(sc[:], score_row[:]).then_inc(s_sc, 16)
            sp.wait_ge(s_tail_v, 21)
            sp.dma_start(kernels, kout[:]).then_inc(s_out, 16)
            sp.wait_ge(s_out, 16)

        @block.gpsimd
        def _(pool):
            nc.gpsimd.memset(half[:], -0.5).then_inc(s_half, 1)
            pool.wait_ge(s_half, 1)
            pool.wait_ge(s_w, 16 * len(loads))

            def power(b, i):
                pool.wait_ge(s_stats, 4 * b + 4)
                wait(pool, s_en, 2 * b)
                nc.gpsimd.tensor_tensor(rstd[:], var[:], half[:], ALU.pow).then_inc(s_rstd, 1)
                pool.wait_ge(s_en, 2 * b + 2)
                wait(pool, s_eh, b)
                nc.gpsimd.tensor_tensor(e4[:], e3[:], hbb[:], ALU.add).then_inc(s_e4, 1)

            def keep(b, i):
                pool.wait_ge(s_eh, b + 1)
                nc.gpsimd.tensor_copy(eh[:, bass.ds(b, 1), :].rearrange("p o n -> p (o n)"), ehs[:, i, :]).then_inc(s_kept, 1)

            pipeline(pool, [(0, power), (1, keep)])
            pool.wait_ge(s_tail_v, 11)
            nc.gpsimd.tensor_tensor(rstd[0:B, :], var[0:B, :], half[0:B, :], ALU.pow).then_inc(s_tail_g, 1)

        @block.tensor
        def _(pe):
            pe.wait_ge(s_w, 16 * len(loads))

            def encode(b, i):
                pe.wait_ge(s_c[i], landed(b, i))
                wait(pe, s_cT, b)
                for k in range(KC):
                    t = nc.tensor.transpose(pT[:, k * P:(k + 1) * P], c[:, i, k * P:(k + 1) * P], ident[:])
                t.then_inc(s_turned, 1)
                pe.wait_ge(s_cT, b + 1)
                wait(pe, s_stats, 4 * b - 3)
                for k in range(KC):
                    mm = nc.tensor.matmul(pE[:], cT[:, k, :], hw[:, k, :], start=k == 0, stop=k == KC - 1)
                mm.then_inc(s_e, 1)

            def score(b, i):
                pe.wait_ge(s_eh, b + 1)
                wait(pe, s_ehTs, b)
                for k in range(C // P):
                    t = nc.tensor.transpose(pU[:, k * P:(k + 1) * P], ehs[:, i, k * P:(k + 1) * P], ident[:])
                t.then_inc(s_ehT, 1)
                pe.wait_ge(s_ehTs, b + 1)
                wait(pe, s_t1, b)
                for k in range(C // P):
                    mm = nc.tensor.matmul(pH[:, 0:P], w1[:, k, :], ehT[:, k, :], start=k == 0, stop=k == C // P - 1)
                mm.then_inc(s_h, 1)
                pe.wait_ge(s_t1, b + 1)
                wait(pe, s_row, b)
                nc.tensor.matmul(pA[0:1, 0:P], w2[:], t1[:], start=True, stop=True).then_inc(s_a, 1)

            pipeline(pe, [(0, encode), (1, score)])
            pe.wait_ge(s_tail_v, 3)
            nc.tensor.transpose(pT[:, 0:B], aw[:], ident[0:B, 0:B]).then_inc(s_tail_p, 1)
            pe.wait_ge(s_tail_v, 5)
            pe.wait_ge(s_kept, B)
            for b in range(B):
                mm = nc.tensor.matmul(pE[0:B, :], awd[:, b, :], eh[:, b, :], start=b == 0, stop=b == B - 1)
            mm.then_inc(s_tail_p, 1)
            pe.wait_ge(s_tail_v, 6)
            for k in range(C // P):
                t = nc.tensor.transpose(pT[:, k * B:(k + 1) * B], cc[:, k * P:(k + 1) * P], ident[0:B, 0:B])
            t.then_inc(s_tail_p, 1)
            pe.wait_ge(s_tail_v, 7)
            for k in range(C // P):
                mm = nc.tensor.matmul(pU[0:B, 0:D], ccT[:, k, :], k1[:, k, :], start=k == 0, stop=k == C // P - 1)
            mm.then_inc(s_tail_p, 1)
            pe.wait_ge(s_tail_a, 2)
            for k in range(KC):
                t = nc.tensor.transpose(pT[:, k * B:(k + 1) * B], u4[:, k * P:(k + 1) * P], ident[0:B, 0:B])
            t.then_inc(s_tail_p, 1)
            pe.wait_ge(s_tail_v, 15)
            for k in range(KC):
                mm = nc.tensor.matmul(pH[0:B, 0:H * TAPS], uT[:, k, :], k2[:, k, :], start=k == 0, stop=k == KC - 1)
            mm.then_inc(s_tail_p, 1)

        @block.scalar
        def _(act):
            act.wait_ge(s_w, 16 * len(loads))

            def encode(b, i):
                act.wait_ge(s_turned, b + 1)
                wait(act, s_e, b)
                nc.scalar.activation(cT[:].rearrange("p a b -> p (a b)"), pT[:, 0:D], ACT.Copy).then_inc(s_cT, 1)
                act.wait_ge(s_e4, b + 1)
                wait(act, s_kept, b - 1)
                wait(act, s_ehT, b - 1)
                nc.scalar.activation(ehs[:, i, :], e4[:], ACT.Gelu).then_inc(s_eh, 1)

            def score(b, i):
                act.wait_ge(s_ehT, b + 1)
                wait(act, s_h, b)
                nc.scalar.activation(ehT[:].rearrange("p a b -> p (a b)"), pU[:], ACT.Copy).then_inc(s_ehTs, 1)
                act.wait_ge(s_h, b + 1)
                wait(act, s_a, b)
                nc.scalar.activation(t1[:], pH[:, 0:P], ACT.Gelu, bias=b1[:]).then_inc(s_t1, 1)
                act.wait_ge(s_a, b + 1)
                nc.scalar.activation(score_row[0:1, bass.ds(b * S, S)], pA[0:1, 0:P], ACT.Copy).then_inc(s_row, 1)

            pipeline(act, [(0, encode), (1, score)])
            act.wait_ge(s_tail_v, 1)
            nc.scalar.activation(ex[:], sc[:], ACT.Exp, bias=neg[:], accum_out=esum[:]).then_inc(s_tail_a, 1)
            act.wait_ge(s_tail_v, 14)
            nc.scalar.activation(u4[:], u3[:], ACT.Gelu).then_inc(s_tail_a, 1)
            act.wait_ge(s_tail_v, 18)
            nc.scalar.activation(kp[:], kd[:], ACT.Exp).then_inc(s_tail_a, 1)

        @block.vector
        def _(dve):
            dve.wait_ge(s_w, 16 * len(loads))

            def encode(b, i):
                dve.wait_ge(s_e, b + 1)
                nc.vector.tensor_tensor(e1[:], pE[:], hb[:], ALU.add).then_inc(s_stats, 1)
                dve.wait_ge(s_stats, 4 * b + 1)
                nc.vector.bn_stats(stats[:], e1[:]).then_inc(s_stats, 1)
                dve.wait_ge(s_stats, 4 * b + 2)
                nc.vector.memset(spare[:], 0.0)
                nc.vector.bn_aggr(mv[:], stats[:]).then_inc(s_stats, 1)
                dve.wait_ge(s_stats, 4 * b + 3)
                wait(dve, s_rstd, b)
                nc.vector.tensor_scalar(var[:], mv[:, 1:2], LN_EPS, None, ALU.add).then_inc(s_stats, 1)
                dve.wait_ge(s_rstd, b + 1)
                nc.vector.tensor_scalar(e2[:], e1[:], mv[:, 0:1], rstd[:], ALU.subtract, ALU.mult).then_inc(s_en, 1)
                dve.wait_ge(s_en, 2 * b + 1)
                wait(dve, s_e4, b)
                nc.vector.tensor_tensor(e3[:], e2[:], hg[:], ALU.mult).then_inc(s_en, 1)

            pipeline(dve, [(0, encode)])
            tail = [0]

            def step(instruction):
                tail[0] += 1
                instruction.then_inc(s_tail_v, 1)
                dve.wait_ge(s_tail_v, tail[0])

            dve.wait_ge(s_sc, 16)
            nc.vector.tensor_scalar(sc[:], sc[:], b2[:], None, ALU.add).then_inc(s_half, 1)
            dve.wait_ge(s_half, 2)
            step(nc.vector.tensor_reduce(neg[:], sc[:], AX.X, ALU.max, negate=True))
            dve.wait_ge(s_tail_a, 1)
            step(nc.vector.reciprocal(er[:], esum[:]))
            step(nc.vector.tensor_scalar(aw[:], ex[:], er[:], None, ALU.mult))
            dve.wait_ge(s_tail_p, 1)
            step(nc.vector.tensor_copy(awT[:], pT[:, 0:B]))
            step(nc.vector.tensor_tensor(awd[:], diag[:], awT[:].unsqueeze(1).to_broadcast([P, B, B]), ALU.mult))
            dve.wait_ge(s_tail_p, 2)
            step(nc.vector.tensor_copy(cc[:], pE[0:B, :]))
            dve.wait_ge(s_tail_p, 3)
            step(nc.vector.tensor_copy(ccT[:].rearrange("p a b -> p (a b)"), pT[:, 0:C // P * B]))
            dve.wait_ge(s_tail_p, 4)
            step(nc.vector.tensor_tensor(u1[:], pU[0:B, 0:D], kb1[:], ALU.add))
            step(nc.vector.bn_stats(stats[0:B, :], u1[:]))
            step(nc.vector.bn_aggr(mv[0:B, :], stats[0:B, :]))
            step(nc.vector.tensor_scalar(var[0:B, :], mv[0:B, 1:2], LN_EPS, None, ALU.add))
            dve.wait_ge(s_tail_g, 1)
            step(nc.vector.tensor_scalar(u2[:], u1[:], mv[0:B, 0:1], rstd[0:B, :], ALU.subtract, ALU.mult))
            step(nc.vector.tensor_tensor(u1[:], u2[:], kg[:], ALU.mult))
            step(nc.vector.tensor_tensor(u3[:], u1[:], kb[:], ALU.add))
            dve.wait_ge(s_tail_p, 5)
            step(nc.vector.tensor_copy(uT[:].rearrange("p a b -> p (a b)"), pT[:, 0:KC * B]))
            dve.wait_ge(s_tail_p, 6)
            step(nc.vector.tensor_tensor(kout[:], pH[0:B, 0:H * TAPS], kb2[:], ALU.add))
            by_head = [t[:].rearrange("p (h t) -> p h t", h=H) for t in (kout, kd, kp)]
            step(nc.vector.tensor_reduce(kmax[:], by_head[0], AX.X, ALU.max))
            step(nc.vector.tensor_tensor(by_head[1], by_head[0], kmax[:].unsqueeze(2).to_broadcast([B, H, TAPS]), ALU.subtract))
            dve.wait_ge(s_tail_a, 3)
            step(nc.vector.tensor_reduce(ksum[:], by_head[2], AX.X, ALU.add))
            step(nc.vector.reciprocal(kr[:], ksum[:]))
            step(nc.vector.tensor_tensor(by_head[0], by_head[2], kr[:].unsqueeze(2).to_broadcast([B, H, TAPS]), ALU.mult))

def cross_attention_1(nc, x_in, x_out, w, kernels=None):
    with ExitStack() as ctx:
        ph = Phase(nc, ctx, "xa1")
        wq, wk = ph.sb("wq", [P, KC, TILES, P]), ph.sb("wk", [P, KC, TILES, P])
        wv, wo = ph.sb("wv", [P, KC, D]), ph.sb("wo", [P, KC, D])
        bo, ident, identb = ph.sb("bo", [P, D]), ph.sb("ident", [P, P]), ph.sb("identb", [P, P], BF16)
        causal_u8, keep, minus = ph.sb("causal_u8", [P, P], U8), ph.sb("keep", [P, P]), ph.sb("minus", [P, P], BF16)
        band, tap_of, taps = ph.sb("band", [P, ROW3]), ph.sb("tap_of", [1, TAPS, P]), ph.sb("taps", [1, B * H, TAPS])
        x, xbo, xT = ph.sb("x", [P, 2, D]), ph.sb("xbo", [P, 2, D]), ph.sb("xT", [P, KC, P])
        qT, kT, v = ph.sb("qT", [P, 2, BANK]), ph.sb("kT", [P, 2, BANK]), ph.sb("v", [P, 2, D])
        mine = ph.sb("mine", [P, 2, H * 3, 3])
        bands = ph.sb("bands", [P, 2, TILES * 3, ROW3])
        kept = ph.sb("kept", [P, 2, TILES, S + 2])
        prob, probT = ph.sb("prob", [P, 2, BANK]), ph.sb("probT", [P, 2, BANK])
        negmax, rowsum, rinv = ph.sb("negmax", [P, 2, H]), ph.sb("rowsum", [P, 2, H]), ph.sb("rinv", [P, H])
        o, oT = ph.sb("o", [P, D]), ph.sb("oT", [P, KC, P])
        y, xo = ph.sb("y", [P, 2, D]), ph.sb("xo", [P, 2, D])
        ln = LayerNorm(ph)
        pT, pQK, pV = ph.bank("pT"), ph.bank("pQK"), ph.bank("pV")
        pA, pS, pP, pO = ph.bank("pA"), [ph.bank("pS0"), ph.bank("pS1")], ph.bank("pP"), ph.bank("pO")
        s_w, s_const = ph.sem("weights"), ph.sem("const")
        s_x, s_stored = ph.sems("x"), ph.sems("stored")
        s_xbo, s_turned, s_xT = ph.sem("xbo"), ph.sem("turned"), ph.sem("xTs")
        s_q, s_k, s_v, s_tap = ph.sem("q"), ph.sem("k"), ph.sem("v"), ph.sem("tap")
        s_qs, s_ks, s_vs, s_mine = ph.sem("qs"), ph.sem("ks"), ph.sem("vs"), ph.sem("mine")
        s_bands, s_a, s_kept = ph.sem("bands"), ph.sem("a"), ph.sem("kept")
        s_scores, s_max, s_prob = ph.sem("scores"), ph.sem("max"), ph.sem("prob")
        s_pT, s_pTs, s_o = ph.sem("probT"), ph.sem("probTs"), ph.sem("o")
        s_rinv, s_on, s_oT, s_oTs, s_y, s_ys = (ph.sem(n) for n in ("rinv", "on", "oT", "oTs", "y", "ys"))
        G = SLOTS
        SCALE = float(DK) ** -0.5
        block = ctx.enter_context(nc.Block())
        loads = [
            (ident[:], w["ident"]), (identb[:], w["ident_bf16"]), (causal_u8[:], w["causal_u8"]),
            (band[:], w["band"]), (tap_of[:], w["tap_of"]), (taps[:].rearrange("o a t -> o (a t)"), kernels.rearrange("b n -> (b n)").rearrange("(o n) -> o n", o=1)),
            (wq[:], w["L1_xattn_Wq_slots"].rearrange("(c p) (t m) -> p c t m", p=P, t=TILES)),
            (wk[:], w["L1_xattn_Wk_slots"].rearrange("(c p) (t m) -> p c t m", p=P, t=TILES)),
            (wv[:], w["L1_xattn_Wv"].rearrange("(c p) n -> p c n", p=P)),
            (wo[:], w["L1_xattn_proj_W"].rearrange("(c p) n -> p c n", p=P)), (bo[:], to_all(w["L1_xattn_proj_b"])),
        ]

        @block.sync
        def _(sp):
            for to, of in loads:
                sp.dma_start(to, of).then_inc(s_w, 16)

            def load(b, i):
                wait(sp, s_xbo, b - 1)
                wait(sp, s_turned, b - 1)
                sp.dma_start(x[:, i, :], tokens(x_in, b)).then_inc(s_x[i], 16)

            pipeline(sp, [(0, load)])

        @block.gpsimd
        def _(pool):
            ln.constants(pool)
            nc.gpsimd.memset(kept[:], 0.0).then_inc(s_const, 1)
            pool.wait_ge(s_w, 16 * len(loads))

            def add_bo(b, i):
                pool.wait_ge(s_x[i], landed(b, i))
                wait(pool, s_ys, b - 1)
                nc.gpsimd.tensor_tensor(xbo[:, i, :], x[:, i, :], bo[:], ALU.add).then_inc(s_xbo, 1)

            def build_bands(b, i):
                pool.wait_ge(s_mine, b + 1)
                for g in range(G):
                    wait(pool, s_scores, G * b + g - 1)
                    n = TILES * 3
                    nc.gpsimd.tensor_tensor(bands[:, g % 2, :, :].rearrange("p a (m r) -> p a m r", r=3),
                                            band[:].rearrange("p (m r) -> p m r", r=3).unsqueeze(1).to_broadcast([P, n, ROW3 // 3, 3]),
                                            mine[:, i, n * g:n * g + n, :].unsqueeze(2).to_broadcast([P, n, ROW3 // 3, 3]), ALU.mult).then_inc(s_bands, 1)

            pipeline(pool, [(2, lambda b, i: ln.power(pool, b)), (0, add_bo), (1, build_bands)])

        @block.tensor
        def _(pe):
            pe.wait_ge(s_w, 16 * len(loads))
            pe.wait_ge(s_const, 3)

            def project(b, i):
                pe.wait_ge(s_x[i], landed(b, i))
                wait(pe, s_oTs, b - 1)
                for k in range(KC):
                    t = nc.tensor.transpose(pT[:, k * P:(k + 1) * P], x[:, i, k * P:(k + 1) * P], ident[:])
                t.then_inc(s_turned, 1)
                pe.wait_ge(s_xT, b + 1)
                wait(pe, s_mine, b)
                for t in range(TILES):
                    for k in range(KC):
                        mm = nc.tensor.matmul(pQK[:, t * P:(t + 1) * P], wq[:, k, t, :], xT[:, k, :], start=k == 0, stop=k == KC - 1)
                mm.then_inc(s_q, 1)
                wait(pe, s_ys, b - 1)
                wait(pe, s_vs, b)
                for k in range(KC):
                    mm = nc.tensor.matmul(pV[:, 0:D], xT[:, k, :], wv[:, k, :], start=k == 0, stop=k == KC - 1)
                mm.then_inc(s_v, 1)
                pe.wait_ge(s_qs, b + 1)
                for t in range(TILES):
                    for k in range(KC):
                        mm = nc.tensor.matmul(pQK[:, t * P:(t + 1) * P], wk[:, k, t, :], xT[:, k, :], start=k == 0, stop=k == KC - 1)
                mm.then_inc(s_k, 1)
                pe.wait_ge(s_ks, b + 1)
                mine_taps = taps[0:1, bass.ds(b * H, H), :].rearrange("o h (a c) -> o h a c", a=3)
                for r in range(3):
                    for a in range(3):
                        mm = nc.tensor.matmul(pQK[:, r * 48:(r + 1) * 48].rearrange("p (h c) -> p h c", h=H), tap_of[:, 3 * r + a, :],
                                              mine_taps[:, :, a, :], start=a == 0, stop=a == 2)
                mm.then_inc(s_tap, 1)

            def attend(b, i):
                pe.wait_ge(s_qs, b + 1)
                pe.wait_ge(s_ks, b + 1)
                pe.wait_ge(s_vs, b + 1)

                def products(g):
                    wait(pe, s_kept, G * b + g)
                    r = slice(32 * g, 32 * g + DK)
                    for t in range(TILES):
                        mm = nc.tensor.matmul(pA[:, t * P:(t + 1) * P], qT[r, i, t * P:(t + 1) * P], kT[r, i, t * P:(t + 1) * P], start=True, stop=True)
                    mm.then_inc(s_a, 1)

                def convolve(g):
                    wait(pe, s_prob, G * b + g - 1)
                    nc.tensor.matmul(pS[g % 2][:].rearrange("p (t s) -> p t s", t=TILES), identb[:], minus[:].unsqueeze(1).to_broadcast([P, TILES, S]),
                                     start=True, stop=False, skip_group_check=True)
                    pe.wait_ge(s_kept, G * b + g + 1)
                    pe.wait_ge(s_bands, G * b + g + 1)
                    for t in range(TILES):
                        for c in range(3):
                            mm = nc.tensor.matmul(pS[g % 2][:, t * P:(t + 1) * P], bands[:, g % 2, 3 * t + c, 0:P], kept[:, g % 2, t, c:c + S],
                                                  start=False, stop=t == TILES - 1 and c == 2, skip_group_check=True)
                    mm.then_inc(s_scores, 1)

                def turn(g):
                    pe.wait_ge(s_prob, G * b + g + 1)
                    wait(pe, s_pTs, G * b + g)
                    for t in range(TILES):
                        mm = nc.tensor.transpose(pP[:, t * P:(t + 1) * P], prob[:, g % 2, t * P:(t + 1) * P], ident[:])
                    mm.then_inc(s_pT, 1)

                def values(g):
                    pe.wait_ge(s_pTs, G * b + g + 1)
                    if g == 0:
                        wait(pe, s_on, b)
                    for t in range(TILES):
                        h = TILES * g + t
                        mm = nc.tensor.matmul(pO[:, h * DK:(h + 1) * DK], probT[:, g % 2, t * P:(t + 1) * P],
                                              v[:, i, h * DK:(h + 1) * DK], start=True, stop=True)
                    mm.then_inc(s_o, 1)

                for s in range(G + 3):
                    for lag, f in enumerate((products, convolve, turn, values)):
                        if 0 <= s - lag < G:
                            f(s - lag)

            def output(b, i):
                pe.wait_ge(s_on, b + 1)
                pe.wait_ge(s_xT, lagged(b, 2))
                for k in range(KC):
                    mm = nc.tensor.transpose(pT[:, k * P:(k + 1) * P], o[:, k * P:(k + 1) * P], ident[:])
                mm.then_inc(s_oT, 1)
                pe.wait_ge(s_oTs, b + 1)
                pe.wait_ge(s_vs, lagged(b, 2))
                for k in range(KC):
                    mm = nc.tensor.matmul(pV[:, 0:D], oT[:, k, :], wo[:, k, :], start=k == 0, stop=k == KC - 1)
                mm.then_inc(s_y, 1)

            pipeline(pe, [(0, project), (1, attend), (1, output)])

        @block.scalar
        def _(act):
            def turned(b, i):
                act.wait_ge(s_turned, b + 1)
                wait(act, s_k, b)
                nc.scalar.activation(xT[:].rearrange("p a b -> p (a b)"), pT[:, 0:D], ACT.Copy).then_inc(s_xT, 1)

            def copy_taps(b, i):
                act.wait_ge(s_tap, b + 1)
                wait(act, s_bands, G * (b - 1))
                nc.scalar.activation(mine[:, i, :, :].rearrange("p n r -> p r n"), pQK[:, 0:144].rearrange("p (r n) -> p r n", r=3), ACT.Copy).then_inc(s_mine, 1)

            def softmax(b, i):
                for g in range(G):
                    act.wait_ge(s_max, G * b + g + 1)
                    wait(act, s_pT, G * b + g - 1)
                    for t in range(TILES):
                        h = TILES * g + t
                        e = nc.scalar.activation(prob[:, g % 2, t * P:(t + 1) * P], pS[g % 2][:, t * P:(t + 1) * P], ACT.Exp,
                                                 bias=negmax[:, i, h:h + 1], accum_out=rowsum[:, i, h:h + 1])
                    e.then_inc(s_prob, 1)

            def output(b, i):
                act.wait_ge(s_oT, b + 1)
                wait(act, s_y, b)
                nc.scalar.activation(oT[:].rearrange("p a b -> p (a b)"), pT[:, 0:D], ACT.Copy).then_inc(s_oTs, 1)

            def store(b, i):
                act.wait_ge(ln.s_done, b + 1)
                act.dma_start(tokens(x_out, b), xo[:, i, :]).then_inc(s_stored[i], 16)

            pipeline(act, [(0, turned), (0, copy_taps), (1, softmax), (1, output), (2, store)])
            for i in range(2):
                act.wait_ge(s_stored[i], 16 * B // 2)

        @block.vector
        def _(dve):
            dve.wait_ge(s_w, 16 * len(loads))
            nc.vector.tensor_scalar(keep[:], causal_u8[:], -1.0, 1.0, ALU.mult, ALU.add).then_inc(s_const, 1)
            nc.vector.tensor_scalar(minus[:], causal_u8[:], -1e30, None, ALU.mult).then_inc(s_const, 1)
            dve.wait_ge(s_const, 3)

            def evacuate(b, i):
                dve.wait_ge(s_q, b + 1)
                wait(dve, s_a, G * (b - 1))
                nc.vector.tensor_scalar(qT[:, i, :], pQK[:], SCALE, None, ALU.mult).then_inc(s_qs, 1)
                dve.wait_ge(s_v, b + 1)
                wait(dve, s_o, G * (b - 1))
                nc.vector.tensor_copy(v[:, i, :], pV[:, 0:D]).then_inc(s_vs, 1)
                dve.wait_ge(s_k, b + 1)
                nc.vector.tensor_copy(kT[:, i, :], pQK[:]).then_inc(s_ks, 1)

            def softmax(b, i):
                def masked(g):
                    dve.wait_ge(s_a, G * b + g + 1)
                    wait(dve, s_scores, G * b + g - 1)
                    nc.vector.tensor_tensor(kept[:, g % 2, :, 1:S + 1], pA[:].rearrange("p (t s) -> p t s", t=TILES),
                                            keep[:].unsqueeze(1).to_broadcast([P, TILES, S]), ALU.mult).then_inc(s_kept, 1)

                def largest(g):
                    dve.wait_ge(s_scores, G * b + g + 1)
                    if g == 0:
                        wait(dve, s_prob, G * (b - 1))
                    nc.vector.tensor_reduce(negmax[:, i, TILES * g:TILES * g + TILES], pS[g % 2][:].rearrange("p (t s) -> p t s", t=TILES),
                                            AX.X, ALU.max, negate=True).then_inc(s_max, 1)

                def turned(g):
                    dve.wait_ge(s_pT, G * b + g + 1)
                    wait(dve, s_o, G * b + g - 1)
                    nc.vector.tensor_copy(probT[:, g % 2, :], pP[:]).then_inc(s_pTs, 1)

                for s in range(G + 2):
                    for lag, f in enumerate((masked, largest, turned)):
                        if 0 <= s - lag < G:
                            f(s - lag)

            def output(b, i):
                dve.wait_ge(s_prob, G * b + G)
                nc.vector.reciprocal(rinv[:], rowsum[:, i, :]).then_inc(s_rinv, 1)
                dve.wait_ge(s_rinv, b + 1)
                dve.wait_ge(s_o, G * b + G)
                wait(dve, s_oT, b)
                nc.vector.tensor_tensor(o[:].rearrange("p (h d) -> p h d", h=H), pO[:, 0:D].rearrange("p (h d) -> p h d", h=H),
                                        rinv[:].unsqueeze(2).to_broadcast([P, H, DK]), ALU.mult).then_inc(s_on, 1)
                dve.wait_ge(s_y, b + 1)
                dve.wait_ge(s_xbo, b + 1)
                nc.vector.tensor_tensor(y[:, i, :], pV[:, 0:D], xbo[:, i, :], ALU.add).then_inc(s_ys, 1)
                dve.wait_ge(s_ys, b + 1)
                ln.statistics(dve, y[:, i, :], b)

            def norm(b, i):
                wait(dve, s_stored[i], landed(b - 2, i))
                ln.result(dve, y[:, i, :], xo[:, i, :], b)

            pipeline(dve, [(2, norm), (0, evacuate), (1, softmax), (1, output)])


GROUPS, TOP_GROUPS = 8, 4
INTER = 128
SHARED = 2
ALL = E + SHARED
NB = B * S // BANK
TB = BANK // P
WG, WD = KC * 2 * INTER, D

RING = 8
DEEP = 4


def moe_ffn_1(nc, x_in, x_out, w, rows, results, places, experts):
    with ExitStack() as ctx:
        ph = Phase(nc, ctx, "moe")
        NT = TILES_OF_ROWS
        HT = NT // 2
        ident, gate_w, bias = ph.sb("ident", [P, P]), ph.sb("gate_w", [P, KC, E]), ph.sb("bias", [P, E])
        lower = ph.sb("lower", [P, GROUPS, GROUPS])
        upto, ones, tile_at = ph.sb("upto", [P, P], BF16), ph.sb("ones", [P, P], BF16), ph.sb("tile_at", [P, 2])
        acc, xT, xt = ph.sb("acc", [P, B, D]), ph.sb("xT", [P, KC, B * S]), ph.sb("xt", [P, 2, KC, P])
        x = ph.sb("x", [P, 2, D])
        ra, rb, rc, rd, re = (ph.sb(n, [P, B * E]) for n in ("ra", "rb", "rc", "rd", "re"))
        share, row_of = ph.sb("share", [P, B * E]), ph.sb("row_of", [P, B * E])
        chosen = ph.sb("chosen", [P, B * E], BF16)
        gmax, grank, gmask = (ph.sb(n, [P, B, GROUPS]) for n in ("gmax", "grank", "gmask"))
        top8, more, need, total, rtotal = (ph.sb(n, [P, B, c]) for n, c in (("top8", 8), ("more", 1), ("need", 1), ("total", 1), ("rtotal", 1)))
        wanted = ph.sb("wanted", [P, B, 1])
        row8, place, weight = ph.sb("row8", [P, B, 8]), ph.sb("place", [P, B, 8], U32), ph.sb("weight", [P, B, 8])
        na, nb, tiles, first = (ph.sb(n, [P, E]) for n in ("na", "nb", "tiles", "first"))
        before, of_tile, expert = ph.sb("before", [P, 2, E]), ph.sb("of_tile", [P, 2]), ph.sb("expert", [P, 2], U32)
        expert_row = ph.sb("expert_row", [1, NT], U32)
        xs, at = ph.sb("xs", [P, RING, D]), ph.sb("at", [P, RING, 8], U32)
        we = ph.sb("we", [P, RING, WG + WD])
        g, h = ph.sb("g", [P, 2, BANK]), ph.sb("h", [P, 2, BANK])
        xg, xgT, yg = ph.sb("xg", [P, RING, D]), ph.sb("xgT", [P, 2, KC, P]), ph.sb("yg", [P, RING, D])
        got, wcol = ph.sb("got", [P, DEEP, TOP_K, D]), ph.sb("wcol", [P, DEEP, 8])
        sums, xo = ph.sb("sums", [P, DEEP, D]), ph.sb("xo", [P, DEEP, D])
        spare = ph.sb("spare", [P, 1])
        ln = LayerNorm(ph)
        pG, pU, pD = ([ph.bank(f"{n}{i}") for i in range(c)] for n, c in (("pG", 2), ("pU", 2), ("pD", 4)))
        s_c, s_acc0, s_x, s_w, s_stored = ph.sem("constants"), ph.sem("acc0"), ph.sems("x"), ph.sems("shared"), ph.sems("stored", DEEP)
        s_turned, s_xt, s_xT, s_logits, s_exp = (ph.sem(n) for n in ("turned", "xt", "xT", "logits", "exp"))
        s_spare, s_ones, s_route, s_chosen, s_before, s_placed, s_out_places, s_row = (ph.sem(n) for n in ("spare", "ones", "route", "chosen", "before", "placed", "out_places", "row"))
        s_gate, s_up, s_g, s_h, s_down, s_acc = (ph.sem(n) for n in ("gate", "up", "g", "h", "down", "acc"))
        s_xs, s_spread = ph.sems("xs", RING), ph.sems("spread", RING)
        s_we, s_xg, s_kept = ph.sems("we", RING), ph.sems("xg", RING // 2), ph.sems("kept", RING // 2)
        s_xgt, s_xgT, s_gu, s_gate_t, s_ht, s_dt, s_yg = (ph.sem(n) for n in ("xgt", "xgT", "gu", "gate_t", "ht", "dt", "yg"))
        s_at, s_got, s_wcol, s_sum = ph.sems("at", DEEP), ph.sems("got", DEEP), ph.sem("wcol"), ph.sem("sum")
        block = ctx.enter_context(nc.Block())
        ROUTED = 129
        places_of = lambda b: places[bass.ds(b, 1)].rearrange("o p k -> (o p) k")
        tiles_of = lambda dram, t: dram[bass.ds(t * P, 2 * P), :].rearrange("(a p) d -> p a d", a=2)

        @block.sync
        def _(sp):
            for to, of in ((ident[:], w["ident"]), (gate_w[:], w["L1_ffn_gate_wT"].rearrange("(c p) n -> p c n", p=P)),
                           (bias[:], to_all(w["L1_ffn_gate_bias"])), (lower[:], w["moe_lower_group"]), (upto[:], w["upto_bf16"]),
                           (tile_at[:], w["moe_tile_number"])):
                sp.dma_start(to, of).then_inc(s_c, 16)

            def load_x(b, i):
                wait(sp, s_turned, b - 1)
                sp.dma_start(x[:, i, :], tokens(x_in, b)).then_inc(s_x[i], 16)

            pipeline(sp, [(0, load_x)])
            sp.dma_start(acc[:], x_in.rearrange("b p d -> p b d")).then_inc(s_acc0, 16)
            for n in range(SHARED):
                sp.dma_start(we[:, n, :], w["L1_ffn_experts"][E + n]).then_inc(s_w[n], 16)

            sp.wait_ge(s_placed, 2)
            sp.dma_start(places.rearrange("b p k -> p b k"), place[:]).then_inc(s_out_places, 16)
            for n in range(2):
                sp.dma_start(experts[n * HT:(n + 1) * HT].rearrange("(p o) -> p o", o=1), expert[0:HT, n:n + 1]).then_inc(s_out_places, 16)
            sp.wait_ge(s_out_places, 48)
            sp.dma_start(expert_row[:], experts.rearrange("(o n) -> o n", o=1)).then_inc(s_row, 16)

            def token_rows(b, i):
                wait(sp, s_spread[i], landed(b - RING, i, TOP_K, RING))
                sp.dma_start(xs[:, i, :], tokens(x_in, b)).then_inc(s_xs[i], 16)
                sp.dma_start(at[:, i, :], places_of(b)).then_inc(s_xs[i], 16)

            pipeline(sp, [(0, token_rows)], body=RING)
            sp.wait_ge(s_row, 16)
            sp.wait_ge(s_down, SHARED * NB)
            for i in range(RING):
                sp.wait_ge(s_spread[i], 16 * TOP_K * B // RING)

            def tile(t, i):
                e = sp.value_load(expert_row[0:1, bass.ds(t, 1)], min_val=0, max_val=E - 1)
                if i % 2 == 0:
                    wait(sp, s_xgt, t - RING + 2)
                    sp.dma_start(xg[:, i:i + 2, :], tiles_of(rows, t)).then_inc(s_xg[i // 2], 16)
                wait(sp, s_dt, t - RING + 1)
                sp.dma_start(we[:, i, :], w["L1_ffn_experts"][bass.ds(e, 1)].rearrange("o p n -> (o p) n")).then_inc(s_we[i], 16)

            pipeline(sp, [(0, tile)], n=NT, body=RING)

            def places_again(b, i):
                wait(sp, s_got[i], landed(b - DEEP, i, TOP_K, DEEP))
                sp.dma_start(at[:, i, :], places_of(b)).then_inc(s_at[i], 16)

            pipeline(sp, [(0, places_again)], body=DEEP)

        @block.gpsimd
        def _(pool):
            ln.constants(pool)
            nc.gpsimd.memset(ones[:], 1.0).then_inc(s_ones, 1)

            def take_waits(n):
                wait(pool, s_spare, n)
                nc.gpsimd.tensor_tensor(spare[:], ln.one[:], ln.one[:], ALU.mult).then_inc(s_spare, 1)

            def spread(b, i):
                pool.wait_ge(s_xs[i], landed(b, i, 2, RING))
                take_waits(b)
                for k in range(TOP_K):
                    pool.indirect_dma_start(rows, bass.IndirectOffsetOnAxis(ap=at[:, i, k:k + 1], axis=0), xs[:, i, :], None).then_inc(s_spread[i], 16)

            pipeline(pool, [(0, spread)], body=RING)
            for i in range(RING // 2):
                pool.wait_ge(s_kept[i], 16 * NT // RING)

            def gather(b, i):
                pool.wait_ge(s_at[i], landed(b, i, 1, DEEP))
                wait(pool, s_sum, TOP_K * (b - DEEP + 1))
                take_waits(B + b)
                for k in range(TOP_K):
                    pool.indirect_dma_start(got[:, i, k, :], None, results, bass.IndirectOffsetOnAxis(ap=at[:, i, k:k + 1], axis=0)).then_inc(s_got[i], 16)

            pipeline(pool, [(0, gather), (3, lambda b, i: ln.power(pool, b))], body=DEEP)

        @block.tensor
        def _(pe):
            pe.wait_ge(s_c, 6 * 16)

            def turn(b, i):
                pe.wait_ge(s_x[i], landed(b, i))
                wait(pe, s_xt, b - 1)
                wait(pe, s_xT, b - 1)
                for k in range(KC):
                    t = nc.tensor.transpose(pG[i][:, k * P:(k + 1) * P], x[:, i, k * P:(k + 1) * P], ident[:])
                t.then_inc(s_turned, 1)

            def logits(b, i):
                pe.wait_ge(s_xt, b + 1)
                wait(pe, s_exp, b - 1)
                for k in range(KC):
                    mm = nc.tensor.matmul(pU[i][:, 0:E], xt[:, i, k, :], gate_w[:, k, :], start=k == 0, stop=k == KC - 1)
                mm.then_inc(s_logits, 1)

            pipeline(pe, [(0, turn), (1, logits)])
            pe.wait_ge(s_ones, 1)
            pe.wait_ge(s_chosen, 1)
            for n in range(2):
                c = slice(n * BANK, (n + 1) * BANK)
                nc.tensor.matmul(pG[n][:], upto[:], chosen[:, c], start=True, stop=True).then_inc(s_before, 1)
                nc.tensor.matmul(pU[n][:], ones[:], chosen[:, c], start=True, stop=True).then_inc(s_before, 1)
            pe.wait_ge(s_placed, 1)

            def gate_up(e, n):
                if n == 0:
                    pe.wait_ge(s_w[e], 16)
                u = NB * e + n
                for half, (bank, free, done) in enumerate(((pG[n % 2], s_g, s_gate), (pU[n % 2], s_h, s_up))):
                    wait(pe, free, u - 1)
                    for k in range(KC):
                        c = (2 * k + half) * INTER
                        mm = nc.tensor.matmul(bank[:], we[:, e, c:c + INTER], xT[:, k, n * BANK:(n + 1) * BANK], start=k == 0, stop=k == KC - 1)
                    mm.then_inc(done, 1)

            def down(e, n):
                u = NB * e + n
                pe.wait_ge(s_h, u + 1)
                wait(pe, s_acc, TB * (u - 1))
                for t in range(TB):
                    bank = pD[2 * (n % 2) + t // 2]
                    mm = nc.tensor.matmul(bank[:, (t % 2) * D:(t % 2 + 1) * D], h[:, n % 2, t * P:(t + 1) * P], we[:, e, WG:WG + WD], start=True, stop=True)
                mm.then_inc(s_down, 1)

            for u in range(SHARED * NB + 1):
                if u < SHARED * NB:
                    gate_up(u // NB, u % NB)
                if u > 0:
                    down((u - 1) // NB, (u - 1) % NB)
            pe.wait_ge(s_acc, SHARED * B)

            def turn_rows(t, i):
                pe.wait_ge(s_xg[i // 2], landed(t, i, 1, RING))
                wait(pe, s_xgT, t - 1)
                for k in range(KC):
                    m = nc.tensor.transpose(pG[i % 2][:, k * P:(k + 1) * P], xg[:, i, k * P:(k + 1) * P], ident[:])
                m.then_inc(s_xgt, 1)

            def rows_gate_up(t, i):
                pe.wait_ge(s_we[i], landed(t, i, 1, RING))
                pe.wait_ge(s_xgT, t + 1)
                wait(pe, s_ht, t - 1)
                for half in range(2):
                    for k in range(KC):
                        c = (2 * k + half) * INTER
                        m = nc.tensor.matmul(pU[i % 2][:, half * P:(half + 1) * P], we[:, i, c:c + INTER], xgT[:, i % 2, k, :], start=k == 0, stop=k == KC - 1)
                m.then_inc(s_gu, 1)

            def rows_down(t, i):
                pe.wait_ge(s_ht, t + 1)
                wait(pe, s_yg, t - 1)
                nc.tensor.matmul(pD[i % 2][:, 0:D], h[:, i % 2, 0:P], we[:, i, WG:WG + WD], start=True, stop=True).then_inc(s_dt, 1)

            pipeline(pe, [(3, rows_down), (0, turn_rows), (1, rows_gate_up)], n=NT, body=RING)

        @block.scalar
        def _(act):
            def turned(b, i):
                act.wait_ge(s_turned, b + 1)
                wait(act, s_logits, b - 1)
                nc.scalar.activation(xt[:, i, :, :].rearrange("p c t -> p (c t)"), pG[i][:, 0:D], ACT.Copy).then_inc(s_xt, 1)

            def minus_exp(b, i):
                act.wait_ge(s_logits, b + 1)
                nc.scalar.activation(ra[:, bass.ds(b * E, E)], pU[i][:, 0:E], ACT.Exp, scale=-1.0).then_inc(s_exp, 1)

            pipeline(act, [(0, turned), (1, minus_exp)])
            for u in range(SHARED * NB):
                act.wait_ge(s_gate, u + 1)
                wait(act, s_h, u - 1)
                nc.scalar.activation(g[:, u % 2, :], pG[u % 2][:], ACT.Silu).then_inc(s_g, 1)
            act.wait_ge(s_h, SHARED * NB)

            def gated(t, i):
                act.wait_ge(s_gu, t + 1)
                wait(act, s_ht, t - 1)
                nc.scalar.activation(g[:, i % 2, 0:P], pU[i % 2][:, 0:P], ACT.Silu).then_inc(s_gate_t, 1)

            def results_out(t, i):
                act.wait_ge(s_dt, t + 1)
                wait(act, s_kept[i // 2], landed(t - RING, i, 1, RING))
                nc.scalar.activation(yg[:, i, :], pD[i % 2][:, 0:D], ACT.Copy).then_inc(s_yg, 1)
                if i % 2 == 1:
                    act.wait_ge(s_yg, t + 1)
                    act.dma_start(tiles_of(results, t - 1), yg[:, i - 1:i + 1, :]).then_inc(s_kept[i // 2], 16)

            pipeline(act, [(1, gated), (3, results_out)], n=NT, body=RING)

            def store(b, i):
                act.wait_ge(ln.s_done, b + 1)
                act.dma_start(tokens(x_out, b), xo[:, i, :]).then_inc(s_stored[i], 16)

            pipeline(act, [(0, store)], body=DEEP)
            for i in range(DEEP):
                act.wait_ge(s_stored[i], 16 * B // DEEP)

        @block.vector
        def _(dve):
            dve.wait_ge(s_c, 6 * 16)

            def turned(b, i):
                dve.wait_ge(s_xt, b + 1)
                nc.vector.tensor_copy(xT[:, :, bass.ds(b * S, S)], xt[:, i, :, :]).then_inc(s_xT, 1)

            pipeline(dve, [(0, turned)])
            dve.wait_ge(s_exp, B)
            done = [0]

            def step(*instructions):
                for ins in instructions:
                    ins.then_inc(s_route, 1)
                done[0] += len(instructions)
                dve.wait_ge(s_route, done[0])

            def running(a, b, size, part):
                far = 1
                while far < size:
                    V.tensor_copy(part(b, 0, far), part(a, 0, far)).then_inc(s_route, 1)
                    done[0] += 1
                    step(V.tensor_tensor(part(b, far, size), part(a, far, size), part(a, 0, size - far), ALU.add))
                    a, b, far = b, a, 2 * far
                return a

            V = nc.vector
            per_expert = lambda t: t[:].rearrange("p (b e) -> p b e", e=E)
            per_group = lambda t: t[:].rearrange("p (q e) -> p q e", e=E // GROUPS)
            pairs = lambda t: t[:].rearrange("p (b g f) -> p b g f", b=B, g=GROUPS)
            step(V.tensor_scalar(ra[:], ra[:], 1.0, None, ALU.add))
            step(V.reciprocal(rb[:], ra[:]))
            step(V.tensor_tensor(per_expert(ra), per_expert(rb), bias[:].unsqueeze(1).to_broadcast([P, B, E]), ALU.add))
            step(V.tensor_reduce(gmax[:].rearrange("p b g -> p (b g)"), per_group(ra), AX.X, ALU.max))
            mine, other = gmax[:].unsqueeze(3).to_broadcast([P, B, GROUPS, GROUPS]), gmax[:].unsqueeze(2).to_broadcast([P, B, GROUPS, GROUPS])
            step(V.tensor_tensor(pairs(rb), other, mine, ALU.is_gt), V.tensor_tensor(pairs(rc), other, mine, ALU.is_equal))
            step(V.tensor_tensor(pairs(rc), pairs(rc), lower[:].unsqueeze(1).to_broadcast([P, B, GROUPS, GROUPS]), ALU.mult))
            step(V.tensor_tensor(rb[:], rb[:], rc[:], ALU.add))
            step(V.tensor_reduce(grank[:], pairs(rb), AX.X, ALU.add))
            step(V.tensor_scalar(gmask[:], grank[:], float(TOP_GROUPS), None, ALU.is_lt))
            step(V.tensor_tensor(per_group(rb), per_group(ra), gmask[:].rearrange("p b g -> p (b g)").unsqueeze(2).to_broadcast([P, B * GROUPS, E // GROUPS]),
                                 ALU.mult))
            step(*(V.max(top8[:, b, :], rb[:, b * E:(b + 1) * E]) for b in range(B)))
            sixth = top8[:, :, TOP_K - 1:TOP_K].to_broadcast([P, B, E])
            step(V.tensor_tensor(per_expert(ra), per_expert(rb), sixth, ALU.is_gt), V.tensor_tensor(per_expert(rc), per_expert(rb), sixth, ALU.is_equal))
            step(V.tensor_reduce(more[:].rearrange("p b o -> p (b o)"), per_expert(ra), AX.X, ALU.add))
            step(V.tensor_scalar(need[:], more[:], -1.0, float(TOP_K), ALU.mult, ALU.add))
            step(V.tensor_copy(re[:], rc[:]))
            count = running(re, rd, E, lambda t, a, z: per_expert(t)[:, :, a:z])
            to = rd if count is re else re
            step(V.tensor_tensor(per_expert(to), per_expert(count), need[:].to_broadcast([P, B, E]), ALU.is_le))
            step(V.tensor_tensor(to[:], to[:], rc[:], ALU.mult))
            step(V.tensor_tensor(ra[:], ra[:], to[:], ALU.add))
            V.tensor_copy(chosen[:], ra[:]).then_inc(s_chosen, 1)
            step(V.tensor_tensor(rd[:], rb[:], ra[:], ALU.mult))
            step(V.tensor_reduce(total[:].rearrange("p b o -> p (b o)"), per_expert(rd), AX.X, ALU.add))
            step(V.tensor_scalar(total[:], total[:], 1e-8, None, ALU.add))
            step(V.reciprocal(rtotal[:], total[:]))
            step(V.tensor_tensor(per_expert(share), per_expert(rd), rtotal[:].to_broadcast([P, B, E]), ALU.mult))
            dve.wait_ge(s_before, 4)
            step(V.tensor_copy(rc[:, 0:BANK], pU[0][:]), V.tensor_copy(rc[:, BANK:2 * BANK], pU[1][:]))
            step(V.tensor_copy(re[:], rc[:]))
            sums_b = running(re, rd, B, lambda t, a, z: per_expert(t)[:, a:z, :])
            free = rd if sums_b is re else re
            step(V.tensor_tensor(free[:], sums_b[:], rc[:], ALU.subtract), V.tensor_copy(na[:], per_expert(sums_b)[:, B - 1, :]))
            step(V.tensor_scalar(nb[:], na[:], P / 2 - 0.5, 1.0 / P, ALU.add, ALU.mult))
            step(V.tensor_scalar(nb[:], nb[:], MAGIC, None, ALU.add))
            step(V.tensor_scalar(na[:], nb[:], MAGIC, None, ALU.subtract))
            step(V.tensor_copy(tiles[:], na[:]))
            last = running(na, nb, E, lambda t, a, z: t[:, a:z])
            step(V.tensor_tensor(first[:], last[:], tiles[:], ALU.subtract))
            step(V.scalar_tensor_tensor(per_expert(rc), first[:].unsqueeze(1).to_broadcast([P, B, E]), float(P), per_expert(free), ALU.mult, ALU.add))
            step(*(V.tensor_tensor(rc[:, n * BANK:(n + 1) * BANK], rc[:, n * BANK:(n + 1) * BANK], pG[n][:], ALU.add) for n in range(2)))
            step(V.tensor_tensor(row_of[:], rc[:], ra[:], ALU.mult))
            step(*(V.max(row8[:, b, :], row_of[:, b * E:(b + 1) * E]) for b in range(B)))
            step(V.tensor_scalar(row8[:, :, 0:TOP_K], row8[:, :, 0:TOP_K], 1.0, None, ALU.subtract))
            V.tensor_scalar(place[:], row8[:], 0.0, None, ALU.max).then_inc(s_placed, 1)
            step(V.tensor_tensor(before[:], last[:].unsqueeze(1).to_broadcast([P, 2, E]), tile_at[:].unsqueeze(2).to_broadcast([P, 2, E]), ALU.is_le))
            step(V.tensor_reduce(of_tile[:], before[:], AX.X, ALU.add))
            V.tensor_scalar(expert[:], of_tile[:], float(E - 1), None, ALU.min).then_inc(s_placed, 1)
            dve.wait_ge(s_acc0, 16)

            def product(u):
                dve.wait_ge(s_g, u + 1)
                dve.wait_ge(s_up, u + 1)
                wait(dve, s_down, u - 1)
                V.tensor_tensor(h[:, u % 2, :], g[:, u % 2, :], pU[u % 2][:], ALU.mult).then_inc(s_h, 1)

            def add(u):
                dve.wait_ge(s_down, u + 1)
                wait(dve, s_acc, TB * (u + 1 - NB))
                for t in range(TB // 2):
                    c = (u % NB) * TB + 2 * t
                    two = acc[:, c:c + 2, :].rearrange("p t d -> p (t d)")
                    V.tensor_tensor(two, pD[2 * (u % 2) + t][:], two, ALU.add).then_inc(s_acc, 2)

            for u in range(SHARED * NB + 1):
                if u < SHARED * NB:
                    product(u)
                if u > 0:
                    add(u - 1)
            for k in range(TOP_K):
                pair = (rb, rc, rd)[k % 3]
                step(V.tensor_scalar(wanted[:], row8[:, :, k:k + 1], 1.0, None, ALU.add))
                step(V.tensor_tensor(per_expert(pair), per_expert(row_of), wanted[:].to_broadcast([P, B, E]), ALU.is_equal))
                step(V.tensor_tensor(pair[:], pair[:], share[:], ALU.mult))
                step(V.tensor_reduce(weight[:, :, k], per_expert(pair), AX.X, ALU.add))
            assert done[0] == ROUTED, done[0]

            def turned_rows(t, i):
                dve.wait_ge(s_xgt, t + 1)
                wait(dve, s_gu, t - 1)
                V.tensor_copy(xgT[:, i % 2, :, :].rearrange("p c t -> p (c t)"), pG[i % 2][:, 0:D]).then_inc(s_xgT, 1)

            def product_rows(t, i):
                dve.wait_ge(s_gate_t, t + 1)
                wait(dve, s_dt, t - 1)
                V.tensor_tensor(h[:, i % 2, 0:P], g[:, i % 2, 0:P], pU[i % 2][:, P:2 * P], ALU.mult).then_inc(s_ht, 1)

            pipeline(dve, [(0, turned_rows), (2, product_rows)], n=NT, body=RING)

            def weigh(b, i):
                wait(dve, s_sum, TOP_K * (b - DEEP + 1))
                V.tensor_copy(wcol[:, i, 0:TOP_K], weight[:, bass.ds(b, 1), 0:TOP_K].rearrange("p o k -> p (o k)")).then_inc(s_wcol, 1)
                dve.wait_ge(s_wcol, b + 1)
                dve.wait_ge(s_got[i], landed(b, i, TOP_K, DEEP))
                for k in range(TOP_K):
                    before_ = acc[:, bass.ds(b, 1), :].rearrange("p o d -> p (o d)") if k == 0 else sums[:, i, :]
                    wait(dve, s_sum, TOP_K * b + k)
                    V.scalar_tensor_tensor(sums[:, i, :], got[:, i, k, :], wcol[:, i, k:k + 1], before_, ALU.mult, ALU.add).then_inc(s_sum, 1)
                dve.wait_ge(s_sum, TOP_K * (b + 1))
                ln.statistics(dve, sums[:, i, :], b)

            def norm(b, i):
                wait(dve, s_stored[i], landed(b - DEEP, i, 1, DEEP))
                ln.result(dve, sums[:, i, :], xo[:, i, :], b)

            pipeline(dve, [(1, norm), (0, weigh)], body=DEEP)


def _slots(w):
    w = w.reshape(-1, 4, 4, 16).transpose(0, 2, 1, 3)
    out = np.zeros(w.shape[:3] + (32,), w.dtype)
    out[..., :16] = w
    return out.reshape(w.shape[0], 512)


def _constants(bf16):
    o = {"ident": np.eye(P, dtype=np.float32), "ident_bf16": np.eye(P, dtype=bf16)}
    at = np.arange(P)
    o["upto"] = (at[:, None] <= at[None, :]).astype(np.float32)
    o["future_bf16"] = np.where(at[:, None] > at[None, :], -1e30, 0.0).astype(bf16)
    o["diag"] = np.ascontiguousarray(np.broadcast_to(np.eye(B, dtype=np.float32), (P, B, B)))
    col = np.arange(ROW3)
    o["band"] = ((np.abs(at[:, None] - col[None, :]) <= 1) & (col[None, :] < P)).astype(np.float32)
    o["tap_of"] = np.stack([((at - r + 1) % 3 == t) for r in range(3) for t in range(3)]).astype(np.float32).reshape(1, 9, P)
    t, j = at % W, np.arange(W)
    early = j[None, :] <= t[:, None]
    o["rank_cap"] = np.where(early, 3e38, -3e38).astype(np.float32)
    o["rank_floor"] = np.where(early, 0, W).astype(np.float32)
    o["rank_never"] = np.where(early, NEVER, 0).astype(np.float32)
    k = np.arange(8)
    o["rank_later"] = np.ascontiguousarray(np.broadcast_to(k[None, :] >= k[:, None], (P, 8, 8))).astype(bf16)
    o["rank_hidden"] = np.where((at[None, :] >= TOP) & (at[None, :] > W + t[:, None]), NEVER, 0).astype(bf16)
    o["moe_lower_group"] = np.ascontiguousarray(np.broadcast_to((k[None, :] < k[:, None]).astype(np.float32), (P, 8, 8)))
    half = DR // 2
    o["rope_fold"] = ((at[:, None] % DR == at[None, :] % DR) & (at[:, None] < 2 * DR)).astype(np.float32)
    theta = 1.0 / 10000.0 ** (2.0 * np.arange(half) / DR)
    f, pos = theta[at % half][:, None], np.arange(float(S))[None, :]
    sign = np.where(at % DR < half, -1.0, 1.0)[:, None]
    pq = np.where(at[:, None] < 2 * DR, pos, 2 * pos - (W - 1)) * f
    own = (at[:, None] // DR) % 2 == 0
    c, s = np.cos(pq), np.sin(pq)
    query = np.stack([np.where(own, c, sign * s), np.where(own, -s, sign * c)], axis=1)
    pk = pos * f
    key_own = np.stack([np.cos(pk), -np.sin(pk)], axis=1)
    key_other = np.stack([sign * np.sin(pk), sign * np.cos(pk)], axis=1)
    o["rope_trig"] = np.stack([query, key_own, key_other], axis=1).astype(np.float32)
    row = np.arange(TOP) % SORTED
    ps = (W + 0.0 + row)[:, None] * theta[np.arange(DR) % half][None, :]
    sign_row = np.where(np.arange(DR) < half, -1.0, 1.0)[None, :]
    of_cos = np.stack([np.cos(ps), sign_row * np.sin(ps)], axis=1)
    of_sin = np.stack([-np.sin(ps), sign_row * np.cos(ps)], axis=1)
    o["rope_sorted"] = np.stack([of_cos, of_sin], axis=1).astype(np.float32)
    o["rope_rank_of_row"] = row.astype(np.float32).reshape(TOP, 1)
    jj, tt = at[:, None], W + np.arange(W)[None, :]
    o["rope_local"] = ((jj >= tt - (W - 1)) & (jj <= tt)).astype(np.float32)
    o["upto_bf16"] = o["upto"].astype(bf16)
    o["moe_tile_number"] = np.stack([at, TILES_OF_ROWS // 2 + at], axis=1).astype(np.float32)
    o["rope_future"] = (jj > tt).astype(np.float32)
    return o


def _layout(a, bf16):
    o = _constants(bf16)
    T = lambda m: np.ascontiguousarray(m.T)
    o["x"], o["ctx_1024"] = a["x"], a["ctx_1024"]
    o["mask_keys"] = a["mask_Bx1xS2_bf1"]
    o["causal_u8"] = a["mask_SxS_bc0"]
    same = {
        "L0_attn": "idx_wq idx_w W_dq W_dkv W_uq W_uk W_uv W_out",
        "L0_xattn": "Wv Wo bv bo",
        "L1_attn": "delta norm_weight",
        "L1_xattn": "hist_W hist_b hist_ln_g hist_ln_b ctx_W1 ctx_b1 ctx_W2 ctx_b2 kg_W1 kg_b1 kg_ln_g kg_ln_b kg_W2 kg_b2 Wv proj_W proj_b",
        "L1_ffn": "gate_bias",
    }
    for part, names in same.items():
        for n in names.split():
            o[f"{part}_{n}"] = a[f"{part}_{n}"]
    g = lambda n: a["L0_attn_" + n]
    o["L0_attn_idx_wk_twice"] = np.concatenate([g("idx_wk")] * 2, axis=1)
    swap = np.r_[16:32, 0:16]
    kr = g("W_kr")
    o["L0_attn_W_kr_copies"] = np.concatenate([np.tile(kr, (1, 4)), np.tile(kr[:, swap], (1, 4))], axis=1)
    qr = g("W_qr").reshape(P, HA, DR)
    o["L0_attn_W_qr_copies"] = np.concatenate([qr, qr[:, :, swap]] * 2, axis=2).reshape(P, HA * P)
    o["L0_attn_raw_columns"] = np.tile(g("raw_delta"), 8).reshape(P, 1)
    o["L0_attn_raw_rows"] = np.tile(g("raw_delta"), 2).reshape(1, DR)
    for part in ("L0_xattn", "L1_xattn"):
        for n in ("Wq", "Wk"):
            o[f"{part}_{n}_slots"] = _slots(a[f"{part}_{n}"])
    for n in ("bq", "bk"):
        o[f"L0_xattn_{n}_slots"] = T(_slots(a["L0_xattn_" + n][None])[0].reshape(4, P))
    for n in ("Wq", "Wk"):
        o[f"L1_attn_{n}T_slots"] = _slots(T(a["L1_attn_" + n]))
    o["L1_attn_WvfT"] = T(np.concatenate([a["L1_attn_Wv"], a["L1_attn_Wf"]]))
    o["L1_attn_WoT"] = T(a["L1_attn_Wo"])
    for n in ("gate", "up", "down"):
        o[f"L0_ffn_w_{n}T"] = T(a[f"L0_ffn_w_{n}"])
    g = lambda n: a["L1_ffn_" + n]
    o["L1_ffn_gate_wT"] = T(g("gate_w"))
    gate = np.concatenate([g("eg_w"), g("sg_w").reshape(SHARED, INTER, D)])
    up = np.concatenate([g("eu_w"), g("su_w").reshape(SHARED, INTER, D)])
    down = np.concatenate([g("ed_w"), g("sd_w").reshape(D, SHARED, INTER).transpose(1, 0, 2)])
    gate_up = np.stack([gate, up], axis=1).reshape(ALL, 2, INTER, KC, P).transpose(0, 4, 3, 1, 2).reshape(ALL, P, WG)
    o["L1_ffn_experts"] = np.concatenate([gate_up, down.transpose(0, 2, 1)], axis=2)
    return {n: np.ascontiguousarray(v) for n, v in o.items()}


def build(nc, x, out, w):
    middle = [nc.dram_tensor(f"x{n}", (B, S, D), F32, kind="Internal").ap() for n in range(5)]
    ranks = nc.dram_tensor("ranks", (B, S - W, W), BF16, kind="Internal").ap()
    hidden = nc.dram_tensor("hidden", (B, S - W, S), BF16, kind="Internal").ap()
    kernels = nc.dram_tensor("kernels", (B, H * TAPS), F32, kind="Internal").ap()
    rows = nc.dram_tensor("rows", (TILES_OF_ROWS * P, D), F32, kind="Internal").ap()
    results = nc.dram_tensor("results", (TILES_OF_ROWS * P, D), F32, kind="Internal").ap()
    places = nc.dram_tensor("places", (B, P, 8), U32, kind="Internal").ap()
    experts = nc.dram_tensor("experts", (TILES_OF_ROWS,), U32, kind="Internal").ap()
    rank_keys_0(nc, x, ranks, hidden, w)
    sparse_attention_0(nc, x, middle[0], w, ranks, hidden)
    cross_attention_0(nc, middle[0], middle[1], w)
    ternary_ffn_0(nc, middle[1], middle[2], w, rows)
    linear_attention_1(nc, middle[2], middle[3], w)
    context_kernels_1(nc, kernels, w)
    cross_attention_1(nc, middle[3], middle[4], w, kernels)
    moe_ffn_1(nc, middle[4], out, w, rows, results, places, experts)


def kernel(**inputs):
    import concourse.bacc as bacc
    from concourse.bass_utils import run_bass_kernel_spmd
    from ml_dtypes import bfloat16

    arrays = _layout({n: np.ascontiguousarray(v) for n, v in inputs.items()}, bfloat16)
    nc = bacc.Bacc("TRN2", target_bir_lowering=False, num_devices=1)
    w = {n: nc.dram_tensor(n, a.shape, mybir.dt.from_np(a.dtype), kind="ExternalInput").ap() for n, a in arrays.items()}
    out = nc.dram_tensor("out", (B, S, D), F32, kind="ExternalOutput").ap()
    build(nc, w["x"], out, w)
    return run_bass_kernel_spmd(nc, [arrays], core_ids=[0]).results[0]["out"]
```

```python
from contextlib import ExitStack

import numpy as np

import concourse.bass as bass
from concourse import mybir

F32 = mybir.dt.float32
BF16 = mybir.dt.bfloat16
U8 = mybir.dt.uint8
U32 = mybir.dt.uint32
ALU = mybir.AluOpType
ACT = mybir.ActivationFunctionType
AX = mybir.AxisListType

B, S, D = 16, 128, 256
P = 128
KC = D // P
BANK = 512
MAGIC = 1.5 * 2.0**23
LN_EPS = 1e-5
E, TOP_K = 64, 6
TILES_OF_ROWS = (B * S * TOP_K + E * (P - 1)) // P + 1
CLEAR = TILES_OF_ROWS // B


class Phase:

    def __init__(self, nc, ctx, name):
        self.nc, self.ctx, self.name, self.semaphores = nc, ctx, name, []
        ctx.callback(self.clear)

    def clear(self):
        self.nc.clear_and_free_semaphores(self.semaphores)
        self.nc.all_engine_barrier()

    def sb(self, name, shape, dt=F32):
        return self.ctx.enter_context(self.nc.sbuf_tensor(f"{self.name}_{name}", shape, dt))

    def bank(self, name, dt=F32):
        return self.ctx.enter_context(self.nc.psum_tensor(f"{self.name}_{name}", [P, BANK * (2 if dt == BF16 else 1)], dt))

    def sem(self, name):
        self.semaphores.append(self.nc.alloc_semaphore(name=f"{self.name}_{name}"))
        return self.semaphores[-1]

    def sems(self, name, n=2):
        return [self.sem(f"{name}{i}") for i in range(n)]


class Early:

    def __init__(self, nc, ctx, phase, tensors):
        self.sem = nc.alloc_semaphore(name=f"{phase}_weights")
        ctx.callback(lambda: (nc.clear_and_free_semaphores([self.sem]), nc.all_engine_barrier()))
        self.tiles = {name: ctx.enter_context(nc.sbuf_tensor(f"{phase}_{name}", shape, dt)) for name, shape, dt, _ in tensors}
        self.loads = [(self.tiles[name], source) for name, _, _, source in tensors]

    def load(self, eng):
        for tile, source in self.loads:
            eng.dma_start(tile[:], source).then_inc(self.sem, 16)

    def wait(self, eng):
        eng.wait_ge(self.sem, 16 * len(self.loads))

    def get(self, names):
        return (self.tiles[name] for name in names.split())


def chunks(matrix, **kw):
    return matrix.rearrange("(c p) n -> p c n", p=P)


def wait(eng, sem, value):
    if not isinstance(value, int) or value > 0:
        eng.wait_ge(sem, value)


def landed(b, i, loads=1, buffers=2):
    return 16 // buffers * loads * (b - i) + 16 * loads


def pipeline(eng, stages, n=B, body=2):
    most = max(lag for lag, _ in stages)
    peel = -(-most // body) * body + body

    def straight(times):
        for t in times:
            for lag, f in stages:
                if 0 <= t - lag < n:
                    f(t - lag, (t - lag) % body)

    straight(range(peel))
    with eng.Fori(peel // body, n // body) as m:
        for k in range(body):
            for lag, f in stages:
                f(body * m + (k - lag), (k - lag) % body)
    straight(range(n, n + most))


def tokens(dram, b):
    return dram[bass.ds(b, 1)].rearrange("o p d -> (o p) d")


def to_all(row, parts=P):
    return row.rearrange("(o n) -> o n", o=1).to_broadcast([parts, row.shape[0]])


class LayerNorm:

    def __init__(self, ph, eps=LN_EPS, tag="ln"):
        self.nc, self.eps = ph.nc, eps
        self.stats, self.mv = ph.sb(tag + "_stats", [P, 6]), ph.sb(tag + "_mv", [P, 2])
        self.var, self.rstd, self.half = ph.sb(tag + "_var", [P, 1]), ph.sb(tag + "_rstd", [P, 1]), ph.sb(tag + "_half", [P, 1])
        self.one = ph.sb(tag + "_one", [P, 1])
        self.spare = ph.sb(tag + "_spare", [P, 1])
        self.s_half = ph.sem(tag + "_half")
        self.s_stats = ph.sem(tag + "_stats")
        self.s_rstd, self.s_done = ph.sem(tag + "_rstd"), ph.sem(tag + "_done")

    def constants(self, pool):
        self.nc.gpsimd.memset(self.half[:], -0.5).then_inc(self.s_half, 1)
        self.nc.gpsimd.memset(self.one[:], 1.0).then_inc(self.s_half, 1)
        pool.wait_ge(self.s_half, 2)

    def statistics(self, dve, y, b):
        nc = self.nc
        nc.vector.bn_stats(self.stats[:], y).then_inc(self.s_stats, 1)
        dve.wait_ge(self.s_stats, 3 * b + 1)
        nc.vector.memset(self.spare[:], 0.0)
        nc.vector.bn_aggr(self.mv[:], self.stats[:]).then_inc(self.s_stats, 1)
        dve.wait_ge(self.s_stats, 3 * b + 2)
        wait(dve, self.s_rstd, b)
        nc.vector.tensor_scalar(self.var[:], self.mv[:, 1:2], self.eps, None, ALU.add).then_inc(self.s_stats, 1)

    def power(self, pool, b):
        pool.wait_ge(self.s_stats, 3 * b + 3)
        wait(pool, self.s_done, b)
        self.nc.gpsimd.tensor_tensor(self.rstd[:], self.var[:], self.half[:], ALU.pow).then_inc(self.s_rstd, 1)

    def result(self, dve, y, xo, b):
        dve.wait_ge(self.s_rstd, b + 1)
        self.nc.vector.tensor_scalar(xo, y, self.mv[:, 0:1], self.rstd[:], ALU.subtract, ALU.mult).then_inc(self.s_done, 1)


def lagged(b, n, last=B):
    return min(b + n, last) if isinstance(b, int) else b + n


HA, DH, DR = 8, 64, 32
HI, W = 4, 64
TOP = 96
SORTED = TOP - W
NEVER = -1e30


def rank_keys_0(nc, x_in, ranks, hidden, w, prefetch=()):
    with ExitStack() as ctx:
        ph = Phase(nc, ctx, "rk0")
        NP = B // 2
        wq, wk = ph.sb("wq", [P, KC, HI * DH]), ph.sb("wk", [P, KC, P])
        wi, ident = ph.sb("wi", [P, HI]), ph.sb("ident", [P, P])
        cap, floor, never = ph.sb("cap", [P, W]), ph.sb("floor", [P, W]), ph.sb("never", [P, W])
        later = ph.sb("later", [P, 8, 8], BF16)
        x, xT = ph.sb("x", [P, 2, 2, D]), ph.sb("xT", [P, 2, KC, S])
        qT, kT = ph.sb("qT", [P, 2, 2, W]), ph.sb("kT", [P, 2, W])
        r, index0, index = ph.sb("r", [P, HI, W]), ph.sb("index0", [P, W]), ph.sb("index", [P, W])
        before = ph.sb("before", [P, W, W], BF16)
        half, quarter, eighth = (ph.sb(f"part{n}", [P, W, W // n], BF16) for n in (2, 4, 8))
        same, tie = ph.sb("same", [P, 8, 8, 8], BF16), ph.sb("tie", [P, W])
        count, rank0 = ph.sb("count", [P, W]), ph.sb("rank0", [P, W])
        rank, hid = ph.sb("rank", [P, 2, W], BF16), ph.sb("hid", [P, 2, S], BF16)
        pT, pQ, pK, pI = ph.bank("pT"), ph.bank("pQ"), ph.bank("pK"), [ph.bank("pI0"), ph.bank("pI1")]
        s_r = ph.sem("r")
        s_w, s_x, s_stored = ph.sem("weights"), ph.sems("x"), ph.sems("stored")
        s_turned, s_xT, s_q, s_qs, s_i, s_iv, s_rank, s_hid = (ph.sem(n) for n in ("turned", "xT", "q", "qs", "i", "iv", "rank", "hid"))
        block = ctx.enter_context(nc.Block())
        loads = [
            (wq[:], w["L0_attn_idx_wq"].rearrange("(c p) n -> p c n", p=P)), (wk[:], w["L0_attn_idx_wk_twice"].rearrange("(c p) n -> p c n", p=P)),
            (wi[:], to_all(w["L0_attn_idx_w"])), (ident[:], w["ident"]), (cap[:], w["rank_cap"]), (floor[:], w["rank_floor"]),
            (never[:], w["rank_never"]), (later[:], w["rank_later"]),
            (hid[:, 0, :], w["rank_hidden"]), (hid[:, 1, :], w["rank_hidden"]),
        ]
        NV = 17 + 6 + 2

        @block.sync
        def _(sp):
            for to, of in loads:
                sp.dma_start(to, of).then_inc(s_w, 16)

            def load(b, i):
                wait(sp, s_turned, b - 1)
                sp.dma_start(x[:, i, :, :], x_in[bass.ds(2 * b, 2)].rearrange("o p d -> p o d")).then_inc(s_x[i], 16)

            pipeline(sp, [(0, load)], n=NP)
            for tensors in prefetch:
                tensors.load(sp)

        @block.tensor
        def _(pe):
            pe.wait_ge(s_w, 16 * len(loads))

            def index_scores(b, i):
                pe.wait_ge(s_x[i], landed(b, i))
                wait(pe, s_xT, b)
                for o in range(2):
                    for k in range(KC):
                        t = nc.tensor.transpose(pT[:, (2 * o + k) * P:(2 * o + k + 1) * P], x[:, i, o, k * P:(k + 1) * P], ident[:])
                t.then_inc(s_turned, 1)
                pe.wait_ge(s_xT, b + 1)
                wait(pe, s_qs, 2 * b)
                for m in range(2):
                    for k in range(KC):
                        nc.tensor.matmul(pQ[:, m * P:(m + 1) * P].rearrange("p (o t) -> p o t", o=2), wq[:, k, m * P:(m + 1) * P],
                                         xT[:, :, k, W:S], start=k == 0, stop=k == KC - 1)
                for k in range(KC):
                    mm = nc.tensor.matmul(pK[:, 0:P].rearrange("p (o t) -> p o t", o=2), wk[:, k, :], xT[:, :, k, 0:W], start=k == 0, stop=k == KC - 1)
                mm.then_inc(s_q, 1)
                pe.wait_ge(s_qs, 2 * b + 2)
                wait(pe, s_r, 2 * b)
                nc.tensor.matmul(pK[:, P:P + 2], ident[:], ident[:, 0:2], start=True, stop=True)
                for o in range(2):
                    for h in range(HI):
                        rows = slice(64 * (h % 2), 64 * (h % 2) + DH)
                        mm = nc.tensor.matmul(pI[h % 2][64 * o:64 * o + W, (h // 2) * W:(h // 2 + 1) * W], qT[rows, h // 2, o, :], kT[rows, o, :],
                                              start=True, stop=True)
                mm.then_inc(s_i, 1)

            pipeline(pe, [(0, index_scores)], n=NP)

        @block.scalar
        def _(act):
            def copies(b, i):
                act.wait_ge(s_turned, b + 1)
                wait(act, s_q, b)
                nc.scalar.activation(xT[:].rearrange("p a b c -> p (a b c)"), pT[:], ACT.Copy).then_inc(s_xT, 1)
                act.wait_ge(s_q, b + 1)
                wait(act, s_i, b)
                nc.scalar.activation(qT[:].rearrange("p a b c -> p (a b c)"), pQ[:, 0:2 * P], ACT.Copy).then_inc(s_qs, 1)
                nc.scalar.activation(kT[:].rearrange("p a b -> p (a b)"), pK[:, 0:P], ACT.Copy).then_inc(s_qs, 1)

            def store(b, i):
                act.wait_ge(s_rank, b + 1)
                act.wait_ge(s_hid, b + 1)
                act.dma_start(ranks[bass.ds(2 * b, 2)].rearrange("o t j -> (o t) j"), rank[:, i, :]).then_inc(s_stored[i], 16)
                act.dma_start(hidden[bass.ds(2 * b, 2)].rearrange("o t j -> (o t) j"), hid[:, i, :]).then_inc(s_stored[i], 16)

            pipeline(act, [(0, copies), (1, store)], n=NP)
            for i in range(2):
                act.wait_ge(s_stored[i], 16 * NP)

        @block.vector
        def _(dve):
            dve.wait_ge(s_w, 16 * len(loads))

            def rank_all(b, i):
                dve.wait_ge(s_i, b + 1)
                for e in range(2):
                    nc.vector.scalar_tensor_tensor(r[:, e::2, :], pI[e][:, 0:2 * W].rearrange("p (m j) -> p m j", m=2), 0.0,
                                                   wi[:, e::2].unsqueeze(2).to_broadcast([P, 2, W]), ALU.max, ALU.mult).then_inc(s_r, 1)
                dve.wait_ge(s_r, 2 * b + 2)
                nc.vector.tensor_reduce(index0[:], r[:].rearrange("p h j -> p j h"), AX.X, ALU.add).then_inc(s_iv, 1)
                dve.wait_ge(s_iv, NV * b + 1)
                nc.vector.tensor_tensor(index[:], index0[:], cap[:], ALU.min).then_inc(s_iv, 1)
                dve.wait_ge(s_iv, NV * b + 2)
                for n in range(8):
                    js = slice(8 * n, 8 * n + 8)
                    mine = index[:, js].unsqueeze(2)
                    low = 8 * n + 8
                    nc.vector.tensor_tensor(before[:, js, 0:low], index[:, 0:low].unsqueeze(1).to_broadcast([P, 8, low]),
                                            mine.to_broadcast([P, 8, low]), ALU.is_ge).then_inc(s_iv, 1)
                    if low < W:
                        nc.vector.tensor_tensor(before[:, js, low:W], index[:, low:W].unsqueeze(1).to_broadcast([P, 8, W - low]),
                                                mine.to_broadcast([P, 8, W - low]), ALU.is_gt).then_inc(s_iv, 1)
                blocks = index[:].rearrange("p (n j) -> p n j", j=8)
                nc.vector.tensor_tensor(same[:], blocks.unsqueeze(2).to_broadcast([P, 8, 8, 8]), blocks.unsqueeze(3).to_broadcast([P, 8, 8, 8]),
                                        ALU.is_equal).then_inc(s_iv, 1)
                dve.wait_ge(s_iv, NV * b + 18)
                nc.vector.tensor_tensor(same[:], same[:], later[:].unsqueeze(1).to_broadcast([P, 8, 8, 8]), ALU.mult).then_inc(s_iv, 1)
                nc.vector.tensor_tensor(half[:], before[:, :, 0:W // 2], before[:, :, W // 2:W], ALU.add).then_inc(s_iv, 1)
                dve.wait_ge(s_iv, NV * b + 20)
                nc.vector.tensor_tensor(quarter[:], half[:, :, 0:W // 4], half[:, :, W // 4:W // 2], ALU.add).then_inc(s_iv, 1)
                nc.vector.tensor_reduce(tie[:], same[:].rearrange("p n j k -> p (n j) k"), AX.X, ALU.add).then_inc(s_iv, 1)
                dve.wait_ge(s_iv, NV * b + 21)
                nc.vector.tensor_tensor(eighth[:], quarter[:, :, 0:W // 8], quarter[:, :, W // 8:W // 4], ALU.add).then_inc(s_iv, 1)
                dve.wait_ge(s_iv, NV * b + 23)
                nc.vector.tensor_reduce(count[:], eighth[:], AX.X, ALU.add).then_inc(s_iv, 1)
                dve.wait_ge(s_iv, NV * b + 24)
                nc.vector.tensor_tensor(rank0[:], count[:], tie[:], ALU.subtract).then_inc(s_iv, 1)
                dve.wait_ge(s_iv, NV * b + 25)
                wait(dve, s_stored[i], landed(b - 2, i, 2))
                nc.vector.tensor_tensor(rank[:, i, :], rank0[:], floor[:], ALU.max).then_inc(s_rank, 1)
                nc.vector.scalar_tensor_tensor(hid[:, i, 0:W], rank0[:], float(SORTED), never[:], ALU.is_ge, ALU.mult).then_inc(s_hid, 1)

            pipeline(dve, [(0, rank_all)], n=NP)


def sparse_attention_0_early(w):
    g = lambda n: w["L0_attn_" + n]
    return [
        ("wdq", [P, KC, P], F32, chunks(g("W_dq"))), ("wdkv", [P, KC, DH], F32, chunks(g("W_dkv"))),
        ("wkr", [P, KC, 2, P], F32, g("W_kr_copies").rearrange("(c p) (a n) -> p c a n", p=P, a=2)),
        ("wuq", [P, BANK], F32, g("W_uq")), ("wuk", [DH, BANK], F32, g("W_uk")), ("wuv", [DH, BANK], F32, g("W_uv")),
        ("wqr", [P, HA, P], F32, g("W_qr_copies").rearrange("p (h n) -> p h n", h=HA)), ("wout", [P, HA // 2, D], F32, chunks(g("W_out"))),
        ("ident", [P, P], F32, w["ident"]), ("identb", [P, P], BF16, w["ident_bf16"]), ("fold", [P, P], F32, w["rope_fold"]),
        ("trig", [P, 3, 2, P], F32, w["rope_trig"]), ("srt", [TOP, 2, 2, DR], F32, w["rope_sorted"]),
        ("raw_c", [P, 1], F32, g("raw_columns")), ("raw_r", [TOP, DR], F32, g("raw_rows").to_broadcast([TOP, DR])), ("sel", [TOP, 1], F32, w["rope_rank_of_row"]),
        ("local", [P, W], F32, w["rope_local"]), ("future", [P, W], F32, w["rope_future"]),
    ]


def sparse_attention_0(nc, x_in, x_out, w, ranks, hidden, early, prefetch=()):
    with ExitStack() as ctx:
        ph = Phase(nc, ctx, "sa0")
        LATE = S - W
        Q4 = LATE // 4
        NT = HA // 2
        SCALE = float(DH + DR) ** -0.5
        PI = 3.1415925
        wdq, wdkv, wkr, wuq, wuk, wuv, wqr, wout = early.get("wdq wdkv wkr wuq wuk wuv wqr wout")
        ident, identb, fold, trig, srt = early.get("ident identb fold trig srt")
        raw_c, raw_r, sel, local, future = early.get("raw_c raw_r sel local future")
        ang = [ph.sb(f"ang{n}", [P, 1 + DR]) for n in range(5)]
        cs = ph.sb("cs", [P, 2, 1 + DR])
        tab, tab2 = ph.sb("tab", [P, 3, P]), ph.sb("tab2", [P, 3, P])
        st, st2 = ph.sb("st", [TOP, 2, DR]), ph.sb("st2", [TOP, 2, DR])
        part, parts = [ph.sb(f"part{n}", [TOP, 2, DR], BF16) for n in range(3)], ph.sb("parts", [TOP, 2, DR], BF16)
        x, xr, xT = ph.sb("x", [P, 2, D]), ph.sb("xr", [P, 2, D]), ph.sb("xT", [P, KC, P])
        rank, onehot = ph.sb("rank", [TOP, 2, LATE * W], BF16), ph.sb("onehot", [TOP, 2, LATE * W], BF16)
        hid = ph.sb("hid", [W, 2, S], BF16)
        low = ph.sb("low", [P, 2, P])
        kmin, kexp, kmu, krot = ph.sb("kmin", [P, 2 * P]), ph.sb("kexp", [P, 2 * P]), ph.sb("kmu", [P, 2 * P]), ph.sb("krot", [P, 2, P])
        qc, kc, v = ph.sb("qc", [P, 2, NT, 2, P]), ph.sb("kc", [P, 2, NT, P]), ph.sb("v", [P, 2, HA, DH + 1])
        qmin, qmu = ph.sb("qmin", [P, 2, BANK]), ph.sb("qmu", [P, 2, BANK])
        qrot = ph.sb("qrot", [P, 2, HA, P])
        ka, kb = ph.sb("ka", [P, 2, P]), ph.sb("kb", [P, 2, P])
        ql = ph.sb("ql", [P, 2, Q4, 4, HA])
        g1, g2, ks = ph.sb("g1", [P, BANK]), ph.sb("g2", [P, BANK]), ph.sb("ks", [P, 2, Q4, W])
        sa, sb_ = ph.sb("sa", [TOP, BANK]), ph.sb("sbb", [P, BANK])
        m1, m2 = ph.sb("m1", [P, BANK]), ph.sb("m2", [P, BANK])
        neg, rs = ph.sb("neg", [P, 2, NT]), ph.sb("rs", [P, 2, NT])
        pa, pb = ph.sb("pa", [P, NT, TOP]), ph.sb("pb", [P, NT, P])
        paT, pbT = ph.sb("paT", [TOP, BANK]), ph.sb("pbT", [P, BANK])
        rinv, o, oT = ph.sb("rinv", [P, HA]), ph.sb("o", [P, HA * DH]), ph.sb("oT", [P, NT, P])
        y, xo = ph.sb("y", [P, 2, D]), ph.sb("xo", [P, 2, D])
        ln = LayerNorm(ph)
        pT, p1, pA, pB = ph.bank("pT"), ph.bank("p1"), ph.bank("pA"), ph.bank("pB")
        bA, b1, b2, b3 = ph.bank("bA"), ph.bank("b1"), ph.bank("b2"), ph.bank("b3")
        names = ("const tab turned xTs low lows kmin kexp kmu krot onehot qk qcs kcs v vs qr qmin qexp qmu qrot fold ql "
                 "g gs ks s sab m sta stb turned_a turned_b max prob pta ptb ptsa ptsb o rinv on oT oTs y ys").split()
        s = {n: ph.sem(n) for n in names}
        s_set, s_ang, s_ang2 = ph.sem("set"), ph.sem("ang"), ph.sem("ang2")
        s_x, s_xr, s_rank, s_stored = ph.sems("x"), ph.sems("xr"), ph.sems("rank"), ph.sems("stored")
        block = ctx.enter_context(nc.Block())
        NZ = 6

        @block.sync
        def _(sp):
            def load(b, i):
                wait(sp, s["turned"], b - 1)
                sp.dma_start(x[:, i, :], tokens(x_in, b)).then_inc(s_x[i], 16)

            def load_ranks(b, i):
                wait(sp, s["onehot"], b - 1)
                wait(sp, s["s"], b - 1)
                sp.dma_start(rank[:, i, :], ranks[bass.ds(b, 1)].rearrange("o t j -> o (t j)").to_broadcast([TOP, LATE * W])).then_inc(s_rank[i], 16)
                sp.dma_start(hid[:, i, :], hidden[bass.ds(b, 1)].rearrange("o t j -> (o t) j")).then_inc(s_rank[i], 16)

            def load_again(b, i):
                wait(sp, s["ys"], b - 1)
                sp.dma_start(xr[:, i, :], tokens(x_in, b)).then_inc(s_xr[i], 16)

            pipeline(sp, [(0, load), (1, load_ranks), (2, load_again)])
            for tensors in prefetch:
                tensors.load(sp)

        @block.gpsimd
        def _(pool):
            ln.constants(pool)
            for t in (qc, ka, kb, ql):
                nc.gpsimd.memset(t[:], 0.0).then_inc(s["const"], 1)
            nc.gpsimd.memset(v[:], 1.0).then_inc(s["const"], 1)
            nc.gpsimd.memset(rs[:], 0.0).then_inc(s["const"], 1)

            def sorted_keys(b, i):
                for n in range(2):
                    pool.wait_ge(s["gs"], 4 * b + 2 * n + 2)
                    nc.gpsimd.tensor_tensor(ks[:, i, 8 * n:8 * n + 8, :].rearrange("p t j -> p (t j)"), g1[:], g2[:], ALU.add).then_inc(s["ks"], 1)

            def mix(b, i):
                pool.wait_ge(s["m"], 2 * b + 2)
                nc.gpsimd.tensor_tensor(m1[:], m1[:], m2[:], ALU.add).then_inc(s["sab"], 1)

            pipeline(pool, [(2, mix), (3, lambda b, i: ln.power(pool, b)), (1, sorted_keys)])

        @block.tensor
        def _(pe):
            early.wait(pe)
            pe.wait_ge(s["const"], NZ)
            pe.wait_ge(s["tab"], 1)

            def turn_x(b, i):
                pe.wait_ge(s_x[i], landed(b, i))
                wait(pe, s["vs"], b)
                wait(pe, s["oTs"], b - 2)
                for k in range(KC):
                    t = nc.tensor.transpose(pT[:, k * P:(k + 1) * P], x[:, i, k * P:(k + 1) * P], ident[:])
                t.then_inc(s["turned"], 1)

            def low_rank(b, i):
                pe.wait_ge(s["xTs"], b + 1)
                wait(pe, s["ys"], b - 2)
                wait(pe, s["kmu"], b)
                wait(pe, s["lows"], 2 * b)
                for k in range(KC):
                    nc.tensor.matmul(p1[:, 0:P], wdq[:, k, :], xT[:, k, :], start=k == 0, stop=k == KC - 1)
                for k in range(KC):
                    nc.tensor.matmul(p1[0:DH, P:2 * P], wdkv[:, k, :], xT[:, k, :], start=k == 0, stop=k == KC - 1)
                for a in range(2):
                    for k in range(KC):
                        mm = nc.tensor.matmul(p1[:, (2 + a) * P:(3 + a) * P], wkr[:, k, a, :], xT[:, k, :], start=k == 0, stop=k == KC - 1)
                mm.then_inc(s["low"], 1)

            def content(b, i):
                pe.wait_ge(s["lows"], 2 * b + 2)
                wait(pe, s["gs"], 4 * b)
                for t in range(NT):
                    mm = nc.tensor.matmul(pA[:, t * P:(t + 1) * P], wuq[:, t * P:(t + 1) * P], low[:, 0, :], start=True, stop=True)
                for t in range(NT):
                    mm = nc.tensor.matmul(pB[:, t * P:(t + 1) * P], wuk[:, t * P:(t + 1) * P], low[0:DH, 1, :], start=True, stop=True)
                mm.then_inc(s["qk"], 1)
                mm = nc.tensor.matmul(pT[:], low[0:DH, 1, :], wuv[:], start=True, stop=True)
                mm.then_inc(s["v"], 1)

            def rotary(b, i):
                pe.wait_ge(s["qcs"], 2 * b + 2)
                pe.wait_ge(s["kcs"], b + 1)
                for h in range(HA):
                    bank = pA if h < 4 else pB
                    mm = nc.tensor.matmul(bank[:, (h % 4) * P:(h % 4 + 1) * P], wqr[:, h, :], low[:, 0, :], start=True, stop=True)
                    if h % 4 == 3:
                        mm.then_inc(s["qr"], 1)

            def fold_queries(b, i):
                pe.wait_ge(s["qrot"], 2 * b + 2)
                nc.tensor.matmul(pA[:].rearrange("p (h t) -> p h t", h=HA), fold[:], qrot[:, i, :, W:S], start=True, stop=True).then_inc(s["fold"], 1)

            def sorted_angles(n):
                def f(b, i):
                    pe.wait_ge(s["onehot"], b + 1)
                    pe.wait_ge(s["ql"], 4 * b + 4)
                    wait(pe, s["gs"], 4 * b + 2 * n)
                    for c, bank in enumerate((pA, pB)):
                        for q in range(4):
                            at = (q * Q4 + 8 * n) * W
                            mm = nc.tensor.matmul(bank[32 * q:32 * q + 32, :], parts[:, c, :], onehot[:, i, at:at + BANK], start=True, stop=True)
                    mm.then_inc(s["g"], 1)
                return 1, f

            def scores(b, i):
                pe.wait_ge(s["krot"], 3 * b + 3)
                wait(pe, s["on"], 2 * b)
                wait(pe, s["ptsa"], b)
                wait(pe, s["ptsb"], b)
                nc.tensor.matmul(b1[:].rearrange("p (h t) -> p h t", h=HA), hid[:, i, :], identb[0:W, 0:W].unsqueeze(1).to_broadcast([W, HA, W]),
                                 start=True, stop=False, skip_group_check=True)
                nc.tensor.matmul(b3[:].rearrange("p (h t) -> p h t", h=HA), ka[:, i, :], qrot[:, i, :, W:S], start=True, stop=True)
                nc.tensor.matmul(b2[:].rearrange("p (h t) -> p h t", h=HA), kb[:, i, :], qrot[:, i, :, W:S], start=True, stop=True)
                nc.tensor.matmul(bA[0:TOP, :].rearrange("p (h t) -> p h t", h=HA), ka[:, i, 0:TOP], qrot[:, i, :, 0:W],
                                 start=True, stop=False, skip_group_check=True)
                for t in range(NT):
                    nc.tensor.matmul(bA[0:TOP, t * P:(t + 1) * P].rearrange("p (h t) -> p h t", h=2), kc[:, i, t, 0:TOP], qc[:, i, t, :, 0:W],
                                     start=False, stop=False, skip_group_check=True)
                for t in range(NT):
                    nc.tensor.matmul(b1[:, t * P:(t + 1) * P].rearrange("p (h t) -> p h t", h=2), kc[:, i, t, :], qc[:, i, t, :, W:S],
                                     start=False, stop=False, skip_group_check=True)
                pe.wait_ge(s["ks"], 2 * b + 2)
                by_quarter = b1[0:W, :].rearrange("p (h q t) -> p q h t", h=HA, q=4)
                for t in range(Q4):
                    mm = nc.tensor.matmul(by_quarter[:, :, :, t], ks[:, i, t, :], ql[:, i, t, :, :],
                                          start=False, stop=t == Q4 - 1, skip_group_check=True)
                mm.then_inc(s["s"], 1)

            def turn_scores(b, i):
                pe.wait_ge(s["sta"], b + 1)
                for t in range(NT):
                    mm = nc.tensor.transpose(bA[:, t * TOP:(t + 1) * TOP], sa[:, t * P:(t + 1) * P], ident[0:TOP, 0:TOP])
                mm.then_inc(s["turned_a"], 1)
                pe.wait_ge(s["stb"], b + 1)
                for t in range(NT):
                    mm = nc.tensor.transpose(b1[:, t * P:(t + 1) * P], sb_[:, t * P:(t + 1) * P], ident[:])
                mm.then_inc(s["turned_b"], 1)

            def turn_probabilities(b, i):
                pe.wait_ge(s["prob"], 2 * b + 1)
                for t in range(NT):
                    mm = nc.tensor.transpose(b2[0:TOP, t * P:(t + 1) * P], pa[:, t, :], ident[:])
                mm.then_inc(s["pta"], 1)
                pe.wait_ge(s["prob"], 2 * b + 2)
                for t in range(NT):
                    mm = nc.tensor.transpose(b3[:, t * P:(t + 1) * P], pb[:, t, :], ident[:])
                mm.then_inc(s["ptb"], 1)

            def values(b, i):
                at = lambda h: slice((h % 4) * (DH + 1), (h % 4 + 1) * (DH + 1))
                bank = lambda h: bA if h < 4 else b1
                pe.wait_ge(s["ptsa"], b + 1)
                for h in range(HA):
                    nc.tensor.matmul(bank(h)[0:W, at(h)], paT[:, h * W:(h + 1) * W], v[0:TOP, i, h, :], start=True, stop=True)
                pe.wait_ge(s["ptsb"], b + 1)
                for h in range(HA):
                    mm = nc.tensor.matmul(bank(h)[W:S, at(h)], pbT[:, h * W:(h + 1) * W], v[:, i, h, :], start=True, stop=True)
                mm.then_inc(s["o"], 1)

            def turn_output(b, i):
                pe.wait_ge(s["on"], 2 * b + 2)
                pe.wait_ge(s["vs"], lagged(b, 3))
                for t in range(NT):
                    mm = nc.tensor.transpose(pT[:, t * P:(t + 1) * P], o[:, t * P:(t + 1) * P], ident[:])
                mm.then_inc(s["oT"], 1)

            def output(b, i):
                pe.wait_ge(s["oTs"], b + 1)
                pe.wait_ge(s["lows"], lagged(2 * b, 6, 2 * B))
                pe.wait_ge(s["kmin"], lagged(b, 3))
                pe.wait_ge(s["kmu"], lagged(b, 3))
                wait(pe, s["ys"], b)
                for t in range(NT):
                    mm = nc.tensor.matmul(p1[:, 0:D], oT[:, t, :], wout[:, t, :], start=t == 0, stop=t == NT - 1)
                mm.then_inc(s["y"], 1)

            pipeline(pe, [(1, low_rank), (2, scores), (1, content), (2, turn_scores), (3, turn_output), (1, rotary), (2, turn_probabilities), (2, values),
                          (3, output), (1, fold_queries), (0, turn_x), sorted_angles(0), sorted_angles(1)])

        @block.scalar
        def _(act):
            flat = lambda t: t.rearrange("p a b -> p (a b)")
            act.wait_ge(s_ang, 1)
            nc.scalar.activation(ang[1][:], ang[0][:], ACT.Exp, scale=-1.0).then_inc(s_ang2, 1)
            act.wait_ge(s_ang, 6)
            nc.scalar.activation(cs[:, 1, :], ang[3][:], ACT.Sin).then_inc(s_ang2, 1)
            nc.scalar.activation(cs[:, 0, :], ang[4][:], ACT.Sin).then_inc(s_ang2, 1)

            def turned(b, i):
                act.wait_ge(s["turned"], b + 1)
                wait(act, s["low"], b)
                nc.scalar.activation(flat(xT[:]), pT[:, 0:D], ACT.Copy).then_inc(s["xTs"], 1)

            def low_rank(b, i):
                act.wait_ge(s["low"], b + 1)
                wait(act, s["qr"], 2 * b)
                wait(act, s["v"], b)
                nc.scalar.activation(low[:, 0, :], p1[:, 0:P], ACT.Copy).then_inc(s["lows"], 1)
                nc.scalar.activation(low[0:DH, 1, :], p1[0:DH, P:2 * P], ACT.Copy).then_inc(s["lows"], 1)

            def content(b, i):
                act.wait_ge(s["qk"], b + 1)
                wait(act, s["s"], b - 1)
                nc.scalar.activation(flat(kc[:, i, :, :]), pB[:], ACT.Copy).then_inc(s["kcs"], 1)
                act.wait_ge(s["v"], b + 1)
                wait(act, s["o"], b - 1)
                nc.scalar.activation(v[:, i, :, 0:DH], pT[:].rearrange("p (h d) -> p h d", h=HA), ACT.Copy).then_inc(s["vs"], 1)

            def softplus_exp(b, i):
                act.wait_ge(s["kmin"], b + 1)
                wait(act, s["kmu"], b)
                nc.scalar.activation(kexp[:], kmin[:], ACT.Exp).then_inc(s["kexp"], 1)
                for n in range(2):
                    act.wait_ge(s["qmin"], 2 * b + n + 1)
                    nc.scalar.activation(qmin[:, n, :], qmin[:, n, :], ACT.Exp).then_inc(s["qexp"], 1)

            def softplus_log(b, i):
                act.wait_ge(s["kexp"], 2 * b + 1)
                nc.scalar.activation(kexp[:], kexp[:], ACT.Ln, bias=1.0).then_inc(s["kexp"], 1)
                for n in range(2):
                    act.wait_ge(s["qexp"], 4 * b + 2 + n)
                    nc.scalar.activation(qmin[:, n, :], qmin[:, n, :], ACT.Ln, bias=1.0).then_inc(s["qexp"], 1)

            def early_scores(b, i):
                act.wait_ge(s["s"], b + 1)
                wait(act, s["turned_a"], b)
                nc.scalar.activation(sa[:], bA[0:TOP, :], ACT.Copy).then_inc(s["sta"], 1)

            def softmax(b, i):
                for n, (bank, p, width, read) in enumerate(((bA, pa, TOP, s["pta"]), (b1, pb, P, s["ptb"]))):
                    act.wait_ge(s["max"], 2 * b + n + 1)
                    wait(act, read, b)
                    for t in range(NT):
                        e = nc.scalar.activation(p[:, t, :], bank[:, t * width:(t + 1) * width], ACT.Exp, bias=neg[:, n, t:t + 1])
                    e.then_inc(s["prob"], 1)

            def late_probabilities(b, i):
                act.wait_ge(s["ptb"], b + 1)
                wait(act, s["o"], b)
                nc.scalar.activation(pbT[:], b3[:], ACT.Copy).then_inc(s["ptsb"], 1)

            def output(b, i):
                act.wait_ge(s["oT"], b + 1)
                wait(act, s["y"], b)
                nc.scalar.activation(flat(oT[:]), pT[:], ACT.Copy).then_inc(s["oTs"], 1)

            def store(b, i):
                act.wait_ge(ln.s_done, b + 1)
                act.dma_start(tokens(x_out, b), xo[:, i, :]).then_inc(s_stored[i], 16)

            pipeline(act, [(1, low_rank), (2, early_scores), (1, content), (2, softmax), (3, output), (1, softplus_exp), (4, store), (2, late_probabilities),
                           (1, softplus_log), (0, turned)])
            for i in range(2):
                act.wait_ge(s_stored[i], 16 * B // 2)

        @block.vector
        def _(dve):
            early.wait(dve)
            done = [0]

            def step(instruction):
                done[0] += 1
                instruction.then_inc(s_ang, 1)
                dve.wait_ge(s_ang, done[0])

            nc.vector.memset(ang[0][:], 0.0).then_inc(s_set, 1)
            dve.wait_ge(s_set, 1)
            nc.vector.tensor_copy(ang[0][:, 0:1], raw_c[:]).then_inc(s_set, 1)
            dve.wait_ge(s_set, 2)
            step(nc.vector.tensor_copy(ang[0][0:TOP, 1:1 + DR], raw_r[:]))
            dve.wait_ge(s_ang2, 1)
            step(nc.vector.tensor_scalar(ang[2][:], ang[1][:], 1.0, None, ALU.add))
            step(nc.vector.reciprocal(ang[1][:], ang[2][:]))
            step(nc.vector.tensor_scalar(ang[2][:], ang[1][:], -2.0 * float(np.pi), float(np.pi), ALU.mult, ALU.add))
            step(nc.vector.tensor_scalar(ang[3][:], ang[2][:], PI, -PI, ALU.min, ALU.max))
            nc.vector.scalar_tensor_tensor(ang[2][:], ang[3][:], -1.0, ang[3][:], ALU.mult, ALU.max).then_inc(s_set, 1)
            dve.wait_ge(s_set, 3)
            step(nc.vector.tensor_scalar(ang[4][:], ang[2][:], -1.0, float(np.pi) / 2, ALU.mult, ALU.add))
            dve.wait_ge(s_ang2, 3)
            step(nc.vector.tensor_scalar(cs[:], cs[:], -1.0, None, ALU.mult))
            step(nc.vector.tensor_scalar(tab[:], trig[:, :, 0, :], cs[:, 0, 0:1], None, ALU.mult))
            step(nc.vector.scalar_tensor_tensor(tab2[:], trig[:, :, 1, :], cs[:, 1, 0:1], tab[:], ALU.mult, ALU.add))
            step(nc.vector.tensor_scalar(tab[:, 0, :], tab2[:, 0, :], SCALE, None, ALU.mult))
            for n in range(2):
                rows = cs[0:TOP, n, 1:1 + DR].unsqueeze(1).to_broadcast([TOP, 2, DR])
                step(nc.vector.tensor_tensor((st, st2)[n][:], srt[:, n, :, :], rows, ALU.mult))
            step(nc.vector.tensor_tensor(st[:], st[:], st2[:], ALU.add))
            for n in range(3):
                step(nc.vector.tensor_copy(part[n][:], st[:]))
                if n < 2:
                    step(nc.vector.tensor_tensor(st[:], st[:], part[n][:], ALU.subtract))
            for n in range(3):
                rows = slice(32 * n, 32 * n + 32)
                step(nc.vector.tensor_copy(parts[rows], part[n][rows]))
            nc.vector.memset(rinv[:], 0.0).then_inc(s["tab"], 1)
            dve.wait_ge(s["const"], NZ)

            def key_angles(b, i):
                dve.wait_ge(s["lows"], 2 * b + 2)
                wait(dve, s["kexp"], 2 * b)
                nc.vector.tensor_scalar(kmin[:], p1[:, 2 * P:4 * P], 60.0, None, ALU.min).then_inc(s["kmin"], 1)

            def contents(b, i):
                dve.wait_ge(s["qk"], b + 1)
                wait(dve, s["s"], b - 1)
                for n in range(2):
                    rows = slice(64 * n, 64 * n + 64)
                    nc.vector.tensor_scalar(qc[rows, i, :, n, :], pA[rows, :].rearrange("p (t q) -> p t q", t=NT), SCALE, None, ALU.mult).then_inc(s["qcs"], 1)
                dve.wait_ge(s_rank[i], landed(b, i, 2))
                wait(dve, s["g"], 2 * (b - 1))
                nc.vector.tensor_scalar(onehot[:, i, :], rank[:, i, :], sel[:], None, ALU.is_equal).then_inc(s["onehot"], 1)

            def query_angles(b, i):
                for n, bank in enumerate((pA, pB)):
                    dve.wait_ge(s["qr"], 2 * b + n + 1)
                    wait(dve, s["qmu"], 2 * b)
                    nc.vector.tensor_scalar(qmin[:, n, :], bank[:], 60.0, None, ALU.min).then_inc(s["qmin"], 1)

            def angles(b, i):
                dve.wait_ge(s["kexp"], 2 * b + 2)
                nc.vector.tensor_tensor(kmu[:], kexp[:], p1[:, 2 * P:4 * P], ALU.max).then_inc(s["kmu"], 1)
                for n, bank in enumerate((pA, pB)):
                    dve.wait_ge(s["qexp"], 4 * b + 3 + n)
                    nc.vector.tensor_tensor(qmu[:, n, :], qmin[:, n, :], bank[:], ALU.max).then_inc(s["qmu"], 1)
                    dve.wait_ge(s["qmu"], 2 * b + n + 1)
                    wait(dve, s["s"], b - 1)
                    nc.vector.tensor_tensor(qrot[:, i, 4 * n:4 * n + 4, :], qmu[:, n, :].rearrange("p (h t) -> p h t", h=4),
                                            tab[:, 0, :].unsqueeze(1).to_broadcast([P, 4, P]), ALU.mult).then_inc(s["qrot"], 1)
                dve.wait_ge(s["kmu"], b + 1)
                nc.vector.tensor_tensor(krot[:], kmu[:].rearrange("p (a j) -> p a j", a=2), tab2[:, 1:3, :], ALU.mult).then_inc(s["krot"], 1)
                dve.wait_ge(s["krot"], 3 * b + 1)
                nc.vector.tensor_tensor(ka[0:64, i, :], krot[0:64, 0, :], krot[0:64, 1, :], ALU.add).then_inc(s["krot"], 1)
                nc.vector.tensor_tensor(kb[64:128, i, :], krot[64:128, 0, :], krot[64:128, 1, :], ALU.add).then_inc(s["krot"], 1)

            def folded_queries(b, i):
                dve.wait_ge(s["fold"], b + 1)
                for q in range(4):
                    rows = slice(32 * q, 32 * q + 32)
                    nc.vector.tensor_copy(ql[rows, i, :, q, :], pA[rows, :].rearrange("p (h q t) -> p q t h", h=HA, q=4)[:, q, :, :]).then_inc(s["ql"], 1)

            def rotate_sorted(n):
                def f(b, i):
                    dve.wait_ge(s["g"], 2 * b + n + 1)
                    wait(dve, s["ks"], 2 * b + n)
                    for c, (bank, t) in enumerate(((pA, g1), (pB, g2))):
                        nc.vector.tensor_tensor(t[:].rearrange("p (t j) -> p t j", j=W), bank[:].rearrange("p (t j) -> p t j", j=W),
                                                kmu[:, c * P:c * P + W].unsqueeze(1).to_broadcast([P, 8, W]), ALU.mult).then_inc(s["gs"], 1)
                return 1, f

            def late_scores(b, i):
                dve.wait_ge(s["s"], b + 1)
                for bank, t, mask in ((b2, m1, local), (b3, m2, future)):
                    nc.vector.tensor_tensor(t[:].rearrange("p (h t) -> p h t", h=HA), bank[:].rearrange("p (h t) -> p h t", h=HA),
                                            mask[:].unsqueeze(1).to_broadcast([P, HA, W]), ALU.mult).then_inc(s["m"], 1)
                dve.wait_ge(s["sab"], b + 1)
                nc.vector.tensor_tensor(sb_[:], b1[:], m1[:], ALU.add).then_inc(s["stb"], 1)

            def largest(b, i):
                for n, (bank, width, turned) in enumerate(((bA, TOP, s["turned_a"]), (b1, P, s["turned_b"]))):
                    dve.wait_ge(turned, b + 1)
                    nc.vector.tensor_reduce(neg[:, n, :], bank[:, 0:NT * width].rearrange("p (t j) -> p t j", t=NT), AX.X, ALU.max,
                                            negate=True).then_inc(s["max"], 1)

            def early_probabilities(b, i):
                dve.wait_ge(s["pta"], b + 1)
                wait(dve, s["o"], b)
                nc.vector.tensor_copy(paT[:], b2[0:TOP, :]).then_inc(s["ptsa"], 1)

            def divide(b, i):
                dve.wait_ge(s["o"], b + 1)
                by_head = [bank[:, 0:4 * (DH + 1)].rearrange("p (h d) -> p h d", h=4) for bank in (bA, b1)]
                for n in range(2):
                    nc.vector.reciprocal(rinv[:, 4 * n:4 * n + 4], by_head[n][:, :, DH]).then_inc(s["rinv"], 1)
                dve.wait_ge(s["rinv"], 2 * b + 2)
                wait(dve, s["oT"], b)
                for n in range(2):
                    nc.vector.tensor_tensor(o[:, n * D:(n + 1) * D].rearrange("p (h d) -> p h d", h=4), by_head[n][:, :, 0:DH],
                                            rinv[:, 4 * n:4 * n + 4].unsqueeze(2).to_broadcast([P, 4, DH]), ALU.mult).then_inc(s["on"], 1)

            def residual(b, i):
                dve.wait_ge(s["y"], b + 1)
                dve.wait_ge(s_xr[i], landed(b, i))
                nc.vector.tensor_tensor(y[:, i, :], p1[:, 0:D], xr[:, i, :], ALU.add).then_inc(s["ys"], 1)
                dve.wait_ge(s["ys"], b + 1)
                ln.statistics(dve, y[:, i, :], b)

            def norm(b, i):
                wait(dve, s_stored[i], landed(b - 2, i))
                ln.result(dve, y[:, i, :], xo[:, i, :], b)

            pipeline(dve, [(2, late_scores), (4, norm), (1, key_angles), (2, largest), (1, contents), (1, query_angles), (2, early_probabilities), (1, angles),
                           (2, divide), (1, folded_queries), (3, residual), rotate_sorted(0), rotate_sorted(1)])


H, DK = 16, 16
SLOTS, TILES = 4, 4
PAIR = 2


def cross_attention_0_early(w):
    g = lambda n: w["L0_xattn_" + n]
    in_tiles = lambda m: m.rearrange("(c p) (t m) -> p c t m", p=P, t=TILES)
    return [
        ("ident", [P, P], F32, w["ident"]), ("wq", [P, KC, TILES, P], F32, in_tiles(g("Wq_slots"))), ("wk", [P, KC, TILES, P], F32, in_tiles(g("Wk_slots"))),
        ("wv", [P, KC, D], F32, chunks(g("Wv"))), ("wo", [P, KC, D], F32, chunks(g("Wo"))),
        ("bq", [P, TILES], F32, g("bq_slots")), ("bk", [P, TILES], F32, g("bk_slots")), ("bv", [P, D], F32, to_all(g("bv"))), ("bo", [P, D], F32, to_all(g("bo"))),
        ("mask_u8", [P, B * S], U8, w["mask_keys"].rearrange("b o s -> o (b s)").to_broadcast([P, B * S])),
    ]


def cross_attention_0(nc, x_in, x_out, w, early, prefetch=()):
    with ExitStack() as ctx:
        ph = Phase(nc, ctx, "xa0")
        ident, wq, wk, wv, wo, bq, bk, bv, bo, mask_u8 = early.get("ident wq wk wv wo bq bk bv bo mask_u8")
        bq4, mask = ph.sb("bq4", [P, TILES]), ph.sb("mask", [P, B * S], BF16)
        mask_b = ph.sb("mask_b", [P, 2, S], BF16)
        ones = ph.sb("ones", [P, P], BF16)
        x, c = ph.sb("x", [P, 2, D]), ph.sb("c", [P, 2, D])
        xbo = ph.sb("xbo", [P, 2, D])
        xcT = ph.sb("xcT", [P, 4, P])
        qT, kT, v = ph.sb("qT", [P, 2, TILES, P]), ph.sb("kT", [P, 2, TILES, P]), ph.sb("v", [P, 2, D])
        prob, probT = ph.sb("prob", [P, 2, BANK]), ph.sb("probT", [P, 2, BANK])
        negmax, rowsum, rinv = ph.sb("negmax", [P, 2, H]), ph.sb("rowsum", [P, 2, H]), ph.sb("rinv", [P, H])
        o, oT = ph.sb("o", [P, D]), ph.sb("oT", [P, KC, P])
        y, xo = ph.sb("y", [P, 2, D]), ph.sb("xo", [P, 2, D])
        ln = LayerNorm(ph)
        pT, pQK, pV, pY = ph.bank("pT"), ph.bank("pQK"), ph.bank("pV"), ph.bank("pY")
        pS, pP, pO = [ph.bank("pS0"), ph.bank("pS1")], ph.bank("pP"), ph.bank("pO")
        s_const, s_mask, s_bq4 = ph.sem("ones"), ph.sem("mask"), ph.sem("bq4")
        s_x, s_stored = ph.sems("x"), ph.sems("stored")
        s_xbo, s_mask_b = ph.sem("xbo"), ph.sem("mask_b")
        s_turned, s_xcT = ph.sem("turned"), ph.sem("xcT")
        s_q, s_k, s_v = ph.sem("q"), ph.sem("k"), ph.sem("v")
        s_qs, s_ks, s_vs = ph.sem("qs"), ph.sem("ks"), ph.sem("vs")
        s_scores, s_max, s_prob = ph.sem("scores"), ph.sem("max"), ph.sem("prob")
        s_pT, s_pTs, s_o = ph.sem("probT"), ph.sem("probTs"), ph.sem("o")
        s_rinv, s_on, s_oT, s_oTs, s_y, s_ys = (ph.sem(n) for n in ("rinv", "on", "oT", "oTs", "y", "ys"))
        G = SLOTS
        SCALE = float(DK) ** -0.5
        block = ctx.enter_context(nc.Block())

        @block.sync
        def _(sp):
            def load(b, i):
                wait(sp, s_xbo, b - 1)
                wait(sp, s_turned, b - 1)
                sp.dma_start(x[:, i, :], tokens(x_in, b)).then_inc(s_x[i], 16)
                sp.dma_start(c[:, i, :], tokens(w["ctx_1024"], b)).then_inc(s_x[i], 16)

            pipeline(sp, [(0, load)])
            for tensors in prefetch:
                tensors.load(sp)

        @block.gpsimd
        def _(pool):
            nc.gpsimd.memset(ones[:], 1.0).then_inc(s_const, 1)
            early.wait(pool)

            def add_bo(b, i):
                pool.wait_ge(s_x[i], landed(b, i, 2))
                wait(pool, s_ys, b - 1)
                nc.gpsimd.tensor_tensor(xbo[:, i, :], x[:, i, :], bo[:], ALU.add).then_inc(s_xbo, 1)

            def copy_mask(b, i):
                wait(pool, s_scores, G * (b - 1))
                nc.gpsimd.tensor_copy(mask_b[:, i, :], mask[:, bass.ds(b * S, S)]).then_inc(s_mask_b, 1)

            def norm(b, i):
                ln.power(pool, b)

            ln.constants(pool)
            pool.wait_ge(s_mask, 1)
            pipeline(pool, [(0, add_bo), (0, copy_mask), (2, norm)])

        @block.tensor
        def _(pe):
            early.wait(pe)
            pe.wait_ge(s_const, 1)

            def turn_inputs(b, i):
                pe.wait_ge(s_x[i], landed(b, i, 2))
                wait(pe, s_oTs, b - 1)
                for j, src in enumerate((x, c)):
                    for k in range(KC):
                        t = nc.tensor.transpose(pT[:, (2 * j + k) * P:(2 * j + k + 1) * P], src[:, i, k * P:(k + 1) * P], ident[:])
                t.then_inc(s_turned, 1)

            def queries(b, i):
                pe.wait_ge(s_xcT, b + 1)
                wait(pe, s_ks, b)
                for t in range(TILES):
                    for k in range(KC):
                        mm = nc.tensor.matmul(pQK[:, t * P:(t + 1) * P], wq[:, k, t, :], xcT[:, k, :], start=k == 0, stop=k == KC - 1)
                mm.then_inc(s_q, 1)

            def context_values(b, i):
                wait(pe, s_vs, b)
                for k in range(KC):
                    mm = nc.tensor.matmul(pV[:, 0:D], xcT[:, 2 + k, :], wv[:, k, :], start=k == 0, stop=k == KC - 1)
                mm.then_inc(s_v, 1)

            def keys(b, i):
                pe.wait_ge(s_qs, b + 1)
                for t in range(TILES):
                    for k in range(KC):
                        mm = nc.tensor.matmul(pQK[:, t * P:(t + 1) * P], wk[:, k, t, :], xcT[:, 2 + k, :], start=k == 0, stop=k == KC - 1)
                mm.then_inc(s_k, 1)

            def scores(g):
                def f(b, i):
                    if g == 0:
                        pe.wait_ge(s_qs, b + 1)
                        pe.wait_ge(s_ks, b + 1)
                        pe.wait_ge(s_vs, b + 1)
                        pe.wait_ge(s_mask_b, b + 1)
                    wait(pe, s_prob, G * b + g - 1)
                    nc.tensor.matmul(pS[g % 2][:].rearrange("p (t s) -> p t s", t=TILES), ones[32 * g:32 * g + 1, :],
                                     mask_b[32 * g:32 * g + 1, i, :].unsqueeze(1).to_broadcast([1, TILES, S]),
                                     start=True, stop=False, skip_group_check=True)
                    r = slice(32 * g, 32 * g + DK)
                    for t in range(TILES):
                        mm = nc.tensor.matmul(pS[g % 2][:, t * P:(t + 1) * P], qT[r, i, t, :], kT[r, i, t, :],
                                              start=False, stop=t == TILES - 1, skip_group_check=True)
                    mm.then_inc(s_scores, 1)
                return 1, f

            def turn(g):
                def f(b, i):
                    pe.wait_ge(s_prob, G * b + g + 1)
                    wait(pe, s_pTs, G * b + g)
                    for t in range(TILES):
                        mm = nc.tensor.transpose(pP[:, t * P:(t + 1) * P], prob[:, g % 2, t * P:(t + 1) * P], ident[:])
                    mm.then_inc(s_pT, 1)
                return 1, f

            def values(g):
                def f(b, i):
                    pe.wait_ge(s_pTs, G * b + g + 1)
                    if g == 0:
                        wait(pe, s_on, b)
                    for t in range(TILES):
                        h = TILES * g + t
                        mm = nc.tensor.matmul(pO[:, h * DK:(h + 1) * DK], probT[:, g % 2, t * P:(t + 1) * P],
                                              v[:, i, h * DK:(h + 1) * DK], start=True, stop=True)
                    mm.then_inc(s_o, 1)
                return 1, f

            def turn_output(b, i):
                pe.wait_ge(s_on, b + 1)
                pe.wait_ge(s_xcT, lagged(b, 2))
                for k in range(KC):
                    mm = nc.tensor.transpose(pT[:, k * P:(k + 1) * P], o[:, k * P:(k + 1) * P], ident[:])
                mm.then_inc(s_oT, 1)

            def output(b, i):
                pe.wait_ge(s_oTs, b + 1)
                wait(pe, s_ys, b)
                for k in range(KC):
                    mm = nc.tensor.matmul(pY[:, 0:D], oT[:, k, :], wo[:, k, :], start=k == 0, stop=k == KC - 1)
                mm.then_inc(s_y, 1)

            pipeline(pe, [scores(0), (2, turn_output), scores(1), (0, turn_inputs), turn(0), (0, queries), scores(2), turn(1), (0, context_values), values(0),
                          scores(3), values(1), turn(2), (0, keys), turn(3), (2, output), values(2), values(3)])

        @block.scalar
        def _(act):
            def turned(b, i):
                act.wait_ge(s_turned, b + 1)
                wait(act, s_k, b)
                nc.scalar.activation(xcT[:].rearrange("p a b -> p (a b)"), pT[:], ACT.Copy).then_inc(s_xcT, 1)

            def softmax(g):
                def f(b, i):
                    act.wait_ge(s_max, G * b + g + 1)
                    wait(act, s_pT, G * b + g - 1)
                    if g == 0:
                        wait(act, s_rinv, b - 1)
                    for t in range(TILES):
                        h = TILES * g + t
                        e = nc.scalar.activation(prob[:, g % 2, t * P:(t + 1) * P], pS[g % 2][:, t * P:(t + 1) * P], ACT.Exp,
                                                 bias=negmax[:, i, h:h + 1], accum_out=rowsum[:, i, h:h + 1])
                    e.then_inc(s_prob, 1)
                return 1, f

            def output(b, i):
                act.wait_ge(s_oT, b + 1)
                wait(act, s_y, b)
                nc.scalar.activation(oT[:].rearrange("p a b -> p (a b)"), pT[:, 0:D], ACT.Copy).then_inc(s_oTs, 1)

            def store(b, i):
                act.wait_ge(ln.s_done, b + 1)
                act.dma_start(tokens(x_out, b), xo[:, i, :]).then_inc(s_stored[i], 16)

            pipeline(act, [(2, output), softmax(0), (0, turned), softmax(1), softmax(2), softmax(3), (3, store)])
            for i in range(2):
                act.wait_ge(s_stored[i], 16 * B // 2)

        @block.vector
        def _(dve):
            early.wait(dve)
            nc.vector.tensor_scalar(mask[:], mask_u8[:], 1.0, 1e9, ALU.subtract, ALU.mult).then_inc(s_mask, 1)
            nc.vector.tensor_scalar(bq4[:], bq[:], SCALE, None, ALU.mult).then_inc(s_bq4, 1)
            dve.wait_ge(s_bq4, 1)

            def queries(b, i):
                dve.wait_ge(s_q, b + 1)
                wait(dve, s_scores, G * (b - 1))
                nc.vector.scalar_tensor_tensor(qT[:, i, :, :], pQK[:].rearrange("p (t s) -> p t s", t=TILES), SCALE,
                                               bq4[:].unsqueeze(2).to_broadcast([P, TILES, S]), ALU.mult, ALU.add).then_inc(s_qs, 1)

            def context_values(b, i):
                dve.wait_ge(s_v, b + 1)
                wait(dve, s_o, G * (b - 1))
                nc.vector.tensor_tensor(v[:, i, :], pV[:, 0:D], bv[:], ALU.add).then_inc(s_vs, 1)

            def keys(b, i):
                dve.wait_ge(s_k, b + 1)
                nc.vector.tensor_tensor(kT[:, i, :, :], pQK[:].rearrange("p (t s) -> p t s", t=TILES),
                                        bk[:].unsqueeze(2).to_broadcast([P, TILES, S]), ALU.add).then_inc(s_ks, 1)

            def largest(g):
                def f(b, i):
                    dve.wait_ge(s_scores, G * b + g + 1)
                    if g == 0:
                        wait(dve, s_prob, G * (b - 1))
                    nc.vector.tensor_reduce(negmax[:, i, TILES * g:TILES * g + TILES], pS[g % 2][:].rearrange("p (t s) -> p t s", t=TILES),
                                            AX.X, ALU.max, negate=True).then_inc(s_max, 1)
                return 1, f

            def turned(g):
                def f(b, i):
                    dve.wait_ge(s_pT, G * b + g + 1)
                    wait(dve, s_o, G * b + g - 1)
                    nc.vector.tensor_copy(probT[:, g % 2, :], pP[:]).then_inc(s_pTs, 1)
                return 1, f

            def divide(b, i):
                dve.wait_ge(s_prob, G * b + G)
                nc.vector.reciprocal(rinv[:], rowsum[:, i, :]).then_inc(s_rinv, 1)
                dve.wait_ge(s_rinv, b + 1)
                dve.wait_ge(s_o, G * b + G)
                wait(dve, s_oT, b)
                nc.vector.tensor_tensor(o[:].rearrange("p (h d) -> p h d", h=H), pO[:, 0:D].rearrange("p (h d) -> p h d", h=H),
                                        rinv[:].unsqueeze(2).to_broadcast([P, H, DK]), ALU.mult).then_inc(s_on, 1)

            def residual(b, i):
                dve.wait_ge(s_y, b + 1)
                dve.wait_ge(s_xbo, b + 1)
                nc.vector.tensor_tensor(y[:, i, :], pY[:, 0:D], xbo[:, i, :], ALU.add).then_inc(s_ys, 1)

            def norm(b, i):
                wait(dve, s_stored[i], landed(b - 2, i))
                ln.result(dve, y[:, i, :], xo[:, i, :], b)

            def statistics(b, i):
                dve.wait_ge(s_ys, b + 1)
                ln.statistics(dve, y[:, i, :], b)

            pipeline(dve, [(2, divide), largest(0), (3, norm), largest(1), turned(0), largest(2), (0, queries), turned(1), (0, context_values), largest(3),
                           turned(2), turned(3), (2, residual), (0, keys), (2, statistics)])


INNER = 1024
IC = INNER // P
QMAX = 127.0


def ternary_ffn_0_early(w):
    tensors = [(n, [P, 2 * INNER // cols, cols], F32, chunks(w[f"L0_ffn_w_{n}T"])) for n, cols in (("gate", INNER), ("up", INNER), ("down", D))]
    return tensors + [("ident", [P, P], BF16, w["ident_bf16"])]


def ternary_ffn_0(nc, x_in, x_out, w, rows, early, prefetch=()):
    with ExitStack() as ctx:
        ph = Phase(nc, ctx, "ff0")
        gate, up, down, ident = early.get("gate up down ident")
        raw = [t[:].rearrange("p c n -> p (c n)") for t in (gate, up, down)]
        tern = [ph.sb(f"tern{n}", [P, 2 * INNER], BF16) for n in range(3)]
        wg = tern[0][:].rearrange("p (c n) -> p c n", c=KC)
        wu = tern[1][:].rearrange("p (c n) -> p c n", c=KC)
        wd = tern[2][:].rearrange("p (c n) -> p c n", c=IC)
        ones = ph.sb("ones", [P, P])
        sums, mean, wscale = ph.sb("sums", [P, 3]), ph.sb("mean", [P, 3]), ph.sb("wscale", [P, 3])
        x, x_again, amax = ph.sb("x", [P, 2, D]), ph.sb("x_again", [P, 2, D]), ph.sb("amax", [P, 2])
        rx, step = ph.sb("rx", [P, 1]), ph.sb("step", [P, 2, 3])
        xr, xq, xqT = ph.sb("xr", [P, D]), ph.sb("xq", [P, 2, D], BF16), ph.sb("xqT", [P, KC, P], BF16)
        g, h, hr = ph.sb("g", [P, INNER]), ph.sb("h", [P, INNER]), ph.sb("hr", [P, INNER])
        hamax, hclip, sh, hstep = (ph.sb(n, [P, c]) for n, c in (("hamax", 1), ("hclip", 1), ("sh", 1), ("hstep", 2)))
        hq, hqT = ph.sb("hq", [P, INNER], BF16), ph.sb("hqT", [P, INNER], BF16)
        y, xo = ph.sb("y", [P, 2, D]), ph.sb("xo", [P, 2, D])
        zeros, s_zeros, s_cleared = ph.sb("zeros", [P, CLEAR * D]), ph.sem("zeros"), ph.sem("cleared")
        ln = LayerNorm(ph)
        pX, pH = ph.bank("pX", BF16), ph.bank("pH", BF16)
        pG, pU, pY = [ph.bank(f"pG{n}") for n in range(2)], [ph.bank(f"pU{n}") for n in range(2)], ph.bank("pY")
        s_ones, s_sum, s_tot, s_mean, s_tern, s_tern_down = (ph.sem(n) for n in ("ones", "sum", "tot", "mean", "tern", "tern_down"))
        s_x, s_x_again, s_stored = ph.sems("x"), ph.sems("x_again"), ph.sems("stored")
        s_amax, s_xq, s_xT, s_xTs = ph.sem("amax"), ph.sem("xq"), ph.sem("xT"), ph.sem("xTs")
        s_gate, s_up, s_g, s_h = ph.sem("gate"), ph.sem("up"), ph.sem("g"), ph.sem("h")
        s_hmax, s_hr, s_hq, s_hT, s_hTs = ph.sem("hmax"), ph.sem("hr"), ph.sem("hq"), ph.sem("hT"), ph.sem("hTs")
        s_y, s_ys = ph.sem("y"), ph.sem("ys")
        NH = INNER // BANK
        block = ctx.enter_context(nc.Block())

        @block.sync
        def _(sp):
            def load(b, i):
                wait(sp, s_xq, 2 * (b - 1))
                sp.dma_start(x[:, i, :], tokens(x_in, b)).then_inc(s_x[i], 16)
                sp.dma_start(rows[bass.ds(b * CLEAR * P, CLEAR * P), :].rearrange("(p a) d -> p (a d)", p=P), zeros[:]).then_inc(s_cleared, 16)

            def load_again(b, i):
                wait(sp, s_ys, b - 1)
                sp.dma_start(x_again[:, i, :], tokens(x_in, b)).then_inc(s_x_again[i], 16)

            sp.wait_ge(s_zeros, 1)
            pipeline(sp, [(0, load), (1, load_again)])
            for tensors in prefetch:
                tensors.load(sp)
            sp.wait_ge(s_cleared, 16 * B)

        @block.gpsimd
        def _(pool):
            ln.constants(pool)
            nc.gpsimd.memset(ones[:], 1.0).then_inc(s_ones, 1)
            nc.gpsimd.memset(zeros[:], 0.0).then_inc(s_zeros, 1)
            pool.wait_ge(s_mean, 2)
            nc.gpsimd.tensor_scalar(raw[2], raw[2], wscale[:, 2:3], MAGIC, ALU.mult, ALU.add).then_inc(s_tern_down, 1)
            pool.wait_ge(s_tern_down, 1)
            nc.gpsimd.tensor_scalar(raw[2], raw[2], MAGIC, 1.0, ALU.subtract, ALU.min).then_inc(s_tern_down, 1)
            pool.wait_ge(s_tern_down, 2)
            nc.gpsimd.tensor_scalar(tern[2][:], raw[2], -1.0, None, ALU.max).then_inc(s_tern_down, 1)
            pipeline(pool, [(3, lambda b, i: ln.power(pool, b))])

        @block.tensor
        def _(pe):
            pe.wait_ge(s_ones, 1)
            early.wait(pe)
            pe.wait_ge(s_sum, 3)
            nc.tensor.matmul(pY[:, 0:3], ones[:], sums[:], start=True, stop=True).then_inc(s_tot, 1)
            pe.wait_ge(s_tern, 6)

            def turn_x(b, i):
                pe.wait_ge(s_xq, 2 * b + 2)
                wait(pe, s_xTs, b)
                for k in range(KC):
                    t = nc.tensor.transpose(pX[:, k * P:(k + 1) * P], xq[:, i, k * P:(k + 1) * P], ident[:])
                t.then_inc(s_xT, 1)

            def gate_up(b, i):
                pe.wait_ge(s_xTs, b + 1)
                for weights, banks, free, done in ((wg, pG, s_g, s_gate), (wu, pU, s_h, s_up)):
                    wait(pe, free, NH * b if free is s_g else b)
                    for n in range(NH):
                        for k in range(KC):
                            mm = nc.tensor.matmul(banks[n][:], xqT[:, k, :], weights[:, k, n * BANK:(n + 1) * BANK], start=k == 0, stop=k == KC - 1)
                    mm.then_inc(done, 1)

            def turn_h(b, i):
                pe.wait_ge(s_hq, b + 1)
                wait(pe, s_hTs, b)
                for k in range(IC):
                    t = nc.tensor.transpose(pH[:, k * P:(k + 1) * P], hq[:, k * P:(k + 1) * P], ident[:])
                t.then_inc(s_hT, 1)

            def down(b, i):
                pe.wait_ge(s_hTs, b + 1)
                pe.wait_ge(s_tern_down, 3)
                wait(pe, s_ys, b)
                for k in range(IC):
                    mm = nc.tensor.matmul(pY[:, 0:D], hqT[:, k * P:(k + 1) * P], wd[:, k, :], start=k == 0, stop=k == IC - 1)
                mm.then_inc(s_y, 1)

            pipeline(pe, [(1, turn_x), (3, down), (1, gate_up), (2, turn_h)])

        @block.scalar
        def _(act):
            def turned(b, i):
                act.wait_ge(s_xT, b + 1)
                wait(act, s_up, b)
                nc.scalar.activation(xqT[:].rearrange("p a b -> p (a b)"), pX[:, 0:D], ACT.Copy).then_inc(s_xTs, 1)

            def gated(b, i):
                act.wait_ge(s_gate, b + 1)
                wait(act, s_h, b)
                for n in range(NH):
                    nc.scalar.activation(g[:, n * BANK:(n + 1) * BANK], pG[n][:], ACT.Silu, scale=step[:, i, 0:1]).then_inc(s_g, 1)

            def round_h(b, i):
                act.wait_ge(s_hmax, 4 * b + 4)
                nc.scalar.activation(hr[:], h[:], ACT.Copy, bias=MAGIC, scale=sh[:]).then_inc(s_hr, 1)

            def turned_h(b, i):
                act.wait_ge(s_hT, b + 1)
                wait(act, s_y, b)
                nc.scalar.activation(hqT[:], pH[:], ACT.Copy).then_inc(s_hTs, 1)

            def store(b, i):
                act.wait_ge(ln.s_done, b + 1)
                act.dma_start(tokens(x_out, b), xo[:, i, :]).then_inc(s_stored[i], 16)

            pipeline(act, [(1, turned), (2, round_h), (1, gated), (2, turned_h), (4, store)])
            for i in range(2):
                act.wait_ge(s_stored[i], 16 * B // 2)

        @block.vector
        def _(dve):
            early.wait(dve)
            for n in range(3):
                nc.vector.tensor_reduce(sums[:, n:n + 1], raw[n], AX.X, ALU.add, apply_absolute_value=True).then_inc(s_sum, 1)
            dve.wait_ge(s_tot, 1)
            nc.vector.tensor_scalar(mean[:], pY[:, 0:3], 1.0 / (D * INNER), 1e-5, ALU.mult, ALU.max).then_inc(s_mean, 1)
            dve.wait_ge(s_mean, 1)
            nc.vector.reciprocal(wscale[:], mean[:]).then_inc(s_mean, 1)
            dve.wait_ge(s_mean, 2)
            for n in range(2):
                nc.vector.tensor_scalar(raw[n], raw[n], wscale[:, n:n + 1], MAGIC, ALU.mult, ALU.add).then_inc(s_tern, 1)
                dve.wait_ge(s_tern, 3 * n + 1)
                nc.vector.tensor_scalar(raw[n], raw[n], MAGIC, 1.0, ALU.subtract, ALU.min).then_inc(s_tern, 1)
                dve.wait_ge(s_tern, 3 * n + 2)
                nc.vector.tensor_scalar(tern[n][:], raw[n], -1.0, None, ALU.max).then_inc(s_tern, 1)

            def quantise(b, i):
                dve.wait_ge(s_x[i], landed(b, i))
                nc.vector.tensor_reduce(amax[:, 0:1], x[:, i, :], AX.X, ALU.max, apply_absolute_value=True).then_inc(s_amax, 1)
                dve.wait_ge(s_amax, 4 * b + 1)
                nc.vector.tensor_scalar(amax[:, 1:2], amax[:, 0:1], 1e-5, 1.0 / QMAX, ALU.max, ALU.mult).then_inc(s_amax, 1)
                dve.wait_ge(s_amax, 4 * b + 2)
                nc.vector.reciprocal(rx[:], amax[:, 1:2]).then_inc(s_amax, 1)
                wait(dve, s_g, NH * (b - 1))
                nc.vector.tensor_scalar(step[:, i, :], mean[:], amax[:, 1:2], None, ALU.mult).then_inc(s_amax, 1)
                dve.wait_ge(s_amax, 4 * b + 4)
                nc.vector.tensor_scalar(xr[:], x[:, i, :], rx[:], MAGIC, ALU.mult, ALU.add).then_inc(s_xq, 1)
                dve.wait_ge(s_xq, 2 * b + 1)
                wait(dve, s_xT, b - 1)
                nc.vector.tensor_scalar(xq[:, i, :], xr[:], MAGIC, None, ALU.subtract).then_inc(s_xq, 1)

            def product(b, i):
                dve.wait_ge(s_g, NH * b + NH)
                dve.wait_ge(s_up, b + 1)
                wait(dve, s_hr, b)
                for n in range(NH):
                    c = slice(n * BANK, (n + 1) * BANK)
                    u = nc.vector.scalar_tensor_tensor(h[:, c], pU[n][:], step[:, i, 1:2], g[:, c], ALU.mult, ALU.mult)
                u.then_inc(s_h, 1)

            def scale_of_h(b, i):
                dve.wait_ge(s_h, b + 1)
                nc.vector.tensor_reduce(hamax[:], h[:], AX.X, ALU.max, apply_absolute_value=True).then_inc(s_hmax, 1)
                dve.wait_ge(s_hmax, 4 * b + 1)
                nc.vector.tensor_scalar(hclip[:], hamax[:], 1e-5, 1.0 / QMAX, ALU.max, ALU.mult).then_inc(s_hmax, 1)
                dve.wait_ge(s_hmax, 4 * b + 2)
                nc.vector.tensor_scalar(hstep[:, i:i + 1], hclip[:], mean[:, 2:3], None, ALU.mult).then_inc(s_hmax, 1)
                nc.vector.reciprocal(sh[:], hclip[:]).then_inc(s_hmax, 1)

            def whole_h(b, i):
                dve.wait_ge(s_hr, b + 1)
                wait(dve, s_hT, b)
                nc.vector.tensor_scalar(hq[:], hr[:], MAGIC, None, ALU.subtract).then_inc(s_hq, 1)

            def residual(b, i):
                dve.wait_ge(s_y, b + 1)
                dve.wait_ge(s_hmax, 4 * b + 3)
                dve.wait_ge(s_x_again[i], landed(b, i))
                nc.vector.scalar_tensor_tensor(y[:, i, :], pY[:, 0:D], hstep[:, i:i + 1], x_again[:, i, :], ALU.mult, ALU.add).then_inc(s_ys, 1)
                dve.wait_ge(s_ys, b + 1)
                ln.statistics(dve, y[:, i, :], b)

            def norm(b, i):
                wait(dve, s_stored[i], landed(b - 2, i))
                ln.result(dve, y[:, i, :], xo[:, i, :], b)

            pipeline(dve, [(4, norm), (2, scale_of_h), (0, quantise), (2, whole_h), (3, residual), (1, product)])


RMS_EPS = 1e-6


def linear_attention_1_early(w):
    g = lambda n: w["L1_attn_" + n]
    in_tiles = lambda m: m.rearrange("(c p) (t m) -> p c t m", p=P, t=TILES)
    return [
        ("ident", [P, P], F32, w["ident"]), ("identb", [P, P], BF16, w["ident_bf16"]), ("upto", [P, P], F32, w["upto"]), ("future", [P, P], BF16, w["future_bf16"]),
        ("wq", [P, KC, TILES, P], F32, in_tiles(g("WqT_slots"))), ("wk", [P, KC, TILES, P], F32, in_tiles(g("WkT_slots"))),
        ("wvf", [P, KC, D + H], F32, chunks(g("WvfT"))), ("wo", [P, KC, D], F32, chunks(g("WoT"))),
        ("delta", [P, H], F32, to_all(g("delta"))), ("weight", [P, D], F32, to_all(g("norm_weight"))),
    ]


def linear_attention_1(nc, x_in, x_out, w, early, prefetch=()):
    with ExitStack() as ctx:
        ph = Phase(nc, ctx, "la1")
        ident, identb, upto, future, wq, wk, wvf, wo, delta, weight = early.get("ident identb upto future wq wk wvf wo delta weight")
        x, xr = ph.sb("x", [P, 2, D]), ph.sb("xr", [P, 2, D])
        xT = ph.sb("xT", [P, KC, P])
        qT, kT, v = ph.sb("qT", [P, 2, BANK]), ph.sb("kT", [P, 2, BANK]), ph.sb("v", [P, 2, D])
        z, az, ez, lz = ph.sb("z", [P, H]), ph.sb("az", [P, H]), ph.sb("ez", [P, H]), ph.sb("lz", [P, H])
        logf, negl = ph.sb("logf", [P, 2, H]), ph.sb("negl", [P, 2, H])
        decay, weighted = ph.sb("decay", [P, 2, BANK]), ph.sb("weighted", [P, 2, BANK])
        square, ssum, ms, rms = ph.sb("square", [P, D]), ph.sb("ssum", [P, 1]), ph.sb("ms", [P, 1]), ph.sb("rms", [P, 1])
        o, oT = ph.sb("o", [P, D]), ph.sb("oT", [P, KC, P])
        y, xo = ph.sb("y", [P, 2, D]), ph.sb("xo", [P, 2, D])
        ln = LayerNorm(ph)
        pT, pQ, pK, pV = ph.bank("pT"), ph.bank("pQ"), ph.bank("pK"), ph.bank("pV")
        pD, pA, pO, pY = ph.bank("pD"), ph.bank("pA"), ph.bank("pO"), ph.bank("pY")
        s_x, s_stored = ph.sems("x"), ph.sems("stored")
        s_xr, s_turned, s_xT = ph.sems("xr"), ph.sem("turned"), ph.sem("xTs")
        s_q, s_k, s_v = ph.sem("q"), ph.sem("k"), ph.sem("v")
        s_qs, s_ks, s_vs = ph.sem("qs"), ph.sem("ks"), ph.sem("vs")
        s_z, s_ez, s_logf, s_l, s_negl = ph.sem("z"), ph.sem("ez"), ph.sem("logf"), ph.sem("l"), ph.sem("negl")
        s_diff, s_decay, s_a, s_aw, s_o = ph.sem("diff"), ph.sem("decay"), ph.sem("a"), ph.sem("aw"), ph.sem("o")
        s_ssum, s_ms, s_rms = ph.sem("ssum"), ph.sem("ms"), ph.sem("rms")
        s_on, s_oT, s_oTs, s_y, s_ys = (ph.sem(n) for n in ("on", "oT", "oTs", "y", "ys"))
        G = SLOTS
        L0 = D + H
        block = ctx.enter_context(nc.Block())

        @block.sync
        def _(sp):
            def load(b, i):
                wait(sp, s_turned, b - 1)
                sp.dma_start(x[:, i, :], tokens(x_in, b)).then_inc(s_x[i], 16)

            def load_again(b, i):
                wait(sp, s_ys, b - 1)
                sp.dma_start(xr[:, i, :], tokens(x_in, b)).then_inc(s_xr[i], 16)

            pipeline(sp, [(0, load), (1, load_again)])
            for tensors in prefetch:
                tensors.load(sp)

        @block.gpsimd
        def _(pool):
            ln.constants(pool)

            def rms_power(b, i):
                pool.wait_ge(s_ms, b + 1)
                wait(pool, s_on, b)
                nc.gpsimd.tensor_tensor(rms[:], ms[:], ln.half[:], ALU.pow).then_inc(s_rms, 1)

            pipeline(pool, [(2, lambda b, i: ln.power(pool, b)), (1, rms_power)])

        @block.tensor
        def _(pe):
            early.wait(pe)

            def turn_x(b, i):
                pe.wait_ge(s_x[i], landed(b, i))
                wait(pe, s_oTs, b - 1)
                for k in range(KC):
                    t = nc.tensor.transpose(pT[:, k * P:(k + 1) * P], x[:, i, k * P:(k + 1) * P], ident[:])
                t.then_inc(s_turned, 1)

            def values_and_gates(b, i):
                pe.wait_ge(s_xT, b + 1)
                wait(pe, s_vs, b)
                wait(pe, s_z, 2 * b)
                wait(pe, s_negl, b)
                for k in range(KC):
                    mm = nc.tensor.matmul(pV[:, 0:L0], xT[:, k, :], wvf[:, k, :], start=k == 0, stop=k == KC - 1)
                mm.then_inc(s_v, 1)

            def project(bank, weights, free, done):
                def f(b, i):
                    wait(pe, free, b)
                    for t in range(TILES):
                        for k in range(KC):
                            mm = nc.tensor.matmul(bank[:, t * P:(t + 1) * P], weights[:, k, t, :], xT[:, k, :], start=k == 0, stop=k == KC - 1)
                    mm.then_inc(done, 1)
                return 0, f

            def running_sum(b, i):
                pe.wait_ge(s_logf, b + 1)
                pe.wait_ge(s_vs, b + 1)
                nc.tensor.matmul(pV[:, L0:L0 + H], upto[:], logf[:, i, :], start=True, stop=True).then_inc(s_l, 1)

            def products(g):
                def f(b, i):
                    wait(pe, s_decay, G * b + g)
                    nc.tensor.matmul(pD[:].rearrange("p (t s) -> p t s", t=TILES), identb[:], future[:].unsqueeze(1).to_broadcast([P, TILES, S]),
                                     start=True, stop=False, skip_group_check=True)
                    for t in range(TILES):
                        h = TILES * g + t
                        mm = nc.tensor.matmul(pD[:, t * P:(t + 1) * P], logf[:, i, h:h + 1].to_broadcast([P, P]), upto[:],
                                              start=False, stop=t == TILES - 1, skip_group_check=True)
                    mm.then_inc(s_diff, 1)
                    pe.wait_ge(s_qs, b + 1)
                    pe.wait_ge(s_ks, b + 1)
                    wait(pe, s_aw, G * b + g)
                    r = slice(32 * g, 32 * g + DK)
                    for t in range(TILES):
                        mm = nc.tensor.matmul(pA[:, t * P:(t + 1) * P], kT[r, i, t * P:(t + 1) * P], qT[r, i, t * P:(t + 1) * P], start=True, stop=True)
                    mm.then_inc(s_a, 1)
                return 1, f

            def values(g):
                def f(b, i):
                    pe.wait_ge(s_aw, G * b + g + 1)
                    if g == 0:
                        wait(pe, s_on, b)
                        wait(pe, s_ssum, b)
                    for t in range(TILES):
                        h = TILES * g + t
                        mm = nc.tensor.matmul(pO[:, h * DK:(h + 1) * DK], weighted[:, g % 2, t * P:(t + 1) * P],
                                              v[:, i, h * DK:(h + 1) * DK], start=True, stop=True)
                    mm.then_inc(s_o, 1)
                return 1, f

            def turn_output(b, i):
                pe.wait_ge(s_on, b + 1)
                pe.wait_ge(s_xT, lagged(b, 2))
                for k in range(KC):
                    mm = nc.tensor.transpose(pT[:, k * P:(k + 1) * P], o[:, k * P:(k + 1) * P], ident[:])
                mm.then_inc(s_oT, 1)

            def output(b, i):
                pe.wait_ge(s_oTs, b + 1)
                wait(pe, s_ys, b)
                for k in range(KC):
                    mm = nc.tensor.matmul(pY[:, 0:D], oT[:, k, :], wo[:, k, :], start=k == 0, stop=k == KC - 1)
                mm.then_inc(s_y, 1)

            pipeline(pe, [products(0), (2, turn_output), products(1), (0, turn_x), values(0), (0, values_and_gates), project(pQ, wq, s_qs, s_q), products(2),
                          products(3), project(pK, wk, s_ks, s_k), values(1), (2, output), values(2), values(3), (0, running_sum)])

        @block.scalar
        def _(act):
            def turned(b, i):
                act.wait_ge(s_turned, b + 1)
                wait(act, s_k, b)
                nc.scalar.activation(xT[:].rearrange("p a b -> p (a b)"), pT[:, 0:D], ACT.Copy).then_inc(s_xT, 1)

            def silu(b, i):
                act.wait_ge(s_q, b + 1)
                wait(act, s_a, G * (b - 1))
                nc.scalar.activation(qT[:, i, :], pQ[:], ACT.Silu).then_inc(s_qs, 1)
                act.wait_ge(s_k, b + 1)
                nc.scalar.activation(kT[:, i, :], pK[:], ACT.Silu).then_inc(s_ks, 1)

            def gate_exp(b, i):
                act.wait_ge(s_z, 2 * b + 2)
                nc.scalar.activation(ez[:], az[:], ACT.Exp, scale=-1.0).then_inc(s_ez, 1)

            def gate_log(b, i):
                act.wait_ge(s_ez, 2 * b + 1)
                wait(act, s_logf, b)
                nc.scalar.activation(lz[:], ez[:], ACT.Ln, bias=1.0).then_inc(s_ez, 1)

            def decays(g):
                def f(b, i):
                    if g == 0:
                        act.wait_ge(s_negl, b + 1)
                    act.wait_ge(s_diff, G * b + g + 1)
                    wait(act, s_aw, G * b + g - 1)
                    for t in range(TILES):
                        h = TILES * g + t
                        e = nc.scalar.activation(decay[:, g % 2, t * P:(t + 1) * P], pD[:, t * P:(t + 1) * P], ACT.Exp, bias=negl[:, i, h:h + 1])
                    e.then_inc(s_decay, 1)
                return 1, f

            def squares(b, i):
                act.wait_ge(s_o, G * b + G)
                wait(act, s_ms, b)
                nc.scalar.activation(square[:], pO[:, 0:D], ACT.Square, accum_out=ssum[:]).then_inc(s_ssum, 1)

            def output(b, i):
                act.wait_ge(s_oT, b + 1)
                wait(act, s_y, b)
                nc.scalar.activation(oT[:].rearrange("p a b -> p (a b)"), pT[:, 0:D], ACT.Copy).then_inc(s_oTs, 1)

            def store(b, i):
                act.wait_ge(ln.s_done, b + 1)
                act.dma_start(tokens(x_out, b), xo[:, i, :]).then_inc(s_stored[i], 16)

            pipeline(act, [decays(0), (2, output), decays(1), (0, turned), (0, gate_exp), decays(2), decays(3), (0, gate_log), (1, squares), (0, silu), (3, store)])
            for i in range(2):
                act.wait_ge(s_stored[i], 16 * B // 2)

        @block.vector
        def _(dve):
            early.wait(dve)

            def gate(b, i):
                dve.wait_ge(s_v, b + 1)
                wait(dve, s_ez, 2 * b)
                nc.vector.tensor_tensor(z[:], pV[:, D:L0], delta[:], ALU.add).then_inc(s_z, 1)
                wait(dve, s_o, G * (b - 1))
                nc.vector.tensor_copy(v[:, i, :], pV[:, 0:D]).then_inc(s_vs, 1)
                dve.wait_ge(s_z, 2 * b + 1)
                nc.vector.scalar_tensor_tensor(az[:], z[:], -1.0, z[:], ALU.mult, ALU.max).then_inc(s_z, 1)

            def gate_log(b, i):
                dve.wait_ge(s_ez, 2 * b + 2)
                wait(dve, s_diff, G * (b - 1))
                nc.vector.scalar_tensor_tensor(logf[:, i, :], z[:], 0.0, lz[:], ALU.min, ALU.subtract).then_inc(s_logf, 1)

            def running_sum(b, i):
                dve.wait_ge(s_l, b + 1)
                wait(dve, s_decay, G * (b - 1))
                nc.vector.tensor_scalar(negl[:, i, :], pV[:, L0:L0 + H], -1.0, None, ALU.mult).then_inc(s_negl, 1)

            def weigh(g):
                def f(b, i):
                    dve.wait_ge(s_a, G * b + g + 1)
                    dve.wait_ge(s_decay, G * b + g + 1)
                    wait(dve, s_o, G * b + g - 1)
                    nc.vector.tensor_tensor(weighted[:, g % 2, :], pA[:], decay[:, g % 2, :], ALU.mult).then_inc(s_aw, 1)
                return 1, f

            def mean_square(b, i):
                dve.wait_ge(s_ssum, b + 1)
                wait(dve, s_rms, b)
                nc.vector.tensor_scalar(ms[:], ssum[:], 1.0 / D, RMS_EPS, ALU.mult, ALU.add).then_inc(s_ms, 1)

            def rms_norm(b, i):
                dve.wait_ge(s_rms, b + 1)
                wait(dve, s_oT, b)
                nc.vector.scalar_tensor_tensor(o[:], pO[:, 0:D], rms[:], weight[:], ALU.mult, ALU.mult).then_inc(s_on, 1)

            def residual(b, i):
                dve.wait_ge(s_y, b + 1)
                dve.wait_ge(s_xr[i], landed(b, i))
                nc.vector.tensor_tensor(y[:, i, :], pY[:, 0:D], xr[:, i, :], ALU.add).then_inc(s_ys, 1)
                dve.wait_ge(s_ys, b + 1)
                ln.statistics(dve, y[:, i, :], b)

            def norm(b, i):
                wait(dve, s_stored[i], landed(b - 2, i))
                ln.result(dve, y[:, i, :], xo[:, i, :], b)

            pipeline(dve, [weigh(0), (3, norm), (2, rms_norm), weigh(1), (0, gate), weigh(2), (0, gate_log), weigh(3), (2, residual), (0, running_sum),
                           (1, mean_square)])


C = 2 * D
F1 = 128
TAPS = 9
ROW3 = 129


def context_kernels_1_early(w):
    g = lambda n: w["L1_xattn_" + n]
    return [
        ("ident", [P, P], F32, w["ident"]), ("diag", [P, B, B], F32, w["diag"]),
        ("hw", [P, KC, C], F32, chunks(g("hist_W"))), ("hb", [P, C], F32, to_all(g("hist_b"))),
        ("hg", [P, C], F32, to_all(g("hist_ln_g"))), ("hbb", [P, C], F32, to_all(g("hist_ln_b"))),
        ("w1", [P, C // P, F1], F32, chunks(g("ctx_W1"))), ("b1", [P, 1], F32, g("ctx_b1").rearrange("(p o) -> p o", o=1)),
        ("w2", [P, 1], F32, g("ctx_W2")), ("b2", [B, 1], F32, to_all(g("ctx_b2"), B)),
        ("k1", [P, C // P, D], F32, chunks(g("kg_W1"))), ("kb1", [B, D], F32, to_all(g("kg_b1"), B)),
        ("kg", [B, D], F32, to_all(g("kg_ln_g"), B)), ("kb", [B, D], F32, to_all(g("kg_ln_b"), B)),
        ("k2", [P, KC, H * TAPS], F32, chunks(g("kg_W2"))), ("kb2", [B, H * TAPS], F32, to_all(g("kg_b2"), B)),
    ]


def context_kernels_1(nc, kernels, w, early, prefetch=()):
    with ExitStack() as ctx:
        ph = Phase(nc, ctx, "ck1")
        ident, diag, hw, hb, hg, hbb, w1, b1, w2, b2 = early.get("ident diag hw hb hg hbb w1 b1 w2 b2")
        k1, kb1, kg, kb, k2, kb2 = early.get("k1 kb1 kg kb k2 kb2")
        c, cT = ph.sb("c", [P, 2, D]), ph.sb("cT", [P, KC, P])
        e1, e2, e3 = ph.sb("e1", [P, C]), ph.sb("e2", [P, C]), ph.sb("e3", [P, C])
        e4 = ph.sb("e4", [P, C])
        ehs = ph.sb("ehs", [P, 2, C])
        eh, ehT, t1 = ph.sb("eh", [P, B, C]), ph.sb("ehT", [P, C // P, P]), ph.sb("t1", [P, P])
        score_row = ph.sb("score_row", [1, B * S])
        stats, mv, var, rstd, half, spare = (ph.sb(n, [P, k]) for n, k in (("stats", 6), ("mv", 2), ("var", 1), ("rstd", 1), ("half", 1), ("spare", 1)))
        sc, neg, ex, esum, er, aw = ph.sb("sc", [B, S]), ph.sb("neg", [B, 1]), ph.sb("ex", [B, S]), ph.sb("esum", [B, 1]), ph.sb("er", [B, 1]), ph.sb("aw", [B, S])
        awT, awd = ph.sb("awT", [P, B]), ph.sb("awd", [P, B, B])
        cc, ccT = ph.sb("cc", [B, C]), ph.sb("ccT", [P, C // P, B])
        u1, u2, u3, u4, uT = ph.sb("u1", [B, D]), ph.sb("u2", [B, D]), ph.sb("u3", [B, D]), ph.sb("u4", [B, D]), ph.sb("uT", [P, KC, B])
        kp, kmax, kd, ksum, kr, kout = ph.sb("kp", [B, H * TAPS]), ph.sb("kmax", [B, H]), ph.sb("kd", [B, H * TAPS]), ph.sb("ksum", [B, H]), ph.sb("kr", [B, H]), ph.sb("kout", [B, H * TAPS])
        pT, pE, pU, pH, pA = ph.bank("pT"), ph.bank("pE"), ph.bank("pU"), ph.bank("pH"), ph.bank("pA")
        s_kept = ph.sem("kept")
        s_half = ph.sem("half")
        s_c = ph.sems("c")
        s_turned, s_cT, s_e, s_stats, s_rstd, s_en, s_e4, s_eh = (ph.sem(n) for n in ("turned", "cT", "e", "stats", "rstd", "en", "e4", "eh"))
        s_ehT, s_ehTs, s_h, s_t1, s_a, s_row = (ph.sem(n) for n in ("ehT", "ehTs", "h", "t1", "a", "row"))
        s_sc, s_tail_v, s_tail_a, s_tail_p, s_tail_g, s_out = (ph.sem(n) for n in ("sc", "tail_v", "tail_a", "tail_p", "tail_g", "out"))
        block = ctx.enter_context(nc.Block())

        @block.sync
        def _(sp):
            def load(b, i):
                wait(sp, s_turned, b - 1)
                sp.dma_start(c[:, i, :], tokens(w["ctx_1024"], b)).then_inc(s_c[i], 16)

            pipeline(sp, [(0, load)])
            for tensors in prefetch:
                tensors.load(sp)
            sp.wait_ge(s_row, B)
            sp.dma_start(sc[:], score_row[:]).then_inc(s_sc, 16)
            sp.wait_ge(s_tail_v, 21)
            sp.dma_start(kernels, kout[:]).then_inc(s_out, 16)
            sp.wait_ge(s_out, 16)

        @block.gpsimd
        def _(pool):
            nc.gpsimd.memset(half[:], -0.5).then_inc(s_half, 1)
            pool.wait_ge(s_half, 1)
            early.wait(pool)

            def power(b, i):
                pool.wait_ge(s_stats, 4 * b + 4)
                wait(pool, s_en, 2 * b)
                nc.gpsimd.tensor_tensor(rstd[:], var[:], half[:], ALU.pow).then_inc(s_rstd, 1)

            def shift(b, i):
                pool.wait_ge(s_en, 2 * b + 2)
                wait(pool, s_eh, b)
                nc.gpsimd.tensor_tensor(e4[:], e3[:], hbb[:], ALU.add).then_inc(s_e4, 1)

            def keep(b, i):
                pool.wait_ge(s_eh, b + 1)
                nc.gpsimd.tensor_copy(eh[:, bass.ds(b, 1), :].rearrange("p o n -> p (o n)"), ehs[:, i, :]).then_inc(s_kept, 1)

            pipeline(pool, [(1, shift), (0, power), (2, keep)])
            pool.wait_ge(s_tail_v, 11)
            nc.gpsimd.tensor_tensor(rstd[0:B, :], var[0:B, :], half[0:B, :], ALU.pow).then_inc(s_tail_g, 1)

        @block.tensor
        def _(pe):
            early.wait(pe)

            def turn_context(b, i):
                pe.wait_ge(s_c[i], landed(b, i))
                wait(pe, s_cT, b)
                for k in range(KC):
                    t = nc.tensor.transpose(pT[:, k * P:(k + 1) * P], c[:, i, k * P:(k + 1) * P], ident[:])
                t.then_inc(s_turned, 1)

            def encode(b, i):
                pe.wait_ge(s_cT, b + 1)
                wait(pe, s_stats, 4 * b - 3)
                for k in range(KC):
                    mm = nc.tensor.matmul(pE[:], cT[:, k, :], hw[:, k, :], start=k == 0, stop=k == KC - 1)
                mm.then_inc(s_e, 1)

            def turn_encoded(b, i):
                pe.wait_ge(s_eh, b + 1)
                wait(pe, s_ehTs, b)
                for k in range(C // P):
                    t = nc.tensor.transpose(pU[:, k * P:(k + 1) * P], ehs[:, i, k * P:(k + 1) * P], ident[:])
                t.then_inc(s_ehT, 1)

            def hidden(b, i):
                pe.wait_ge(s_ehTs, b + 1)
                wait(pe, s_t1, b)
                for k in range(C // P):
                    mm = nc.tensor.matmul(pH[:, 0:P], w1[:, k, :], ehT[:, k, :], start=k == 0, stop=k == C // P - 1)
                mm.then_inc(s_h, 1)

            def score(b, i):
                pe.wait_ge(s_t1, b + 1)
                wait(pe, s_row, b)
                nc.tensor.matmul(pA[0:1, 0:P], w2[:], t1[:], start=True, stop=True).then_inc(s_a, 1)

            pipeline(pe, [(0, turn_context), (3, score), (2, turn_encoded), (0, encode), (2, hidden)])
            pe.wait_ge(s_tail_v, 3)
            nc.tensor.transpose(pT[:, 0:B], aw[:], ident[0:B, 0:B]).then_inc(s_tail_p, 1)
            pe.wait_ge(s_tail_v, 5)
            pe.wait_ge(s_kept, B)
            for b in range(B):
                mm = nc.tensor.matmul(pE[0:B, :], awd[:, b, :], eh[:, b, :], start=b == 0, stop=b == B - 1)
            mm.then_inc(s_tail_p, 1)
            pe.wait_ge(s_tail_v, 6)
            for k in range(C // P):
                t = nc.tensor.transpose(pT[:, k * B:(k + 1) * B], cc[:, k * P:(k + 1) * P], ident[0:B, 0:B])
            t.then_inc(s_tail_p, 1)
            pe.wait_ge(s_tail_v, 7)
            for k in range(C // P):
                mm = nc.tensor.matmul(pU[0:B, 0:D], ccT[:, k, :], k1[:, k, :], start=k == 0, stop=k == C // P - 1)
            mm.then_inc(s_tail_p, 1)
            pe.wait_ge(s_tail_a, 2)
            for k in range(KC):
                t = nc.tensor.transpose(pT[:, k * B:(k + 1) * B], u4[:, k * P:(k + 1) * P], ident[0:B, 0:B])
            t.then_inc(s_tail_p, 1)
            pe.wait_ge(s_tail_v, 15)
            for k in range(KC):
                mm = nc.tensor.matmul(pH[0:B, 0:H * TAPS], uT[:, k, :], k2[:, k, :], start=k == 0, stop=k == KC - 1)
            mm.then_inc(s_tail_p, 1)

        @block.scalar
        def _(act):
            early.wait(act)

            def turned_context(b, i):
                act.wait_ge(s_turned, b + 1)
                wait(act, s_e, b)
                nc.scalar.activation(cT[:].rearrange("p a b -> p (a b)"), pT[:, 0:D], ACT.Copy).then_inc(s_cT, 1)

            def encoded(b, i):
                act.wait_ge(s_e4, b + 1)
                wait(act, s_kept, b - 1)
                wait(act, s_ehT, b - 1)
                nc.scalar.activation(ehs[:, i, :], e4[:], ACT.Gelu).then_inc(s_eh, 1)

            def turned_encoded(b, i):
                act.wait_ge(s_ehT, b + 1)
                wait(act, s_h, b)
                nc.scalar.activation(ehT[:].rearrange("p a b -> p (a b)"), pU[:], ACT.Copy).then_inc(s_ehTs, 1)

            def hidden(b, i):
                act.wait_ge(s_h, b + 1)
                wait(act, s_a, b)
                nc.scalar.activation(t1[:], pH[:, 0:P], ACT.Gelu, bias=b1[:]).then_inc(s_t1, 1)

            def scored(b, i):
                act.wait_ge(s_a, b + 1)
                nc.scalar.activation(score_row[0:1, bass.ds(b * S, S)], pA[0:1, 0:P], ACT.Copy).then_inc(s_row, 1)

            pipeline(act, [(0, turned_context), (3, scored), (2, turned_encoded), (1, encoded), (2, hidden)])
            act.wait_ge(s_tail_v, 1)
            nc.scalar.activation(ex[:], sc[:], ACT.Exp, bias=neg[:], accum_out=esum[:]).then_inc(s_tail_a, 1)
            act.wait_ge(s_tail_v, 14)
            nc.scalar.activation(u4[:], u3[:], ACT.Gelu).then_inc(s_tail_a, 1)
            act.wait_ge(s_tail_v, 18)
            nc.scalar.activation(kp[:], kd[:], ACT.Exp).then_inc(s_tail_a, 1)

        @block.vector
        def _(dve):
            early.wait(dve)

            def encode(b, i):
                dve.wait_ge(s_e, b + 1)
                nc.vector.tensor_tensor(e1[:], pE[:], hb[:], ALU.add).then_inc(s_stats, 1)
                dve.wait_ge(s_stats, 4 * b + 1)
                nc.vector.bn_stats(stats[:], e1[:]).then_inc(s_stats, 1)
                dve.wait_ge(s_stats, 4 * b + 2)
                nc.vector.memset(spare[:], 0.0)
                nc.vector.bn_aggr(mv[:], stats[:]).then_inc(s_stats, 1)
                dve.wait_ge(s_stats, 4 * b + 3)
                wait(dve, s_rstd, b)
                nc.vector.tensor_scalar(var[:], mv[:, 1:2], LN_EPS, None, ALU.add).then_inc(s_stats, 1)

            def normed(b, i):
                dve.wait_ge(s_rstd, b + 1)
                nc.vector.tensor_scalar(e2[:], e1[:], mv[:, 0:1], rstd[:], ALU.subtract, ALU.mult).then_inc(s_en, 1)
                dve.wait_ge(s_en, 2 * b + 1)
                wait(dve, s_e4, b)
                nc.vector.tensor_tensor(e3[:], e2[:], hg[:], ALU.mult).then_inc(s_en, 1)

            pipeline(dve, [(1, normed), (0, encode)])
            tail = [0]

            def step(instruction):
                tail[0] += 1
                instruction.then_inc(s_tail_v, 1)
                dve.wait_ge(s_tail_v, tail[0])

            dve.wait_ge(s_sc, 16)
            nc.vector.tensor_scalar(sc[:], sc[:], b2[:], None, ALU.add).then_inc(s_half, 1)
            dve.wait_ge(s_half, 2)
            step(nc.vector.tensor_reduce(neg[:], sc[:], AX.X, ALU.max, negate=True))
            dve.wait_ge(s_tail_a, 1)
            step(nc.vector.reciprocal(er[:], esum[:]))
            step(nc.vector.tensor_scalar(aw[:], ex[:], er[:], None, ALU.mult))
            dve.wait_ge(s_tail_p, 1)
            step(nc.vector.tensor_copy(awT[:], pT[:, 0:B]))
            step(nc.vector.tensor_tensor(awd[:], diag[:], awT[:].unsqueeze(1).to_broadcast([P, B, B]), ALU.mult))
            dve.wait_ge(s_tail_p, 2)
            step(nc.vector.tensor_copy(cc[:], pE[0:B, :]))
            dve.wait_ge(s_tail_p, 3)
            step(nc.vector.tensor_copy(ccT[:].rearrange("p a b -> p (a b)"), pT[:, 0:C // P * B]))
            dve.wait_ge(s_tail_p, 4)
            step(nc.vector.tensor_tensor(u1[:], pU[0:B, 0:D], kb1[:], ALU.add))
            step(nc.vector.bn_stats(stats[0:B, :], u1[:]))
            step(nc.vector.bn_aggr(mv[0:B, :], stats[0:B, :]))
            step(nc.vector.tensor_scalar(var[0:B, :], mv[0:B, 1:2], LN_EPS, None, ALU.add))
            dve.wait_ge(s_tail_g, 1)
            step(nc.vector.tensor_scalar(u2[:], u1[:], mv[0:B, 0:1], rstd[0:B, :], ALU.subtract, ALU.mult))
            step(nc.vector.tensor_tensor(u1[:], u2[:], kg[:], ALU.mult))
            step(nc.vector.tensor_tensor(u3[:], u1[:], kb[:], ALU.add))
            dve.wait_ge(s_tail_p, 5)
            step(nc.vector.tensor_copy(uT[:].rearrange("p a b -> p (a b)"), pT[:, 0:KC * B]))
            dve.wait_ge(s_tail_p, 6)
            step(nc.vector.tensor_tensor(kout[:], pH[0:B, 0:H * TAPS], kb2[:], ALU.add))
            by_head = [t[:].rearrange("p (h t) -> p h t", h=H) for t in (kout, kd, kp)]
            step(nc.vector.tensor_reduce(kmax[:], by_head[0], AX.X, ALU.max))
            step(nc.vector.tensor_tensor(by_head[1], by_head[0], kmax[:].unsqueeze(2).to_broadcast([B, H, TAPS]), ALU.subtract))
            dve.wait_ge(s_tail_a, 3)
            step(nc.vector.tensor_reduce(ksum[:], by_head[2], AX.X, ALU.add))
            step(nc.vector.reciprocal(kr[:], ksum[:]))
            step(nc.vector.tensor_tensor(by_head[0], by_head[2], kr[:].unsqueeze(2).to_broadcast([B, H, TAPS]), ALU.mult))

def cross_attention_1_early(w):
    g = lambda n: w["L1_xattn_" + n]
    in_tiles = lambda m: m.rearrange("(c p) (t m) -> p c t m", p=P, t=TILES)
    return [
        ("ident", [P, P], F32, w["ident"]), ("identb", [P, P], BF16, w["ident_bf16"]), ("causal_u8", [P, P], U8, w["causal_u8"]),
        ("band", [P, ROW3], F32, w["band"]), ("tap_of", [1, TAPS, P], F32, w["tap_of"]),
        ("wq", [P, KC, TILES, P], F32, in_tiles(g("Wq_slots"))), ("wk", [P, KC, TILES, P], F32, in_tiles(g("Wk_slots"))),
        ("wv", [P, KC, D], F32, chunks(g("Wv"))), ("wo", [P, KC, D], F32, chunks(g("proj_W"))), ("bo", [P, D], F32, to_all(g("proj_b"))),
    ]


def cross_attention_1(nc, x_in, x_out, w, kernels, early, prefetch=()):
    with ExitStack() as ctx:
        ph = Phase(nc, ctx, "xa1")
        ident, identb, causal_u8, band, tap_of, wq, wk, wv, wo, bo = early.get("ident identb causal_u8 band tap_of wq wk wv wo bo")
        keep, minus, taps = ph.sb("keep", [P, P]), ph.sb("minus", [P, P], BF16), ph.sb("taps", [1, B * H, TAPS])
        x, xbo, xT = ph.sb("x", [P, 2, D]), ph.sb("xbo", [P, 2, D]), ph.sb("xT", [P, KC, P])
        qT, kT, v = ph.sb("qT", [P, 2, BANK]), ph.sb("kT", [P, 2, BANK]), ph.sb("v", [P, 2, D])
        mine = ph.sb("mine", [P, 2, H * 3, 3])
        bands = ph.sb("bands", [P, 2, TILES * 3, ROW3])
        kept = ph.sb("kept", [P, 2, TILES, S + 2])
        prob, probT = ph.sb("prob", [P, 2, BANK]), ph.sb("probT", [P, 2, BANK])
        negmax, rowsum, rinv = ph.sb("negmax", [P, 2, H]), ph.sb("rowsum", [P, 2, H]), ph.sb("rinv", [P, H])
        o, oT = ph.sb("o", [P, D]), ph.sb("oT", [P, KC, P])
        y, xo = ph.sb("y", [P, 2, D]), ph.sb("xo", [P, 2, D])
        ln = LayerNorm(ph)
        pT, pQK, pV = ph.bank("pT"), ph.bank("pQK"), ph.bank("pV")
        pA, pS, pP, pO = ph.bank("pA"), [ph.bank("pS0"), ph.bank("pS1")], ph.bank("pP"), ph.bank("pO")
        s_taps, s_const = ph.sem("taps"), ph.sem("const")
        s_x, s_stored = ph.sems("x"), ph.sems("stored")
        s_xbo, s_turned, s_xT = ph.sem("xbo"), ph.sem("turned"), ph.sem("xTs")
        s_q, s_k, s_v, s_tap = ph.sem("q"), ph.sem("k"), ph.sem("v"), ph.sem("tap")
        s_qs, s_ks, s_vs, s_mine = ph.sem("qs"), ph.sem("ks"), ph.sem("vs"), ph.sem("mine")
        s_bands, s_a, s_kept = ph.sem("bands"), ph.sem("a"), ph.sem("kept")
        s_scores, s_max, s_prob = ph.sem("scores"), ph.sem("max"), ph.sem("prob")
        s_pT, s_pTs, s_o = ph.sem("probT"), ph.sem("probTs"), ph.sem("o")
        s_rinv, s_on, s_oT, s_oTs, s_y, s_ys = (ph.sem(n) for n in ("rinv", "on", "oT", "oTs", "y", "ys"))
        G = SLOTS
        SCALE = float(DK) ** -0.5
        block = ctx.enter_context(nc.Block())

        @block.sync
        def _(sp):
            sp.dma_start(taps[:].rearrange("o a t -> o (a t)"), kernels.rearrange("b n -> (b n)").rearrange("(o n) -> o n", o=1)).then_inc(s_taps, 16)

            def load(b, i):
                wait(sp, s_xbo, b - 1)
                wait(sp, s_turned, b - 1)
                sp.dma_start(x[:, i, :], tokens(x_in, b)).then_inc(s_x[i], 16)

            pipeline(sp, [(0, load)])
            for tensors in prefetch:
                tensors.load(sp)

        @block.gpsimd
        def _(pool):
            ln.constants(pool)
            nc.gpsimd.memset(kept[:], 0.0).then_inc(s_const, 1)
            early.wait(pool)

            def add_bo(b, i):
                pool.wait_ge(s_x[i], landed(b, i))
                wait(pool, s_ys, b - 1)
                nc.gpsimd.tensor_tensor(xbo[:, i, :], x[:, i, :], bo[:], ALU.add).then_inc(s_xbo, 1)

            def build_bands(b, i):
                pool.wait_ge(s_mine, b + 1)
                for g in range(G):
                    wait(pool, s_scores, G * b + g - 1)
                    n = TILES * 3
                    nc.gpsimd.tensor_tensor(bands[:, g % 2, :, :].rearrange("p a (m r) -> p a m r", r=3),
                                            band[:].rearrange("p (m r) -> p m r", r=3).unsqueeze(1).to_broadcast([P, n, ROW3 // 3, 3]),
                                            mine[:, i, n * g:n * g + n, :].unsqueeze(2).to_broadcast([P, n, ROW3 // 3, 3]), ALU.mult).then_inc(s_bands, 1)

            pipeline(pool, [(1, build_bands), (0, add_bo), (2, lambda b, i: ln.power(pool, b))])

        @block.tensor
        def _(pe):
            early.wait(pe)
            pe.wait_ge(s_taps, 16)
            pe.wait_ge(s_const, 3)

            def turn_x(b, i):
                pe.wait_ge(s_x[i], landed(b, i))
                wait(pe, s_oTs, b - 1)
                for k in range(KC):
                    t = nc.tensor.transpose(pT[:, k * P:(k + 1) * P], x[:, i, k * P:(k + 1) * P], ident[:])
                t.then_inc(s_turned, 1)

            def queries(b, i):
                pe.wait_ge(s_xT, b + 1)
                wait(pe, s_mine, b)
                for t in range(TILES):
                    for k in range(KC):
                        mm = nc.tensor.matmul(pQK[:, t * P:(t + 1) * P], wq[:, k, t, :], xT[:, k, :], start=k == 0, stop=k == KC - 1)
                mm.then_inc(s_q, 1)

            def project_values(b, i):
                wait(pe, s_ys, b - 1)
                wait(pe, s_vs, b)
                for k in range(KC):
                    mm = nc.tensor.matmul(pV[:, 0:D], xT[:, k, :], wv[:, k, :], start=k == 0, stop=k == KC - 1)
                mm.then_inc(s_v, 1)

            def keys(b, i):
                pe.wait_ge(s_qs, b + 1)
                for t in range(TILES):
                    for k in range(KC):
                        mm = nc.tensor.matmul(pQK[:, t * P:(t + 1) * P], wk[:, k, t, :], xT[:, k, :], start=k == 0, stop=k == KC - 1)
                mm.then_inc(s_k, 1)

            def spread_taps(b, i):
                pe.wait_ge(s_ks, b + 1)
                mine_taps = taps[0:1, bass.ds(b * H, H), :].rearrange("o h (a c) -> o h a c", a=3)
                for r in range(3):
                    for a in range(3):
                        mm = nc.tensor.matmul(pQK[:, r * 48:(r + 1) * 48].rearrange("p (h c) -> p h c", h=H), tap_of[:, 3 * r + a, :],
                                              mine_taps[:, :, a, :], start=a == 0, stop=a == 2)
                mm.then_inc(s_tap, 1)

            def products(g):
                def f(b, i):
                    if g == 0:
                        pe.wait_ge(s_qs, b + 1)
                        pe.wait_ge(s_ks, b + 1)
                        pe.wait_ge(s_vs, b + 1)
                    wait(pe, s_kept, G * b + g)
                    r = slice(32 * g, 32 * g + DK)
                    for t in range(TILES):
                        mm = nc.tensor.matmul(pA[:, t * P:(t + 1) * P], qT[r, i, t * P:(t + 1) * P], kT[r, i, t * P:(t + 1) * P], start=True, stop=True)
                    mm.then_inc(s_a, 1)
                return 1, f

            def convolve(g):
                def f(b, i):
                    wait(pe, s_prob, G * b + g - 1)
                    nc.tensor.matmul(pS[g % 2][:].rearrange("p (t s) -> p t s", t=TILES), identb[:], minus[:].unsqueeze(1).to_broadcast([P, TILES, S]),
                                     start=True, stop=False, skip_group_check=True)
                    pe.wait_ge(s_kept, G * b + g + 1)
                    pe.wait_ge(s_bands, G * b + g + 1)
                    for t in range(TILES):
                        for c in range(3):
                            mm = nc.tensor.matmul(pS[g % 2][:, t * P:(t + 1) * P], bands[:, g % 2, 3 * t + c, 0:P], kept[:, g % 2, t, c:c + S],
                                                  start=False, stop=t == TILES - 1 and c == 2, skip_group_check=True)
                    mm.then_inc(s_scores, 1)
                return 1, f

            def turn(g):
                def f(b, i):
                    pe.wait_ge(s_prob, G * b + g + 1)
                    wait(pe, s_pTs, G * b + g)
                    for t in range(TILES):
                        mm = nc.tensor.transpose(pP[:, t * P:(t + 1) * P], prob[:, g % 2, t * P:(t + 1) * P], ident[:])
                    mm.then_inc(s_pT, 1)
                return 1, f

            def values(g):
                def f(b, i):
                    pe.wait_ge(s_pTs, G * b + g + 1)
                    if g == 0:
                        wait(pe, s_on, b)
                    for t in range(TILES):
                        h = TILES * g + t
                        mm = nc.tensor.matmul(pO[:, h * DK:(h + 1) * DK], probT[:, g % 2, t * P:(t + 1) * P],
                                              v[:, i, h * DK:(h + 1) * DK], start=True, stop=True)
                    mm.then_inc(s_o, 1)
                return 1, f

            def turn_output(b, i):
                pe.wait_ge(s_on, b + 1)
                pe.wait_ge(s_xT, lagged(b, 2))
                for k in range(KC):
                    mm = nc.tensor.transpose(pT[:, k * P:(k + 1) * P], o[:, k * P:(k + 1) * P], ident[:])
                mm.then_inc(s_oT, 1)

            def output(b, i):
                pe.wait_ge(s_oTs, b + 1)
                pe.wait_ge(s_vs, lagged(b, 2))
                for k in range(KC):
                    mm = nc.tensor.matmul(pV[:, 0:D], oT[:, k, :], wo[:, k, :], start=k == 0, stop=k == KC - 1)
                mm.then_inc(s_y, 1)

            pipeline(pe, [products(0), (2, turn_output), products(1), convolve(0), (0, turn_x), convolve(1), turn(0), (2, output), products(2), (0, queries),
                          convolve(2), products(3), values(0), turn(1), (0, project_values), convolve(3), values(1), turn(2), (0, keys), values(2), turn(3),
                          (0, spread_taps), values(3)])

        @block.scalar
        def _(act):
            def turned(b, i):
                act.wait_ge(s_turned, b + 1)
                wait(act, s_k, b)
                nc.scalar.activation(xT[:].rearrange("p a b -> p (a b)"), pT[:, 0:D], ACT.Copy).then_inc(s_xT, 1)

            def copy_taps(b, i):
                act.wait_ge(s_tap, b + 1)
                wait(act, s_bands, G * (b - 1))
                nc.scalar.activation(mine[:, i, :, :].rearrange("p n r -> p r n"), pQK[:, 0:144].rearrange("p (r n) -> p r n", r=3), ACT.Copy).then_inc(s_mine, 1)

            def softmax(g):
                def f(b, i):
                    act.wait_ge(s_max, G * b + g + 1)
                    wait(act, s_pT, G * b + g - 1)
                    if g == 0:
                        wait(act, s_rinv, b - 1)
                    for t in range(TILES):
                        h = TILES * g + t
                        e = nc.scalar.activation(prob[:, g % 2, t * P:(t + 1) * P], pS[g % 2][:, t * P:(t + 1) * P], ACT.Exp,
                                                 bias=negmax[:, i, h:h + 1], accum_out=rowsum[:, i, h:h + 1])
                    e.then_inc(s_prob, 1)
                return 1, f

            def output(b, i):
                act.wait_ge(s_oT, b + 1)
                wait(act, s_y, b)
                nc.scalar.activation(oT[:].rearrange("p a b -> p (a b)"), pT[:, 0:D], ACT.Copy).then_inc(s_oTs, 1)

            def store(b, i):
                act.wait_ge(ln.s_done, b + 1)
                act.dma_start(tokens(x_out, b), xo[:, i, :]).then_inc(s_stored[i], 16)

            pipeline(act, [(2, output), softmax(0), (0, turned), softmax(1), softmax(2), softmax(3), (0, copy_taps), (3, store)])
            for i in range(2):
                act.wait_ge(s_stored[i], 16 * B // 2)

        @block.vector
        def _(dve):
            early.wait(dve)
            nc.vector.tensor_scalar(keep[:], causal_u8[:], -1.0, 1.0, ALU.mult, ALU.add).then_inc(s_const, 1)
            nc.vector.tensor_scalar(minus[:], causal_u8[:], -1e30, None, ALU.mult).then_inc(s_const, 1)
            dve.wait_ge(s_const, 3)

            def queries(b, i):
                dve.wait_ge(s_q, b + 1)
                wait(dve, s_a, G * (b - 1))
                nc.vector.tensor_scalar(qT[:, i, :], pQK[:], SCALE, None, ALU.mult).then_inc(s_qs, 1)

            def copy_values(b, i):
                dve.wait_ge(s_v, b + 1)
                wait(dve, s_o, G * (b - 1))
                nc.vector.tensor_copy(v[:, i, :], pV[:, 0:D]).then_inc(s_vs, 1)

            def keys(b, i):
                dve.wait_ge(s_k, b + 1)
                nc.vector.tensor_copy(kT[:, i, :], pQK[:]).then_inc(s_ks, 1)

            def masked(g):
                def f(b, i):
                    dve.wait_ge(s_a, G * b + g + 1)
                    wait(dve, s_scores, G * b + g - 1)
                    nc.vector.tensor_tensor(kept[:, g % 2, :, 1:S + 1], pA[:].rearrange("p (t s) -> p t s", t=TILES),
                                            keep[:].unsqueeze(1).to_broadcast([P, TILES, S]), ALU.mult).then_inc(s_kept, 1)
                return 1, f

            def largest(g):
                def f(b, i):
                    dve.wait_ge(s_scores, G * b + g + 1)
                    if g == 0:
                        wait(dve, s_prob, G * (b - 1))
                    nc.vector.tensor_reduce(negmax[:, i, TILES * g:TILES * g + TILES], pS[g % 2][:].rearrange("p (t s) -> p t s", t=TILES),
                                            AX.X, ALU.max, negate=True).then_inc(s_max, 1)
                return 1, f

            def turned(g):
                def f(b, i):
                    dve.wait_ge(s_pT, G * b + g + 1)
                    wait(dve, s_o, G * b + g - 1)
                    nc.vector.tensor_copy(probT[:, g % 2, :], pP[:]).then_inc(s_pTs, 1)
                return 1, f

            def divide(b, i):
                dve.wait_ge(s_prob, G * b + G)
                nc.vector.reciprocal(rinv[:], rowsum[:, i, :]).then_inc(s_rinv, 1)
                dve.wait_ge(s_rinv, b + 1)
                dve.wait_ge(s_o, G * b + G)
                wait(dve, s_oT, b)
                nc.vector.tensor_tensor(o[:].rearrange("p (h d) -> p h d", h=H), pO[:, 0:D].rearrange("p (h d) -> p h d", h=H),
                                        rinv[:].unsqueeze(2).to_broadcast([P, H, DK]), ALU.mult).then_inc(s_on, 1)

            def residual(b, i):
                dve.wait_ge(s_y, b + 1)
                dve.wait_ge(s_xbo, b + 1)
                nc.vector.tensor_tensor(y[:, i, :], pV[:, 0:D], xbo[:, i, :], ALU.add).then_inc(s_ys, 1)
                dve.wait_ge(s_ys, b + 1)
                ln.statistics(dve, y[:, i, :], b)

            def norm(b, i):
                wait(dve, s_stored[i], landed(b - 2, i))
                ln.result(dve, y[:, i, :], xo[:, i, :], b)

            pipeline(dve, [(2, divide), masked(0), (3, norm), masked(1), largest(0), largest(1), (2, residual), masked(2), turned(0), (0, queries), largest(2),
                           masked(3), turned(1), (0, copy_values), largest(3), turned(2), (0, keys), turned(3)])


GROUPS, TOP_GROUPS = 8, 4
INTER = 128
SHARED = 2
ALL = E + SHARED
NB = B * S // BANK
TB = BANK // P
WG, WD = KC * 2 * INTER, D

RING = 8
DEEP = 4


def moe_ffn_1(nc, x_in, x_out, w, rows, results, places, experts):
    with ExitStack() as ctx:
        ph = Phase(nc, ctx, "moe")
        NT = TILES_OF_ROWS
        HT = NT // 2
        ident, gate_w, bias = ph.sb("ident", [P, P]), ph.sb("gate_w", [P, KC, E]), ph.sb("bias", [P, E])
        lower = ph.sb("lower", [P, GROUPS, GROUPS])
        upto, ones, tile_at = ph.sb("upto", [P, P], BF16), ph.sb("ones", [P, P], BF16), ph.sb("tile_at", [P, 2])
        acc, xT, xt = ph.sb("acc", [P, B, D]), ph.sb("xT", [P, KC, B * S]), ph.sb("xt", [P, DEEP, KC, P])
        x = ph.sb("x", [P, DEEP, D])
        ra, rb, rc, rd, re = (ph.sb(n, [P, B * E]) for n in ("ra", "rb", "rc", "rd", "re"))
        share, row_of = ph.sb("share", [P, B * E]), ph.sb("row_of", [P, B * E])
        chosen = ph.sb("chosen", [P, B * E], BF16)
        gmax, grank, gmask = (ph.sb(n, [P, B, GROUPS]) for n in ("gmax", "grank", "gmask"))
        top8, more, need, total, rtotal = (ph.sb(n, [P, B, c]) for n, c in (("top8", 8), ("more", 1), ("need", 1), ("total", 1), ("rtotal", 1)))
        wanted = ph.sb("wanted", [P, B, 1])
        row8, place, weight = ph.sb("row8", [P, B, 8]), ph.sb("place", [P, B, 8], U32), ph.sb("weight", [P, B, 8])
        na, nb, tiles, first = (ph.sb(n, [P, E]) for n in ("na", "nb", "tiles", "first"))
        before, of_tile, expert = ph.sb("before", [P, 2, E]), ph.sb("of_tile", [P, 2]), ph.sb("expert", [P, 2], U32)
        expert_row = ph.sb("expert_row", [1, NT], U32)
        xs, at = ph.sb("xs", [P, RING, D]), ph.sb("at", [P, RING, 8], U32)
        we = ph.sb("we", [P, RING, WG + WD])
        g, h = ph.sb("g", [P, 2, BANK]), ph.sb("h", [P, 2, BANK])
        xg, xgT, yg = ph.sb("xg", [P, RING, D]), ph.sb("xgT", [P, 2, KC, P]), ph.sb("yg", [P, RING, D])
        got, wcol = ph.sb("got", [P, DEEP, TOP_K, D]), ph.sb("wcol", [P, DEEP, 8])
        sums, xo = ph.sb("sums", [P, DEEP, D]), ph.sb("xo", [P, DEEP, D])
        spare = ph.sb("spare", [P, 1])
        ln = LayerNorm(ph)
        pG, pU, pD = ([ph.bank(f"{n}{i}") for i in range(c)] for n, c in (("pG", 2), ("pU", 2), ("pD", 4)))
        s_c, s_acc0, s_x, s_w, s_stored = ph.sem("constants"), ph.sem("acc0"), ph.sems("x", DEEP), ph.sems("shared"), ph.sems("stored", DEEP)
        s_turned, s_xt, s_xT, s_logits, s_exp = (ph.sem(n) for n in ("turned", "xt", "xT", "logits", "exp"))
        s_spare, s_ones, s_route, s_chosen, s_before, s_placed, s_out_places, s_row = (ph.sem(n) for n in ("spare", "ones", "route", "chosen", "before", "placed", "out_places", "row"))
        s_gate, s_up, s_g, s_h, s_down, s_acc = (ph.sem(n) for n in ("gate", "up", "g", "h", "down", "acc"))
        s_xs, s_spread = ph.sems("xs", RING), ph.sems("spread", RING)
        s_we, s_xg, s_kept = ph.sems("we", RING), ph.sems("xg", RING // 2), ph.sems("kept", RING // 2)
        s_xgt, s_xgT, s_gu, s_gate_t, s_ht, s_dt, s_yg = (ph.sem(n) for n in ("xgt", "xgT", "gu", "gate_t", "ht", "dt", "yg"))
        s_at, s_got, s_wcol, s_sum = ph.sems("at", DEEP), ph.sems("got", DEEP), ph.sem("wcol"), ph.sem("sum")
        block = ctx.enter_context(nc.Block())
        ROUTED = 129
        places_of = lambda b: places[bass.ds(b, 1)].rearrange("o p k -> (o p) k")
        tiles_of = lambda dram, t: dram[bass.ds(t * P, 2 * P), :].rearrange("(a p) d -> p a d", a=2)

        @block.sync
        def _(sp):
            for to, of in ((ident[:], w["ident"]), (gate_w[:], w["L1_ffn_gate_wT"].rearrange("(c p) n -> p c n", p=P)),
                           (bias[:], to_all(w["L1_ffn_gate_bias"])), (lower[:], w["moe_lower_group"]), (upto[:], w["upto_bf16"]),
                           (tile_at[:], w["moe_tile_number"])):
                sp.dma_start(to, of).then_inc(s_c, 16)

            def load_x(b, i):
                wait(sp, s_turned, b - DEEP + 1)
                sp.dma_start(x[:, i, :], tokens(x_in, b)).then_inc(s_x[i], 16)

            pipeline(sp, [(0, load_x)], body=DEEP)
            sp.dma_start(acc[:], x_in.rearrange("b p d -> p b d")).then_inc(s_acc0, 16)
            for n in range(SHARED):
                sp.dma_start(we[:, n, :], w["L1_ffn_experts"][E + n]).then_inc(s_w[n], 16)

            sp.wait_ge(s_placed, 2)
            sp.dma_start(places.rearrange("b p k -> p b k"), place[:]).then_inc(s_out_places, 16)
            for n in range(2):
                sp.dma_start(experts[n * HT:(n + 1) * HT].rearrange("(p o) -> p o", o=1), expert[0:HT, n:n + 1]).then_inc(s_out_places, 16)
            sp.wait_ge(s_out_places, 48)
            sp.dma_start(expert_row[:], experts.rearrange("(o n) -> o n", o=1)).then_inc(s_row, 16)

            def token_rows(b, i):
                wait(sp, s_spread[i], landed(b - RING, i, TOP_K, RING))
                sp.dma_start(xs[:, i, :], tokens(x_in, b)).then_inc(s_xs[i], 16)
                sp.dma_start(at[:, i, :], places_of(b)).then_inc(s_xs[i], 16)

            pipeline(sp, [(0, token_rows)], body=RING)
            sp.wait_ge(s_row, 16)
            sp.wait_ge(s_down, SHARED * NB)
            for i in range(RING):
                sp.wait_ge(s_spread[i], 16 * TOP_K * B // RING)

            def tile(t, i):
                e = sp.value_load(expert_row[0:1, bass.ds(t, 1)], min_val=0, max_val=E - 1)
                if i % 2 == 0:
                    wait(sp, s_xgt, t - RING + 2)
                    sp.dma_start(xg[:, i:i + 2, :], tiles_of(rows, t)).then_inc(s_xg[i // 2], 16)
                wait(sp, s_dt, t - RING + 1)
                sp.dma_start(we[:, i, :], w["L1_ffn_experts"][bass.ds(e, 1)].rearrange("o p n -> (o p) n")).then_inc(s_we[i], 16)

            pipeline(sp, [(0, tile)], n=NT, body=RING)

            def places_again(b, i):
                wait(sp, s_got[i], landed(b - DEEP, i, TOP_K, DEEP))
                sp.dma_start(at[:, i, :], places_of(b)).then_inc(s_at[i], 16)

            pipeline(sp, [(0, places_again)], body=DEEP)

        @block.gpsimd
        def _(pool):
            ln.constants(pool)
            nc.gpsimd.memset(ones[:], 1.0).then_inc(s_ones, 1)

            def take_waits(n):
                wait(pool, s_spare, n)
                nc.gpsimd.tensor_tensor(spare[:], ln.one[:], ln.one[:], ALU.mult).then_inc(s_spare, 1)

            def spread(b, i):
                pool.wait_ge(s_xs[i], landed(b, i, 2, RING))
                take_waits(b)
                for k in range(TOP_K):
                    pool.indirect_dma_start(rows, bass.IndirectOffsetOnAxis(ap=at[:, i, k:k + 1], axis=0), xs[:, i, :], None).then_inc(s_spread[i], 16)

            pipeline(pool, [(0, spread)], body=RING)
            for i in range(RING // 2):
                pool.wait_ge(s_kept[i], 16 * NT // RING)

            def gather(b, i):
                pool.wait_ge(s_at[i], landed(b, i, 1, DEEP))
                wait(pool, s_sum, TOP_K * (b - DEEP + 1))
                take_waits(B + b)
                for k in range(TOP_K):
                    pool.indirect_dma_start(got[:, i, k, :], None, results, bass.IndirectOffsetOnAxis(ap=at[:, i, k:k + 1], axis=0)).then_inc(s_got[i], 16)

            pipeline(pool, [(0, gather), (3, lambda b, i: ln.power(pool, b))], body=DEEP)

        @block.tensor
        def _(pe):
            pe.wait_ge(s_c, 6 * 16)

            def turn(b, i):
                pe.wait_ge(s_x[i], landed(b, i, 1, DEEP))
                wait(pe, s_xt, b - DEEP + 1)
                for k in range(KC):
                    t = nc.tensor.transpose(pD[i][:, k * P:(k + 1) * P], x[:, i, k * P:(k + 1) * P], ident[:])
                t.then_inc(s_turned, 1)

            def logits(b, i):
                pe.wait_ge(s_xt, b + 1)
                wait(pe, s_exp, b - DEEP + 1)
                for k in range(KC):
                    mm = nc.tensor.matmul((pG + pU)[i][:, 0:E], xt[:, i, k, :], gate_w[:, k, :], start=k == 0, stop=k == KC - 1)
                mm.then_inc(s_logits, 1)

            pipeline(pe, [(0, turn), (1, logits)], body=DEEP)
            pe.wait_ge(s_exp, B)
            pe.wait_ge(s_ones, 1)
            pe.wait_ge(s_chosen, 1)
            for n in range(2):
                c = slice(n * BANK, (n + 1) * BANK)
                nc.tensor.matmul(pG[n][:], upto[:], chosen[:, c], start=True, stop=True).then_inc(s_before, 1)
                nc.tensor.matmul(pU[n][:], ones[:], chosen[:, c], start=True, stop=True).then_inc(s_before, 1)
            pe.wait_ge(s_placed, 1)

            def gate_up(e, n):
                if n == 0:
                    pe.wait_ge(s_w[e], 16)
                u = NB * e + n
                for half, (bank, free, done) in enumerate(((pG[n % 2], s_g, s_gate), (pU[n % 2], s_h, s_up))):
                    wait(pe, free, u - 1)
                    for k in range(KC):
                        c = (2 * k + half) * INTER
                        mm = nc.tensor.matmul(bank[:], we[:, e, c:c + INTER], xT[:, k, n * BANK:(n + 1) * BANK], start=k == 0, stop=k == KC - 1)
                    mm.then_inc(done, 1)

            def down(e, n):
                u = NB * e + n
                pe.wait_ge(s_h, u + 1)
                wait(pe, s_acc, TB * (u - 1))
                for t in range(TB):
                    bank = pD[2 * (n % 2) + t // 2]
                    mm = nc.tensor.matmul(bank[:, (t % 2) * D:(t % 2 + 1) * D], h[:, n % 2, t * P:(t + 1) * P], we[:, e, WG:WG + WD], start=True, stop=True)
                mm.then_inc(s_down, 1)

            for u in range(SHARED * NB + 1):
                if u < SHARED * NB:
                    gate_up(u // NB, u % NB)
                if u > 0:
                    down((u - 1) // NB, (u - 1) % NB)
            pe.wait_ge(s_acc, SHARED * B)

            def turn_rows(t, i):
                pe.wait_ge(s_xg[i // 2], landed(t, i, 1, RING))
                wait(pe, s_xgT, t - 1)
                for k in range(KC):
                    m = nc.tensor.transpose(pG[i % 2][:, k * P:(k + 1) * P], xg[:, i, k * P:(k + 1) * P], ident[:])
                m.then_inc(s_xgt, 1)

            def rows_gate_up(t, i):
                pe.wait_ge(s_we[i], landed(t, i, 1, RING))
                pe.wait_ge(s_xgT, t + 1)
                wait(pe, s_ht, t - 1)
                for half in range(2):
                    for k in range(KC):
                        c = (2 * k + half) * INTER
                        m = nc.tensor.matmul(pU[i % 2][:, half * P:(half + 1) * P], we[:, i, c:c + INTER], xgT[:, i % 2, k, :], start=k == 0, stop=k == KC - 1)
                m.then_inc(s_gu, 1)

            def rows_down(t, i):
                pe.wait_ge(s_ht, t + 1)
                wait(pe, s_yg, t - 1)
                nc.tensor.matmul(pD[i % 2][:, 0:D], h[:, i % 2, 0:P], we[:, i, WG:WG + WD], start=True, stop=True).then_inc(s_dt, 1)

            pipeline(pe, [(3, rows_down), (0, turn_rows), (1, rows_gate_up)], n=NT, body=RING)

        @block.scalar
        def _(act):
            def turned(b, i):
                act.wait_ge(s_turned, b + 1)
                wait(act, s_logits, b - DEEP + 1)
                wait(act, s_xT, b - DEEP + 1)
                nc.scalar.activation(xt[:, i, :, :].rearrange("p c t -> p (c t)"), pD[i][:, 0:D], ACT.Copy).then_inc(s_xt, 1)

            def minus_exp(b, i):
                act.wait_ge(s_logits, b + 1)
                nc.scalar.activation(ra[:, bass.ds(b * E, E)], (pG + pU)[i][:, 0:E], ACT.Exp, scale=-1.0).then_inc(s_exp, 1)

            pipeline(act, [(0, turned), (1, minus_exp)], body=DEEP)
            for u in range(SHARED * NB):
                act.wait_ge(s_gate, u + 1)
                wait(act, s_h, u - 1)
                nc.scalar.activation(g[:, u % 2, :], pG[u % 2][:], ACT.Silu).then_inc(s_g, 1)
            act.wait_ge(s_h, SHARED * NB)

            def gated(t, i):
                act.wait_ge(s_gu, t + 1)
                wait(act, s_ht, t - 1)
                nc.scalar.activation(g[:, i % 2, 0:P], pU[i % 2][:, 0:P], ACT.Silu).then_inc(s_gate_t, 1)

            def results_out(t, i):
                act.wait_ge(s_dt, t + 1)
                wait(act, s_kept[i // 2], landed(t - RING, i, 1, RING))
                nc.scalar.activation(yg[:, i, :], pD[i % 2][:, 0:D], ACT.Copy).then_inc(s_yg, 1)
                if i % 2 == 1:
                    act.wait_ge(s_yg, t + 1)
                    act.dma_start(tiles_of(results, t - 1), yg[:, i - 1:i + 1, :]).then_inc(s_kept[i // 2], 16)

            pipeline(act, [(1, gated), (3, results_out)], n=NT, body=RING)

            def store(b, i):
                act.wait_ge(ln.s_done, b + 1)
                act.dma_start(tokens(x_out, b), xo[:, i, :]).then_inc(s_stored[i], 16)

            pipeline(act, [(0, store)], body=DEEP)
            for i in range(DEEP):
                act.wait_ge(s_stored[i], 16 * B // DEEP)

        @block.vector
        def _(dve):
            dve.wait_ge(s_c, 6 * 16)

            def turned(b, i):
                dve.wait_ge(s_xt, b + 1)
                nc.vector.tensor_copy(xT[:, :, bass.ds(b * S, S)], xt[:, i, :, :]).then_inc(s_xT, 1)

            pipeline(dve, [(0, turned)], body=DEEP)
            dve.wait_ge(s_exp, B)
            done = [0]

            def step(*instructions):
                for ins in instructions:
                    ins.then_inc(s_route, 1)
                done[0] += len(instructions)
                dve.wait_ge(s_route, done[0])

            def running(a, b, size, part):
                far = 1
                while far < size:
                    V.tensor_copy(part(b, 0, far), part(a, 0, far)).then_inc(s_route, 1)
                    done[0] += 1
                    step(V.tensor_tensor(part(b, far, size), part(a, far, size), part(a, 0, size - far), ALU.add))
                    a, b, far = b, a, 2 * far
                return a

            V = nc.vector
            per_expert = lambda t: t[:].rearrange("p (b e) -> p b e", e=E)
            per_group = lambda t: t[:].rearrange("p (q e) -> p q e", e=E // GROUPS)
            pairs = lambda t: t[:].rearrange("p (b g f) -> p b g f", b=B, g=GROUPS)
            step(V.tensor_scalar(ra[:], ra[:], 1.0, None, ALU.add))
            step(V.reciprocal(rb[:], ra[:]))
            step(V.tensor_tensor(per_expert(ra), per_expert(rb), bias[:].unsqueeze(1).to_broadcast([P, B, E]), ALU.add))
            step(V.tensor_reduce(gmax[:].rearrange("p b g -> p (b g)"), per_group(ra), AX.X, ALU.max))
            mine, other = gmax[:].unsqueeze(3).to_broadcast([P, B, GROUPS, GROUPS]), gmax[:].unsqueeze(2).to_broadcast([P, B, GROUPS, GROUPS])
            step(V.tensor_tensor(pairs(rb), other, mine, ALU.is_gt), V.tensor_tensor(pairs(rc), other, mine, ALU.is_equal))
            step(V.tensor_tensor(pairs(rc), pairs(rc), lower[:].unsqueeze(1).to_broadcast([P, B, GROUPS, GROUPS]), ALU.mult))
            step(V.tensor_tensor(rb[:], rb[:], rc[:], ALU.add))
            step(V.tensor_reduce(grank[:], pairs(rb), AX.X, ALU.add))
            step(V.tensor_scalar(gmask[:], grank[:], float(TOP_GROUPS), None, ALU.is_lt))
            step(V.tensor_tensor(per_group(rb), per_group(ra), gmask[:].rearrange("p b g -> p (b g)").unsqueeze(2).to_broadcast([P, B * GROUPS, E // GROUPS]),
                                 ALU.mult))
            step(*(V.max(top8[:, b, :], rb[:, b * E:(b + 1) * E]) for b in range(B)))
            sixth = top8[:, :, TOP_K - 1:TOP_K].to_broadcast([P, B, E])
            step(V.tensor_tensor(per_expert(ra), per_expert(rb), sixth, ALU.is_gt), V.tensor_tensor(per_expert(rc), per_expert(rb), sixth, ALU.is_equal))
            step(V.tensor_reduce(more[:].rearrange("p b o -> p (b o)"), per_expert(ra), AX.X, ALU.add))
            step(V.tensor_scalar(need[:], more[:], -1.0, float(TOP_K), ALU.mult, ALU.add))
            step(V.tensor_copy(re[:], rc[:]))
            count = running(re, rd, E, lambda t, a, z: per_expert(t)[:, :, a:z])
            to = rd if count is re else re
            step(V.tensor_tensor(per_expert(to), per_expert(count), need[:].to_broadcast([P, B, E]), ALU.is_le))
            step(V.tensor_tensor(to[:], to[:], rc[:], ALU.mult))
            step(V.tensor_tensor(ra[:], ra[:], to[:], ALU.add))
            V.tensor_copy(chosen[:], ra[:]).then_inc(s_chosen, 1)
            step(V.tensor_tensor(rd[:], rb[:], ra[:], ALU.mult))
            step(V.tensor_reduce(total[:].rearrange("p b o -> p (b o)"), per_expert(rd), AX.X, ALU.add))
            step(V.tensor_scalar(total[:], total[:], 1e-8, None, ALU.add))
            step(V.reciprocal(rtotal[:], total[:]))
            step(V.tensor_tensor(per_expert(share), per_expert(rd), rtotal[:].to_broadcast([P, B, E]), ALU.mult))
            dve.wait_ge(s_before, 4)
            step(V.tensor_copy(rc[:, 0:BANK], pU[0][:]), V.tensor_copy(rc[:, BANK:2 * BANK], pU[1][:]))
            step(V.tensor_copy(re[:], rc[:]))
            sums_b = running(re, rd, B, lambda t, a, z: per_expert(t)[:, a:z, :])
            free = rd if sums_b is re else re
            step(V.tensor_tensor(free[:], sums_b[:], rc[:], ALU.subtract), V.tensor_copy(na[:], per_expert(sums_b)[:, B - 1, :]))
            step(V.tensor_scalar(nb[:], na[:], P / 2 - 0.5, 1.0 / P, ALU.add, ALU.mult))
            step(V.tensor_scalar(nb[:], nb[:], MAGIC, None, ALU.add))
            step(V.tensor_scalar(na[:], nb[:], MAGIC, None, ALU.subtract))
            step(V.tensor_copy(tiles[:], na[:]))
            last = running(na, nb, E, lambda t, a, z: t[:, a:z])
            step(V.tensor_tensor(first[:], last[:], tiles[:], ALU.subtract))
            step(V.scalar_tensor_tensor(per_expert(rc), first[:].unsqueeze(1).to_broadcast([P, B, E]), float(P), per_expert(free), ALU.mult, ALU.add))
            step(*(V.tensor_tensor(rc[:, n * BANK:(n + 1) * BANK], rc[:, n * BANK:(n + 1) * BANK], pG[n][:], ALU.add) for n in range(2)))
            step(V.tensor_tensor(row_of[:], rc[:], ra[:], ALU.mult))
            step(*(V.max(row8[:, b, :], row_of[:, b * E:(b + 1) * E]) for b in range(B)))
            step(V.tensor_scalar(row8[:, :, 0:TOP_K], row8[:, :, 0:TOP_K], 1.0, None, ALU.subtract))
            V.tensor_scalar(place[:], row8[:], 0.0, None, ALU.max).then_inc(s_placed, 1)
            step(V.tensor_tensor(before[:], last[:].unsqueeze(1).to_broadcast([P, 2, E]), tile_at[:].unsqueeze(2).to_broadcast([P, 2, E]), ALU.is_le))
            step(V.tensor_reduce(of_tile[:], before[:], AX.X, ALU.add))
            V.tensor_scalar(expert[:], of_tile[:], float(E - 1), None, ALU.min).then_inc(s_placed, 1)
            dve.wait_ge(s_acc0, 16)

            def product(u):
                dve.wait_ge(s_g, u + 1)
                dve.wait_ge(s_up, u + 1)
                wait(dve, s_down, u - 1)
                V.tensor_tensor(h[:, u % 2, :], g[:, u % 2, :], pU[u % 2][:], ALU.mult).then_inc(s_h, 1)

            def add(u):
                dve.wait_ge(s_down, u + 1)
                wait(dve, s_acc, TB * (u + 1 - NB))
                for t in range(TB // 2):
                    c = (u % NB) * TB + 2 * t
                    two = acc[:, c:c + 2, :].rearrange("p t d -> p (t d)")
                    V.tensor_tensor(two, pD[2 * (u % 2) + t][:], two, ALU.add).then_inc(s_acc, 2)

            for u in range(SHARED * NB + 1):
                if u < SHARED * NB:
                    product(u)
                if u > 0:
                    add(u - 1)
            for k in range(TOP_K):
                pair = (rb, rc, rd)[k % 3]
                step(V.tensor_scalar(wanted[:], row8[:, :, k:k + 1], 1.0, None, ALU.add))
                step(V.tensor_tensor(per_expert(pair), per_expert(row_of), wanted[:].to_broadcast([P, B, E]), ALU.is_equal))
                step(V.tensor_tensor(pair[:], pair[:], share[:], ALU.mult))
                step(V.tensor_reduce(weight[:, :, k], per_expert(pair), AX.X, ALU.add))
            assert done[0] == ROUTED, done[0]

            def turned_rows(t, i):
                dve.wait_ge(s_xgt, t + 1)
                wait(dve, s_gu, t - 1)
                V.tensor_copy(xgT[:, i % 2, :, :].rearrange("p c t -> p (c t)"), pG[i % 2][:, 0:D]).then_inc(s_xgT, 1)

            def product_rows(t, i):
                dve.wait_ge(s_gate_t, t + 1)
                wait(dve, s_dt, t - 1)
                V.tensor_tensor(h[:, i % 2, 0:P], g[:, i % 2, 0:P], pU[i % 2][:, P:2 * P], ALU.mult).then_inc(s_ht, 1)

            pipeline(dve, [(0, turned_rows), (2, product_rows)], n=NT, body=RING)

            def weigh(b, i):
                wait(dve, s_sum, TOP_K * (b - DEEP + 1))
                V.tensor_copy(wcol[:, i, 0:TOP_K], weight[:, bass.ds(b, 1), 0:TOP_K].rearrange("p o k -> p (o k)")).then_inc(s_wcol, 1)
                dve.wait_ge(s_wcol, b + 1)
                dve.wait_ge(s_got[i], landed(b, i, TOP_K, DEEP))
                for k in range(TOP_K):
                    before_ = acc[:, bass.ds(b, 1), :].rearrange("p o d -> p (o d)") if k == 0 else sums[:, i, :]
                    wait(dve, s_sum, TOP_K * b + k)
                    V.scalar_tensor_tensor(sums[:, i, :], got[:, i, k, :], wcol[:, i, k:k + 1], before_, ALU.mult, ALU.add).then_inc(s_sum, 1)
                dve.wait_ge(s_sum, TOP_K * (b + 1))
                ln.statistics(dve, sums[:, i, :], b)

            def norm(b, i):
                wait(dve, s_stored[i], landed(b - DEEP, i, 1, DEEP))
                ln.result(dve, sums[:, i, :], xo[:, i, :], b)

            pipeline(dve, [(1, norm), (0, weigh)], body=DEEP)


def _slots(w):
    w = w.reshape(-1, 4, 4, 16).transpose(0, 2, 1, 3)
    out = np.zeros(w.shape[:3] + (32,), w.dtype)
    out[..., :16] = w
    return out.reshape(w.shape[0], 512)


def _constants(bf16):
    o = {"ident": np.eye(P, dtype=np.float32), "ident_bf16": np.eye(P, dtype=bf16)}
    at = np.arange(P)
    o["upto"] = (at[:, None] <= at[None, :]).astype(np.float32)
    o["future_bf16"] = np.where(at[:, None] > at[None, :], -1e30, 0.0).astype(bf16)
    o["diag"] = np.ascontiguousarray(np.broadcast_to(np.eye(B, dtype=np.float32), (P, B, B)))
    col = np.arange(ROW3)
    o["band"] = ((np.abs(at[:, None] - col[None, :]) <= 1) & (col[None, :] < P)).astype(np.float32)
    o["tap_of"] = np.stack([((at - r + 1) % 3 == t) for r in range(3) for t in range(3)]).astype(np.float32).reshape(1, 9, P)
    t, j = at % W, np.arange(W)
    early = j[None, :] <= t[:, None]
    o["rank_cap"] = np.where(early, 3e38, -3e38).astype(np.float32)
    o["rank_floor"] = np.where(early, 0, W).astype(np.float32)
    o["rank_never"] = np.where(early, NEVER, 0).astype(np.float32)
    k = np.arange(8)
    o["rank_later"] = np.ascontiguousarray(np.broadcast_to(k[None, :] >= k[:, None], (P, 8, 8))).astype(bf16)
    o["rank_hidden"] = np.where((at[None, :] >= TOP) & (at[None, :] > W + t[:, None]), NEVER, 0).astype(bf16)
    o["moe_lower_group"] = np.ascontiguousarray(np.broadcast_to((k[None, :] < k[:, None]).astype(np.float32), (P, 8, 8)))
    half = DR // 2
    o["rope_fold"] = ((at[:, None] % DR == at[None, :] % DR) & (at[:, None] < 2 * DR)).astype(np.float32)
    theta = 1.0 / 10000.0 ** (2.0 * np.arange(half) / DR)
    f, pos = theta[at % half][:, None], np.arange(float(S))[None, :]
    sign = np.where(at % DR < half, -1.0, 1.0)[:, None]
    pq = np.where(at[:, None] < 2 * DR, pos, 2 * pos - (W - 1)) * f
    own = (at[:, None] // DR) % 2 == 0
    c, s = np.cos(pq), np.sin(pq)
    query = np.stack([np.where(own, c, sign * s), np.where(own, -s, sign * c)], axis=1)
    pk = pos * f
    key_own = np.stack([np.cos(pk), -np.sin(pk)], axis=1)
    key_other = np.stack([sign * np.sin(pk), sign * np.cos(pk)], axis=1)
    o["rope_trig"] = np.stack([query, key_own, key_other], axis=1).astype(np.float32)
    row = np.arange(TOP) % SORTED
    ps = (W + 0.0 + row)[:, None] * theta[np.arange(DR) % half][None, :]
    sign_row = np.where(np.arange(DR) < half, -1.0, 1.0)[None, :]
    of_cos = np.stack([np.cos(ps), sign_row * np.sin(ps)], axis=1)
    of_sin = np.stack([-np.sin(ps), sign_row * np.cos(ps)], axis=1)
    o["rope_sorted"] = np.stack([of_cos, of_sin], axis=1).astype(np.float32)
    o["rope_rank_of_row"] = row.astype(np.float32).reshape(TOP, 1)
    jj, tt = at[:, None], W + np.arange(W)[None, :]
    o["rope_local"] = ((jj >= tt - (W - 1)) & (jj <= tt)).astype(np.float32)
    o["upto_bf16"] = o["upto"].astype(bf16)
    o["moe_tile_number"] = np.stack([at, TILES_OF_ROWS // 2 + at], axis=1).astype(np.float32)
    o["rope_future"] = (jj > tt).astype(np.float32)
    return o


def _layout(a, bf16):
    o = _constants(bf16)
    T = lambda m: np.ascontiguousarray(m.T)
    o["x"], o["ctx_1024"] = a["x"], a["ctx_1024"]
    o["mask_keys"] = a["mask_Bx1xS2_bf1"]
    o["causal_u8"] = a["mask_SxS_bc0"]
    same = {
        "L0_attn": "idx_wq idx_w W_dq W_dkv W_uq W_uk W_uv W_out",
        "L0_xattn": "Wv Wo bv bo",
        "L1_attn": "delta norm_weight",
        "L1_xattn": "hist_W hist_b hist_ln_g hist_ln_b ctx_W1 ctx_b1 ctx_W2 ctx_b2 kg_W1 kg_b1 kg_ln_g kg_ln_b kg_W2 kg_b2 Wv proj_W proj_b",
        "L1_ffn": "gate_bias",
    }
    for part, names in same.items():
        for n in names.split():
            o[f"{part}_{n}"] = a[f"{part}_{n}"]
    g = lambda n: a["L0_attn_" + n]
    o["L0_attn_idx_wk_twice"] = np.concatenate([g("idx_wk")] * 2, axis=1)
    swap = np.r_[16:32, 0:16]
    kr = g("W_kr")
    o["L0_attn_W_kr_copies"] = np.concatenate([np.tile(kr, (1, 4)), np.tile(kr[:, swap], (1, 4))], axis=1)
    qr = g("W_qr").reshape(P, HA, DR)
    o["L0_attn_W_qr_copies"] = np.concatenate([qr, qr[:, :, swap]] * 2, axis=2).reshape(P, HA * P)
    o["L0_attn_raw_columns"] = np.tile(g("raw_delta"), 8).reshape(P, 1)
    o["L0_attn_raw_rows"] = np.tile(g("raw_delta"), 2).reshape(1, DR)
    for part in ("L0_xattn", "L1_xattn"):
        for n in ("Wq", "Wk"):
            o[f"{part}_{n}_slots"] = _slots(a[f"{part}_{n}"])
    for n in ("bq", "bk"):
        o[f"L0_xattn_{n}_slots"] = T(_slots(a["L0_xattn_" + n][None])[0].reshape(4, P))
    for n in ("Wq", "Wk"):
        o[f"L1_attn_{n}T_slots"] = _slots(T(a["L1_attn_" + n]))
    o["L1_attn_WvfT"] = T(np.concatenate([a["L1_attn_Wv"], a["L1_attn_Wf"]]))
    o["L1_attn_WoT"] = T(a["L1_attn_Wo"])
    for n in ("gate", "up", "down"):
        o[f"L0_ffn_w_{n}T"] = T(a[f"L0_ffn_w_{n}"])
    g = lambda n: a["L1_ffn_" + n]
    o["L1_ffn_gate_wT"] = T(g("gate_w"))
    gate = np.concatenate([g("eg_w"), g("sg_w").reshape(SHARED, INTER, D)])
    up = np.concatenate([g("eu_w"), g("su_w").reshape(SHARED, INTER, D)])
    down = np.concatenate([g("ed_w"), g("sd_w").reshape(D, SHARED, INTER).transpose(1, 0, 2)])
    gate_up = np.stack([gate, up], axis=1).reshape(ALL, 2, INTER, KC, P).transpose(0, 4, 3, 1, 2).reshape(ALL, P, WG)
    o["L1_ffn_experts"] = np.concatenate([gate_up, down.transpose(0, 2, 1)], axis=2)
    return {n: np.ascontiguousarray(v) for n, v in o.items()}


def build(nc, x, out, w):
    middle = [nc.dram_tensor(f"x{n}", (B, S, D), F32, kind="Internal").ap() for n in range(5)]
    ranks = nc.dram_tensor("ranks", (B, S - W, W), BF16, kind="Internal").ap()
    hidden = nc.dram_tensor("hidden", (B, S - W, S), BF16, kind="Internal").ap()
    kernels = nc.dram_tensor("kernels", (B, H * TAPS), F32, kind="Internal").ap()
    rows = nc.dram_tensor("rows", (TILES_OF_ROWS * P, D), F32, kind="Internal").ap()
    results = nc.dram_tensor("results", (TILES_OF_ROWS * P, D), F32, kind="Internal").ap()
    places = nc.dram_tensor("places", (B, P, 8), U32, kind="Internal").ap()
    experts = nc.dram_tensor("experts", (TILES_OF_ROWS,), U32, kind="Internal").ap()
    with ExitStack() as ctx:
        cross_0 = Early(nc, ctx, "xa0", cross_attention_0_early(w))
        with ExitStack() as first:
            sparse_0 = Early(nc, first, "sa0", sparse_attention_0_early(w))
            rank_keys_0(nc, x, ranks, hidden, w, [sparse_0])
            sparse_attention_0(nc, x, middle[0], w, ranks, hidden, sparse_0, [cross_0])
        cross_1 = Early(nc, ctx, "xa1", cross_attention_1_early(w))
        context_1 = Early(nc, ctx, "ck1", context_kernels_1_early(w))
        linear_1 = Early(nc, ctx, "la1", linear_attention_1_early(w))
        ternary_0 = Early(nc, ctx, "ff0", ternary_ffn_0_early(w))
        cross_attention_0(nc, middle[0], middle[1], w, cross_0, [ternary_0])
        ternary_ffn_0(nc, middle[1], middle[2], w, rows, ternary_0, [linear_1])
        linear_attention_1(nc, middle[2], middle[3], w, linear_1, [context_1])
        context_kernels_1(nc, kernels, w, context_1, [cross_1])
        cross_attention_1(nc, middle[3], middle[4], w, kernels, cross_1)
    moe_ffn_1(nc, middle[4], out, w, rows, results, places, experts)


def kernel(**inputs):
    import concourse.bacc as bacc
    from concourse.bass_utils import run_bass_kernel_spmd
    from ml_dtypes import bfloat16

    arrays = _layout({n: np.ascontiguousarray(v) for n, v in inputs.items()}, bfloat16)
    nc = bacc.Bacc("TRN2", target_bir_lowering=False, num_devices=1)
    w = {n: nc.dram_tensor(n, a.shape, mybir.dt.from_np(a.dtype), kind="ExternalInput").ap() for n, a in arrays.items()}
    out = nc.dram_tensor("out", (B, S, D), F32, kind="ExternalOutput").ap()
    build(nc, w["x"], out, w)
    return run_bass_kernel_spmd(nc, [arrays], core_ids=[0]).results[0]["out"]
```
